# Optimizing a Trainium2 kernel written in Bass

```python
import numpy as np
import jax
import jax.numpy as jnp

def _softmax(x, axis=-1):
    return jax.nn.softmax(x, axis=axis)

def _gelu(x):
    return jax.nn.gelu(x, approximate=True)

def _silu(x):
    return jax.nn.silu(x)

def _sigmoid(x):
    return jax.nn.sigmoid(x)

def _layernorm(x, axis=-1, eps=1e-05):
    m = jnp.mean(x, axis=axis, keepdims=True)
    v = jnp.var(x, axis=axis, keepdims=True)
    return (x - m) / jnp.sqrt(v + eps)

def _scatter_add(tgt, idx, src, axis=0):
    return tgt.at[idx].add(src)

def _segment_sum(src, seg, n):
    return jax.ops.segment_sum(src, seg, n)
kernel_name = 'mk_vit_tower_cls_d2_tok_img512_r4_8ba7a3'

def setup_inputs(seed: int=0):
    np.random.seed(seed)
    _w = jnp.asarray

    def _rec_inputs():
        import jax
        import jax.numpy as jnp
        _rk = jax.random.key(seed)
        x = 7.57192e-06 + 1.00007 * jax.random.normal(jax.random.fold_in(_rk, 1), (64, 3, 224, 224), jnp.float32)
        cls_tok = 0.02 * jax.random.normal(jax.random.fold_in(_rk, 5), (1, 1, 128), jnp.float32)
        return (x, cls_tok)
    x, cls_tok = _rec_inputs()

    def _L0_tok_setup():
        import jax, jax.numpy as jnp
        import numpy as np
        D_MODEL = 128
        N_HEADS = 8
        D_HEAD = D_MODEL // N_HEADS
        D_FF = 344
        PATCH = 16
        IMG = 224
        N_PATCHES = (IMG // PATCH) ** 2
        T = N_PATCHES + 1
        B = 64
        EPS = 1e-06

        def rmsnorm(x, w):
            xf = x.astype(jnp.float32)
            norm = jax.lax.rsqrt(jnp.mean(xf * xf, axis=-1, keepdims=True) + EPS)
            return (xf * norm).astype(x.dtype) * w

        def _patch_embed(images, conv_w, conv_b, cls_token, pos_emb):
            y = jax.lax.conv_general_dilated(images, conv_w, window_strides=(PATCH, PATCH), padding='VALID', dimension_numbers=('NCHW', 'OIHW', 'NCHW'))
            y = y + conv_b[None, :, None, None]
            patches = y.reshape(y.shape[0], D_MODEL, -1).transpose(0, 2, 1)
            cls = jnp.broadcast_to(cls_token, (images.shape[0], 1, D_MODEL))
            return jnp.concatenate([cls, patches], axis=1) + pos_emb

        def _block(x, ln1w, wqkv, wo, ln2w, wg, wu, wd):
            Bx, Tx, C = x.shape
            h = rmsnorm(x, ln1w)
            qkv = (h @ wqkv.T).reshape(Bx, Tx, 3, N_HEADS, D_HEAD)
            q, k, v = jnp.moveaxis(qkv, 2, 0)
            scale = 1.0 / float(np.sqrt(D_HEAD))
            attn = jnp.einsum('bthd,bshd->bhts', q, k) * scale
            attn = jax.nn.softmax(attn, axis=-1)
            out = jnp.einsum('bhts,bshd->bthd', attn, v).reshape(Bx, Tx, C)
            x = x + out @ wo.T
            h2 = rmsnorm(x, ln2w)
            ff = jax.nn.silu(h2 @ wg.T) * (h2 @ wu.T) @ wd.T
            return x + ff
        key = jax.random.key(seed)
        ks = jax.random.split(key, 16)
        std = 0.02
        d = {'images': jax.random.normal(ks[0], (B, 3, IMG, IMG), dtype=jnp.float32), 'conv_w': jax.random.normal(ks[1], (D_MODEL, 3, PATCH, PATCH), dtype=jnp.float32) * std, 'conv_b': jnp.zeros((D_MODEL,), dtype=jnp.float32), 'cls_token': jax.random.normal(ks[2], (1, 1, D_MODEL), dtype=jnp.float32) * std, 'pos_emb': jax.random.normal(ks[3], (1, T, D_MODEL), dtype=jnp.float32) * std, 'ln_f': jnp.ones((D_MODEL,), dtype=jnp.float32)}
        ki = 4
        for i in range(2):
            d[f'ln1_{i}'] = jnp.ones((D_MODEL,), dtype=jnp.float32)
            d[f'qkv_{i}'] = jax.random.normal(ks[ki + 0], (3 * D_MODEL, D_MODEL), dtype=jnp.float32) * std
            d[f'wo_{i}'] = jax.random.normal(ks[ki + 1], (D_MODEL, D_MODEL), dtype=jnp.float32) * std
            d[f'ln2_{i}'] = jnp.ones((D_MODEL,), dtype=jnp.float32)
            d[f'gate_{i}'] = jax.random.normal(ks[ki + 2], (D_FF, D_MODEL), dtype=jnp.float32) * std
            d[f'up_{i}'] = jax.random.normal(ks[ki + 3], (D_FF, D_MODEL), dtype=jnp.float32) * std
            d[f'down_{i}'] = jax.random.normal(ks[ki + 4], (D_MODEL, D_FF), dtype=jnp.float32) * std
            ki += 5
        return d
    _L0_tok_all = _L0_tok_setup()
    _L0_tok_in = {k: v for k, v in _L0_tok_all.items() if k in ('conv_w', 'conv_b', 'cls_token', 'pos_emb', 'ln_f', 'ln1_0', 'qkv_0', 'wo_0', 'ln2_0', 'gate_0', 'up_0', 'down_0', 'ln1_1', 'qkv_1', 'wo_1', 'ln2_1', 'gate_1', 'up_1', 'down_1')}
    del _L0_tok_all

    def _L0_attn_setup():
        import jax, jax.numpy as jnp
        import numpy as np
        EPS_NORM = 1e-12
        EPS_LN = 1e-05

        def _mlp_enc(x, w1, b1, w2, b2):
            h = jax.nn.gelu(x @ w1 + b1, approximate=False)
            return h @ w2 + b2

        def _l2norm(v):
            n = jnp.sqrt(jnp.sum(v * v, axis=-1, keepdims=True))
            return v / jnp.maximum(n, EPS_NORM)
        key = jax.random.key(seed)
        D, K = (128, 64)
        B, L = (2, 512)
        ks = jax.random.split(key, 16)
        s_d = 1.0 / np.sqrt(D)

        def lin(k, fan_in, fan_out):
            s = 1.0 / np.sqrt(fan_in)
            return jax.random.uniform(k, (fan_in, fan_out), jnp.float32, -s, s)
        return {'x': jax.random.normal(ks[0], (B, L, D), jnp.float32), 'k_w1': lin(ks[1], D, D), 'k_b1': jnp.zeros((D,), jnp.float32), 'k_w2': lin(ks[2], D, K), 'k_b2': jnp.zeros((K,), jnp.float32), 'q_w1': lin(ks[3], D, D), 'q_b1': jnp.zeros((D,), jnp.float32), 'q_w2': lin(ks[4], D, K), 'q_b2': jnp.zeros((K,), jnp.float32), 'v_w': lin(ks[5], D, D), 'v_b': jnp.zeros((D,), jnp.float32), 'ln_g': jnp.ones((D,), jnp.float32), 'ln_b': jnp.zeros((D,), jnp.float32), 'o_w': lin(ks[6], D, D), 'o_b': jnp.zeros((D,), jnp.float32)}
    _L0_attn_all = _L0_attn_setup()
    _L0_attn_in = {k: v for k, v in _L0_attn_all.items() if k in ('k_w1', 'k_b1', 'k_w2', 'k_b2', 'q_w1', 'q_b1', 'q_w2', 'q_b2', 'v_w', 'v_b', 'ln_g', 'ln_b', 'o_w', 'o_b')}
    del _L0_attn_all

    def _L0_ffn_setup():
        import jax, jax.numpy as jnp
        import numpy as np
        B, S, D = (8, 1024, 128)
        H = 512
        O = 128
        E = 8
        TOP_K = 1
        key = jax.random.key(seed)
        ks = jax.random.split(key, 8)
        sc = 0.02
        return {'x': jax.random.normal(ks[0], (B, S, D), dtype=jnp.float32), 'Wr': jax.random.normal(ks[1], (D, E), dtype=jnp.float32) * sc, 'br': jnp.zeros((E,), dtype=jnp.float32), 'W1': jax.random.normal(ks[2], (E, D, H), dtype=jnp.float32) * sc, 'b1': jnp.zeros((E, H), dtype=jnp.float32), 'W2': jax.random.normal(ks[3], (E, H, O), dtype=jnp.float32) * sc, 'b2': jnp.zeros((E, O), dtype=jnp.float32)}
    _L0_ffn_all = _L0_ffn_setup()
    _L0_ffn_in = {k: v for k, v in _L0_ffn_all.items() if k in ('Wr', 'br', 'W1', 'b1', 'W2', 'b2')}
    del _L0_ffn_all

    def _L1_attn_setup():
        import jax, jax.numpy as jnp
        import numpy as np
        B, L, U, H = (16, 256, 128, 2)
        key = jax.random.key(seed)
        ks = jax.random.split(key, 8)
        s = 0.02
        return {'inputs': jax.random.normal(ks[0], (B, L, U), dtype=jnp.float32), 'tW': jax.random.normal(ks[1], (H, U, U), dtype=jnp.float32) * s, 'tb': jnp.zeros((H, U), dtype=jnp.float32), 'cW': jax.random.normal(ks[2], (H, U, U), dtype=jnp.float32) * s, 'cb': jnp.zeros((H, U), dtype=jnp.float32), 'aW': jax.random.normal(ks[3], (3 * U,), dtype=jnp.float32) * s, 'ab': jnp.zeros((1,), dtype=jnp.float32), 'frW': jax.random.normal(ks[4], (2 * U, U), dtype=jnp.float32) * s, 'frb': jnp.zeros((U,), dtype=jnp.float32), 'ffW': jax.random.normal(ks[5], (2 * U, U), dtype=jnp.float32) * s, 'ffb': jnp.zeros((U,), dtype=jnp.float32)}
    _L1_attn_all = _L1_attn_setup()
    _L1_attn_in = {k: v for k, v in _L1_attn_all.items() if k in ('tW', 'tb', 'cW', 'cb', 'aW', 'ab', 'frW', 'frb', 'ffW', 'ffb')}
    del _L1_attn_all

    def _L1_ffn_setup():
        import jax, jax.numpy as jnp
        import numpy as np
        B, T, H = (8, 2048, 128)
        E, R = (4, 16)
        SCALE = 0.04
        key = jax.random.key(seed)
        ks = jax.random.split(key, 7)
        return {'x': jax.random.normal(ks[0], (B, T, H), jnp.float32), 'gate_w': jax.random.normal(ks[1], (E, H), jnp.float32) * SCALE, 'thr_w': jax.random.normal(ks[2], (1, H), jnp.float32) * SCALE, 'fc1_w': jax.random.normal(ks[3], (E, H, H), jnp.float32) * SCALE, 'lora_A': jax.random.normal(ks[4], (E, H, R), jnp.float32) * SCALE, 'lora_B': jax.random.normal(ks[5], (E, R, H), jnp.float32) * SCALE, 'fc2_w': jax.random.normal(ks[6], (E, H, H), jnp.float32) * SCALE}
    _L1_ffn_all = _L1_ffn_setup()
    _L1_ffn_in = {k: v for k, v in _L1_ffn_all.items() if k in ('gate_w', 'thr_w', 'fc1_w', 'lora_A', 'lora_B', 'fc2_w')}
    del _L1_ffn_all
    return {'x': x, 'cls_tok': cls_tok, 'L0_tok_conv_w': _L0_tok_in['conv_w'], 'L0_tok_conv_b': _L0_tok_in['conv_b'], 'L0_tok_cls_token': _L0_tok_in['cls_token'], 'L0_tok_pos_emb': _L0_tok_in['pos_emb'], 'L0_tok_ln_f': _L0_tok_in['ln_f'], 'L0_tok_ln1_0': _L0_tok_in['ln1_0'], 'L0_tok_qkv_0': _L0_tok_in['qkv_0'], 'L0_tok_wo_0': _L0_tok_in['wo_0'], 'L0_tok_ln2_0': _L0_tok_in['ln2_0'], 'L0_tok_gate_0': _L0_tok_in['gate_0'], 'L0_tok_up_0': _L0_tok_in['up_0'], 'L0_tok_down_0': _L0_tok_in['down_0'], 'L0_tok_ln1_1': _L0_tok_in['ln1_1'], 'L0_tok_qkv_1': _L0_tok_in['qkv_1'], 'L0_tok_wo_1': _L0_tok_in['wo_1'], 'L0_tok_ln2_1': _L0_tok_in['ln2_1'], 'L0_tok_gate_1': _L0_tok_in['gate_1'], 'L0_tok_up_1': _L0_tok_in['up_1'], 'L0_tok_down_1': _L0_tok_in['down_1'], 'L0_attn_k_w1': _L0_attn_in['k_w1'], 'L0_attn_k_b1': _L0_attn_in['k_b1'], 'L0_attn_k_w2': _L0_attn_in['k_w2'], 'L0_attn_k_b2': _L0_attn_in['k_b2'], 'L0_attn_q_w1': _L0_attn_in['q_w1'], 'L0_attn_q_b1': _L0_attn_in['q_b1'], 'L0_attn_q_w2': _L0_attn_in['q_w2'], 'L0_attn_q_b2': _L0_attn_in['q_b2'], 'L0_attn_v_w': _L0_attn_in['v_w'], 'L0_attn_v_b': _L0_attn_in['v_b'], 'L0_attn_ln_g': _L0_attn_in['ln_g'], 'L0_attn_ln_b': _L0_attn_in['ln_b'], 'L0_attn_o_w': _L0_attn_in['o_w'], 'L0_attn_o_b': _L0_attn_in['o_b'], 'L0_ffn_Wr': _L0_ffn_in['Wr'], 'L0_ffn_br': _L0_ffn_in['br'], 'L0_ffn_W1': _L0_ffn_in['W1'], 'L0_ffn_b1': _L0_ffn_in['b1'], 'L0_ffn_W2': _L0_ffn_in['W2'], 'L0_ffn_b2': _L0_ffn_in['b2'], 'L1_attn_tW': _L1_attn_in['tW'], 'L1_attn_tb': _L1_attn_in['tb'], 'L1_attn_cW': _L1_attn_in['cW'], 'L1_attn_cb': _L1_attn_in['cb'], 'L1_attn_aW': _L1_attn_in['aW'], 'L1_attn_ab': _L1_attn_in['ab'], 'L1_attn_frW': _L1_attn_in['frW'], 'L1_attn_frb': _L1_attn_in['frb'], 'L1_attn_ffW': _L1_attn_in['ffW'], 'L1_attn_ffb': _L1_attn_in['ffb'], 'L1_ffn_gate_w': _L1_ffn_in['gate_w'], 'L1_ffn_thr_w': _L1_ffn_in['thr_w'], 'L1_ffn_fc1_w': _L1_ffn_in['fc1_w'], 'L1_ffn_lora_A': _L1_ffn_in['lora_A'], 'L1_ffn_lora_B': _L1_ffn_in['lora_B'], 'L1_ffn_fc2_w': _L1_ffn_in['fc2_w']}

def reference(x, cls_tok, L0_tok_conv_w, L0_tok_conv_b, L0_tok_cls_token, L0_tok_pos_emb, L0_tok_ln_f, L0_tok_ln1_0, L0_tok_qkv_0, L0_tok_wo_0, L0_tok_ln2_0, L0_tok_gate_0, L0_tok_up_0, L0_tok_down_0, L0_tok_ln1_1, L0_tok_qkv_1, L0_tok_wo_1, L0_tok_ln2_1, L0_tok_gate_1, L0_tok_up_1, L0_tok_down_1, L0_attn_k_w1, L0_attn_k_b1, L0_attn_k_w2, L0_attn_k_b2, L0_attn_q_w1, L0_attn_q_b1, L0_attn_q_w2, L0_attn_q_b2, L0_attn_v_w, L0_attn_v_b, L0_attn_ln_g, L0_attn_ln_b, L0_attn_o_w, L0_attn_o_b, L0_ffn_Wr, L0_ffn_br, L0_ffn_W1, L0_ffn_b1, L0_ffn_W2, L0_ffn_b2, L1_attn_tW, L1_attn_tb, L1_attn_cW, L1_attn_cb, L1_attn_aW, L1_attn_ab, L1_attn_frW, L1_attn_frb, L1_attn_ffW, L1_attn_ffb, L1_ffn_gate_w, L1_ffn_thr_w, L1_ffn_fc1_w, L1_ffn_lora_A, L1_ffn_lora_B, L1_ffn_fc2_w):
    import jax
    import jax.numpy as jnp

    def _L0_tok_ref(images, conv_w, conv_b, cls_token, pos_emb, ln_f, ln1_0, qkv_0, wo_0, ln2_0, gate_0, up_0, down_0, ln1_1, qkv_1, wo_1, ln2_1, gate_1, up_1, down_1):
        import jax, jax.numpy as jnp
        import numpy as np
        D_MODEL = 128
        N_HEADS = 8
        D_HEAD = D_MODEL // N_HEADS
        D_FF = 344
        PATCH = 16
        IMG = 224
        N_PATCHES = (IMG // PATCH) ** 2
        T = N_PATCHES + 1
        B = 64
        EPS = 1e-06

        def rmsnorm(x, w):
            xf = x.astype(jnp.float32)
            norm = jax.lax.rsqrt(jnp.mean(xf * xf, axis=-1, keepdims=True) + EPS)
            return (xf * norm).astype(x.dtype) * w

        def _patch_embed(images, conv_w, conv_b, cls_token, pos_emb):
            y = jax.lax.conv_general_dilated(images, conv_w, window_strides=(PATCH, PATCH), padding='VALID', dimension_numbers=('NCHW', 'OIHW', 'NCHW'))
            y = y + conv_b[None, :, None, None]
            patches = y.reshape(y.shape[0], D_MODEL, -1).transpose(0, 2, 1)
            cls = jnp.broadcast_to(cls_token, (images.shape[0], 1, D_MODEL))
            return jnp.concatenate([cls, patches], axis=1) + pos_emb

        def _block(x, ln1w, wqkv, wo, ln2w, wg, wu, wd):
            Bx, Tx, C = x.shape
            h = rmsnorm(x, ln1w)
            qkv = (h @ wqkv.T).reshape(Bx, Tx, 3, N_HEADS, D_HEAD)
            q, k, v = jnp.moveaxis(qkv, 2, 0)
            scale = 1.0 / float(np.sqrt(D_HEAD))
            attn = jnp.einsum('bthd,bshd->bhts', q, k) * scale
            attn = jax.nn.softmax(attn, axis=-1)
            out = jnp.einsum('bhts,bshd->bthd', attn, v).reshape(Bx, Tx, C)
            x = x + out @ wo.T
            h2 = rmsnorm(x, ln2w)
            ff = jax.nn.silu(h2 @ wg.T) * (h2 @ wu.T) @ wd.T
            return x + ff
        x = _patch_embed(images, conv_w, conv_b, cls_token, pos_emb)
        x = _block(x, ln1_0, qkv_0, wo_0, ln2_0, gate_0, up_0, down_0)
        x = _block(x, ln1_1, qkv_1, wo_1, ln2_1, gate_1, up_1, down_1)
        return rmsnorm(x, ln_f)

    def _L0_attn_ref(x, k_w1, k_b1, k_w2, k_b2, q_w1, q_b1, q_w2, q_b2, v_w, v_b, ln_g, ln_b, o_w, o_b):
        import jax, jax.numpy as jnp
        import numpy as np
        EPS_NORM = 1e-12
        EPS_LN = 1e-05

        def _mlp_enc(x, w1, b1, w2, b2):
            h = jax.nn.gelu(x @ w1 + b1, approximate=False)
            return h @ w2 + b2

        def _l2norm(v):
            n = jnp.sqrt(jnp.sum(v * v, axis=-1, keepdims=True))
            return v / jnp.maximum(n, EPS_NORM)
        B, L, D = x.shape
        key_vec = _l2norm(_mlp_enc(x, k_w1, k_b1, k_w2, k_b2))
        query_vec = _l2norm(_mlp_enc(x, q_w1, q_b1, q_w2, q_b2))
        V = x @ v_w + v_b
        K = key_vec.shape[-1]
        P = K // 2
        kc = (key_vec[..., 0:2 * P:2] + 1j * key_vec[..., 1:2 * P:2]).astype(jnp.complex64)
        qc = (query_vec[..., 0:2 * P:2] + 1j * query_vec[..., 1:2 * P:2]).astype(jnp.complex64)
        Vc = V.astype(jnp.complex64)
        bound = kc[..., :, None] * Vc[..., None, :]
        memory = jnp.cumsum(bound, axis=1)
        retrieved = jnp.real(jnp.sum(memory * jnp.conj(qc)[..., None], axis=2))
        positions = jnp.arange(1, L + 1, dtype=jnp.float32)
        norm = jnp.sqrt(positions * P)[None, :, None]
        r = retrieved / norm
        mu = jnp.mean(r, axis=-1, keepdims=True)
        var = jnp.mean((r - mu) ** 2, axis=-1, keepdims=True)
        r_ln = (r - mu) / jnp.sqrt(var + EPS_LN) * ln_g + ln_b
        return x + r_ln @ o_w + o_b

    def _L0_ffn_ref(x, Wr, br, W1, b1, W2, b2):
        import jax, jax.numpy as jnp
        import numpy as np
        B, S, D = (8, 1024, 128)
        H = 512
        O = 128
        E = 8
        TOP_K = 1
        b, s, d = x.shape
        xf = x.reshape(-1, d)
        router_logits = xf @ Wr + br
        topk_logits, topk_idx = jax.lax.top_k(router_logits, TOP_K)
        topk_gates = jax.nn.softmax(topk_logits, axis=1)
        out = jnp.zeros((xf.shape[0], O), dtype=x.dtype)
        for k in range(TOP_K):
            idx_k = topk_idx[:, k]
            gate_k = topk_gates[:, k:k + 1]
            for e in range(E):
                h = jax.nn.relu(xf @ W1[e] + b1[e])
                oe = h @ W2[e] + b2[e]
                mask = (idx_k == e)[:, None]
                out = out + jnp.where(mask, gate_k * oe, 0.0)
        return out.reshape(b, s, O)

    def _L1_attn_ref(inputs, tW, tb, cW, cb, aW, ab, frW, frb, ffW, ffb):
        import jax, jax.numpy as jnp
        import numpy as np
        B, L, U, H = (16, 256, 128, 2)
        x = inputs
        for i in range(tW.shape[0]):
            t = jax.nn.relu(x @ tW[i] + tb[i])
            c = jax.nn.sigmoid(x @ cW[i] + cb[i])
            x = t * c + x * (1.0 - c)
        u = x.shape[-1]
        w1, w2, w3 = (aW[:u], aW[u:2 * u], aW[2 * u:])
        s1 = x @ w1
        s2 = x @ w2
        s3 = jnp.einsum('bid,bjd->bij', x * w3, x)
        A = jax.nn.relu(s1[:, :, None] + s2[:, None, :] + s3 + ab[0])
        att = jnp.einsum('bij,bjd->bid', jax.nn.softmax(A, axis=-1), x)
        concat = jnp.concatenate([inputs, att], axis=-1)
        z = jax.nn.sigmoid(concat @ ffW + ffb)
        r = jax.nn.sigmoid(concat @ frW + frb)
        f = z
        return r * inputs + f * z

    def _L1_ffn_ref(x, gate_w, thr_w, fc1_w, lora_A, lora_B, fc2_w):
        import jax, jax.numpy as jnp
        import numpy as np
        B, T, H = (8, 2048, 128)
        E, R = (4, 16)
        SCALE = 0.04
        b, t, h = x.shape
        e = gate_w.shape[0]
        xf = x.reshape(-1, h)
        gate_logits = jax.nn.softmax(xf @ gate_w.T, axis=-1)
        thresholds = jax.nn.sigmoid(xf @ thr_w.T) * (1.0 / e)
        adapted = gate_logits - thresholds
        selected = (adapted >= 0).astype(xf.dtype)
        weights = adapted * selected
        wsum = jnp.sum(weights, axis=-1, keepdims=True)
        wsum = jnp.where(wsum == 0, jnp.ones_like(wsum), wsum)
        weights = weights / wsum
        hidden = jax.nn.relu(jnp.einsum('ni,ehi->neh', xf, fc1_w))
        lo = jnp.einsum('neh,ehr->ner', hidden, lora_A)
        lo = jnp.einsum('ner,ero->neo', lo, lora_B)
        expert_out = jnp.einsum('neo,edo->ned', lo, fc2_w)
        out = jnp.einsum('ne,ned->nd', weights, expert_out)
        return out.reshape(b, t, h)
    h = _L0_tok_ref(x, L0_tok_conv_w, L0_tok_conv_b, L0_tok_cls_token, L0_tok_pos_emb, L0_tok_ln_f, L0_tok_ln1_0, L0_tok_qkv_0, L0_tok_wo_0, L0_tok_ln2_0, L0_tok_gate_0, L0_tok_up_0, L0_tok_down_0, L0_tok_ln1_1, L0_tok_qkv_1, L0_tok_wo_1, L0_tok_ln2_1, L0_tok_gate_1, L0_tok_up_1, L0_tok_down_1)
    h = jnp.concatenate([jnp.broadcast_to(cls_tok, (h.shape[0], 1, h.shape[2])), h], axis=1)
    h = h + _L0_attn_ref(_layernorm(h, axis=-1), L0_attn_k_w1, L0_attn_k_b1, L0_attn_k_w2, L0_attn_k_b2, L0_attn_q_w1, L0_attn_q_b1, L0_attn_q_w2, L0_attn_q_b2, L0_attn_v_w, L0_attn_v_b, L0_attn_ln_g, L0_attn_ln_b, L0_attn_o_w, L0_attn_o_b)
    h = h + _L0_ffn_ref(_layernorm(h, axis=-1), L0_ffn_Wr, L0_ffn_br, L0_ffn_W1, L0_ffn_b1, L0_ffn_W2, L0_ffn_b2)
    h = h + _L1_attn_ref(_layernorm(h, axis=-1), L1_attn_tW, L1_attn_tb, L1_attn_cW, L1_attn_cb, L1_attn_aW, L1_attn_ab, L1_attn_frW, L1_attn_frb, L1_attn_ffW, L1_attn_ffb)
    h = h + _L1_ffn_ref(_layernorm(h, axis=-1), L1_ffn_gate_w, L1_ffn_thr_w, L1_ffn_fc1_w, L1_ffn_lora_A, L1_ffn_lora_B, L1_ffn_fc2_w)
    return h

_drawn_inputs = setup_inputs


def setup_inputs(seed=0):
    import zlib

    import numpy as np

    out = dict(_drawn_inputs(seed))
    spreads = {'L0_tok_conv_b': (0.0, 0.1),
     'L0_tok_ln_f': (1.0, 0.2),
     'L0_tok_ln1_0': (1.0, 0.6),
     'L0_tok_ln2_0': (1.0, 0.6),
     'L0_tok_ln1_1': (1.0, 0.6),
     'L0_tok_ln2_1': (1.0, 0.6),
     'L0_attn_k_b1': (0.0, 0.1),
     'L0_attn_k_b2': (0.0, 0.1),
     'L0_attn_q_b1': (0.0, 0.1),
     'L0_attn_q_b2': (0.0, 0.1),
     'L0_attn_v_b': (0.0, 0.1),
     'L0_attn_ln_g': (1.0, 0.2),
     'L0_attn_ln_b': (0.0, 0.1),
     'L0_attn_o_b': (0.0, 0.1),
     'L0_ffn_br': (0.0, 0.1),
     'L0_ffn_b1': (0.0, 0.559),
     'L0_ffn_b2': (0.0, 0.1),
     'L1_attn_tb': (0.0, 2.0),
     'L1_attn_cb': (0.0, 2.0),
     'L1_attn_frb': (0.0, 0.8),
     'L1_attn_ffb': (0.0, 0.771)}
    factors = {'L1_attn_tW': 22.314,
     'L1_attn_cW': 34.388,
     'L1_attn_aW': 38.309,
     'L1_ffn_gate_w': 8.0,
     'L1_ffn_thr_w': 8.0,
     'L1_ffn_fc1_w': 8.0,
     'L1_ffn_lora_A': 8.0,
     'L1_ffn_lora_B': 8.0,
     'L1_ffn_fc2_w': 8.0}
    for name, (base, spread) in spreads.items():
        noise = np.random.default_rng([zlib.crc32(name.encode()), seed]).standard_normal(out[name].shape)
        drawn = base * np.exp(spread * noise) if base else spread * noise
        out[name] = jnp.asarray(drawn.astype(out[name].dtype))
    for name, factor in factors.items():
        out[name] = (out[name] * factor).astype(out[name].dtype)
    return out
```

```python
import concourse.bass as bass
from concourse import mybir
from contextlib import ExitStack
import numpy as np

P = 128
D = 128
HEADS, DH = 8, 16
PATCH, SIDE = 16, 14
NPATCH = SIDE * SIDE
T = NPATCH + 1
L = T + 1
IMGS = 2
STREAMS = 2
KP = 3 * PATCH * PATCH // P
DFF = 344
FCH = [(0, 128), (128, 128), (256, 88)]
NE, HID = 8, 512
NJ = HID // P
E2, R2 = 4, 16
KD = 64
TC = [(0, 128), (128, T - 128)]
LC = [(0, 128), (128, L - 128)]
TK = 99
NTK = IMGS * L // TK
N = IMGS * L
BLK = 32
TINY = 2.0 ** 20

WSPEC = [("conv", KP * D), ("qkv0", 3 * D), ("qkv1", 3 * D), ("wo0", 2 * D), ("wo1", 2 * D),
         ("gate0", DFF), ("gate1", DFF), ("up0", DFF), ("up1", DFF),
         ("down0", 3 * D), ("down1", 3 * D),
         ("k_w1", D), ("q_w1", D), ("k_w2", KD), ("q_w2", KD), ("v_w", D), ("o_w", D), ("v_b", D),
         ("Wr", NE), ("W1", NE * HID), ("W2", NE * NJ * D),
         ("tW", 2 * D), ("cW", 2 * D), ("frW", 2 * D), ("ffW", 2 * D),
         ("gt", E2 + 1), ("fc1", E2 * D), ("lA", E2 * E2 * R2), ("lB", E2 * E2 * R2), ("fc2", E2 * D),
         ("pos", T), ("br", NTK * NE), ("b1", HID), ("b2", D),
         ("conv_b", 1), ("cls_token", 1), ("cls_tok", 1), ("ln_f", 1), ("ln1_0", 1), ("ln1_1", 1),
         ("ln2_0", 1), ("ln2_1", 1), ("k_b1", 1), ("q_b1", 1), ("k_b2", 1), ("q_b2", 1),
         ("ln_g", 1), ("ln_b", 1), ("o_b", 1), ("tb", 2), ("cb", 2), ("aw", 3), ("ab", 1),
         ("frb", 1), ("ffb", 1)]
CSPEC = [("ident", P), ("centre", D), ("mean", D), ("ones", D), ("hmask", HEADS), ("sel", P),
         ("causal", L + LC[1][1]), ("iota", NTK * NE), ("expsel", NE * P), ("one", L)]


def offsets(spec):
    at, o = {}, 0
    for name, n in spec:
        at[name] = (o, n)
        o += n
    return at, o


WAT, WTOT = offsets(WSPEC)
CAT, CTOT = offsets(CSPEC)
PIECE = 2048


def build(nc, iters, patches, weights, consts, out):
    f32, bf16, i32 = mybir.dt.float32, mybir.dt.bfloat16, mybir.dt.int32
    ALU, ACT, AX = mybir.AluOpType, mybir.ActivationFunctionType, mybir.AxisListType
    LNEXP = "natural_log_exp_and_others"
    ctx = ExitStack()
    with ctx:
        def sb(name, shape, dt=f32):
            return ctx.enter_context(nc.sbuf_tensor(name, shape, dt))

        W = sb("W", [P, WTOT])
        C = sb("C", [P, CTOT])

        def w(name, a=0, b=None, rows=P):
            o, n = WAT[name]
            return W[0:rows, o + a:o + (n if b is None else b)]

        def c(name, a=0, b=None, rows=P):
            o, n = CAT[name]
            return C[0:rows, o + a:o + (n if b is None else b)]

        identb = sb("identb", [P, P], bf16)
        expselb = sb("expselb", [NE, NE, P], bf16)
        w1row = sb("w1row", [P, L])
        owg = sb("owg", [P, D])
        obp = sb("obp", [P, 1])
        G = sb("G", [E2 * R2, D])

        def per_stream(name, shape, dt=f32):
            return [sb(f"{name}{x}", shape, dt) for x in range(STREAMS)]

        img = per_stream("img", [P, KP, IMGS * NPATCH])
        X = per_stream("X", [P, IMGS, L])
        sq = per_stream("sq", [P, N])
        lnv = per_stream("lnv", [P, 2, N])
        rs = per_stream("rs", [P, 2, N])
        h = per_stream("h", [P, IMGS, T])
        z = per_stream("z", [P, IMGS, L])
        kS = per_stream("kS", [P, IMGS, T])
        regA = per_stream("regA", [P, NE * N])
        regB = per_stream("regB", [P, NE * N])
        regC = per_stream("regC", [P, NJ * N])

        def view(reg, at, pattern, **dims):
            n = int(np.prod(list(dims.values())))
            if "one" in dims:
                return [r[:, at:at + n] for r in reg]
            return [r[:, at:at + n].rearrange(f"p ({pattern}) -> p {pattern}", **dims) for r in reg]

        IT = IMGS * T
        qm = view(regA, 0, "h i t", h=HEADS, i=IMGS, t=T)
        xe = view(regA, 0, "e n", e=NE, n=N)
        sil = view(regB, 0, "j n", j=3, n=IT)
        ff = view(regB, 3 * IT, "j n", j=3, n=IT)
        on = view(regB, 6 * IT, "g n", g=2, n=IT)
        mk = view(regB, 0, "e n", e=NE, n=N)
        pt = view(regC, 0, "c a t", c=2, a=2, t=T)
        oS = view(regC, 2 * IT, "g n", g=2, n=IT)
        qS = view(regC, 2 * IT, "i t", i=IMGS, t=T)
        hid = view(regC, 0, "j n", j=NJ, n=N)
        ysel = view(regA, 0, "e n", e=NE, n=N)
        gel = view(regA, 0, "s n", s=2, n=N)
        kq = [v[0:KD] for v in view(regA, 2 * N, "s i t", s=2, i=IMGS, t=L)]
        kqs = [v[0:KD] for v in view(regA, 4 * N, "s n", s=2, n=N)]
        zn = view(regA, 6 * N, "one n", one=1, n=N)
        rS = view(regA, 7 * N, "one n", one=1, n=N)
        vS = view(regB, 0, "i c d", i=IMGS, c=2, d=D)
        As = view(regB, 4 * D, "i n", i=IMGS, n=L + LC[1][1])
        xh = view(regA, 0, "k i t", k=2, i=IMGS, t=L)
        xw = view(regA, 2 * N, "i t", i=IMGS, t=L)
        aS = view(regA, 3 * N, "i c t", i=IMGS, c=2, t=L)
        pTS = view(regA, 5 * N, "i c t", i=IMGS, c=2, t=L)
        att = view(regA, 7 * N, "one n", one=1, n=N)
        tS = view(regB, 0, "one n", one=1, n=N)
        cS = view(regB, N, "one n", one=1, n=N)
        dS = view(regB, 2 * N, "one n", one=1, n=N)
        xTS = view(regB, 3 * N, "i c d", i=IMGS, c=2, d=D)
        wr = [v[0:E2 * R2] for v in view(regB, 5 * N, "one n", one=1, n=N)]
        low = [v[0:E2 * R2] for v in view(regB, 6 * N, "one n", one=1, n=N)]
        va = per_stream("va", [P, IMGS, 2, HEADS, BLK])
        nm = per_stream("nm", [P, IMGS, 2, HEADS], bf16)
        lg = per_stream("lg", [TK, 6, NTK, NE])
        lgs = per_stream("lgs", [TK, 2, NTK])
        ohT = per_stream("ohT", [NE, N])
        ohTb = per_stream("ohTb", [NE, N], bf16)
        am = per_stream("am", [P, 3, IMGS, 2])
        gl = per_stream("gl", [TK, 4, NTK, E2 + 1])
        wrep = per_stream("wrep", [TK, NTK, E2, R2])
        gs = per_stream("gs", [TK, 8, NTK])
        outS = per_stream("outS", [P, N])

        ps = [[ctx.enter_context(nc.psum_tensor(f"ps{x}", [P, 4, 512], f32))] for x in range(STREAMS)]

        def bank(x, b, n=N, rows=P, a=0, row0=0):
            return ps[x][0][row0:row0 + rows, b, a:a + n]

        def banks(x, b, n, rows=P, a=0):
            return ps[x][0][0:rows, b:b + 2, a:a + n]

        class Signal:

            def __init__(self, name, times=1, by=1, blocks=False, split=False):
                self.sems = [ctx.enter_context(nc.semaphore(f"{name}{x if split else ''}"))
                             for x in range(STREAMS if split else 1)]
                self.times, self.by, self.blocks = times, by, blocks

            def of(self, x):
                return self.sems[x % len(self.sems)]

            def done(self, it, x, k=0):
                if len(self.sems) > 1:
                    return it * (self.times * self.by) + (k + 1) * self.by
                at = x * self.times + k if self.blocks else k * STREAMS + x
                return it * (self.times * STREAMS * self.by) + (at + 1) * self.by

        loaded = ctx.enter_context(nc.semaphore("weights_loaded"))
        setup_d = ctx.enter_context(nc.semaphore("setup_vector"))
        setup_p = ctx.enter_context(nc.semaphore("setup_tensor"))
        stored = ctx.enter_context(nc.semaphore("stored"))
        img_loaded = Signal("img_loaded", 1, 16, split=True)
        img_used = Signal("img_used")
        x_ready = Signal("x_ready", 1 + 4 + 1)
        sq_ready = Signal("sq_ready", 5)
        ms_mm = Signal("ms_mm", 5)
        ln_done = Signal("ln_done", 5 + 2 + 5 + 1)
        rs_ready = Signal("rs_ready", 5 + 2 + 5 + 1)
        h_ready = Signal("h_ready", 4)
        qk_mm = Signal("qk_mm", 2)
        v_mm = Signal("v_mm", 2)
        qk_ready = Signal("qk_ready", 2)
        v_ready = Signal("v_ready", 2)
        qm_ready = Signal("qm_ready", 2)
        max_mm = Signal("max_mm", 2 * 8)
        max_ready = Signal("max_ready", 2 * 8)
        score_mm = Signal("score_mm", 2 * 8)
        exp_ready = Signal("exp_ready", 2 * 8)
        pv_mm = Signal("pv_mm", 2)
        o_ready = Signal("o_ready", 2)
        sum_mm = Signal("sum_mm", 2)
        on_ready = Signal("on_ready", 2)
        wo_mm = Signal("wo_mm", 2)
        gu_mm = Signal("gu_mm", 2 * 3)
        sil_ready = Signal("sil_ready", 2 * 3)
        ff_ready = Signal("ff_ready", 2 * 3)
        down_mm = Signal("down_mm", 2)
        cen_mm = Signal("cen_mm", 5)
        csq_ready = Signal("csq_ready", 5)
        var_mm = Signal("var_mm", 5)
        z_ready = Signal("z_ready", 5)
        H_ready = Signal("H_ready", 3)
        Hy_ready = Signal("Hy_ready", NE, blocks=True)
        Hz_ready = Signal("Hz_ready")
        kq1_mm = Signal("kq1_mm")
        v0_mm = Signal("v0_mm")
        gel_ready = Signal("gel_ready")
        v0_ready = Signal("v0_ready")
        kq2_mm = Signal("kq2_mm")
        kq_ready = Signal("kq_ready")
        kqs_ready = Signal("kqs_ready")
        nn_mm = Signal("nn_mm")
        nmax_ready = Signal("nmax_ready")
        kqn_ready = Signal("kqn_ready")
        sc_mm = Signal("sc_mm")
        As_ready = Signal("As_ready")
        r_mm = Signal("r_mm")
        r_ready = Signal("r_ready")
        ao_mm = Signal("ao_mm")
        rt_mm = Signal("rt_mm")
        oh_ready = Signal("oh_ready")
        ohT_mm = Signal("ohT_mm")
        ohT_ready = Signal("ohT_ready")
        mk_mm = Signal("mk_mm", NE)
        mk_ready = Signal("mk_ready", NE)
        xe_ready = Signal("xe_ready", NE)
        hid_mm = Signal("hid_mm", NJ, blocks=True)
        hid_ready = Signal("hid_ready", NJ, blocks=True)
        y_mm = Signal("y_mm", NE + 1, blocks=True)
        ysel_ready = Signal("ysel_ready", NE, blocks=True)
        tc_mm = Signal("tc_mm", 2)
        tc_ready = Signal("tc_ready", 2)
        xh_ready = Signal("xh_ready", 2)
        xw_ready = Signal("xw_ready")
        xT_mm = Signal("xT_mm")
        xT_ready = Signal("xT_ready")
        pair_mm = Signal("pair_mm")
        am_ready = Signal("am_ready")
        ex_ready = Signal("ex_ready")
        p_ready = Signal("p_ready")
        pT_mm = Signal("pT_mm")
        pT_ready = Signal("pT_ready")
        att_mm = Signal("att_mm")
        att_ready = Signal("att_ready")
        gate_mm = Signal("gate_mm")
        gate_ready = Signal("gate_ready")
        gl_mm = Signal("gl_mm")
        gd_ready = Signal("gd_ready")
        ge_ready = Signal("ge_ready")
        wv_ready = Signal("wv_ready")
        h2_mm = Signal("h2_mm", E2, blocks=True)
        h2_ready = Signal("h2_ready", E2, blocks=True)
        wr_mm = Signal("wr_mm")
        wr_ready = Signal("wr_ready")
        lo_mm = Signal("lo_mm")
        low_ready = Signal("low_ready")
        ro_mm = Signal("ro_mm")
        out_ready = Signal("out_ready")
        CHAIN = 22
        own = Signal("vector_own", CHAIN, split=True)

        LOADS = 16 * (-(-WTOT // PIECE) - (-CTOT // PIECE))

        XS = range(STREAMS)
        STEPS = [(i, hp) for i in range(IMGS) for hp in range(HEADS // 2)]
        block = ctx.enter_context(nc.Block())

        @block.sync
        def _(sp):
            for dst, src, n in ((W, weights, WTOT), (C, consts, CTOT)):
                for a in range(0, n, PIECE):
                    sp.dma_start(dst[:, a:min(a + PIECE, n)], src[:, a:min(a + PIECE, n)]).then_inc(loaded, 16)

            def load(it, x):
                sp.dma_start(img[x][:, :, :], patches[it, x]).then_inc(img_loaded.of(x), 16)

            def store(it, x):
                sp.wait_ge(out_ready.of(x), out_ready.done(it, x))
                sp.dma_start(out[it, x], outS[x][:, :]).then_inc(stored, 16)

            for x in XS:
                load(0, x)
            with sp.Fori(0, iters - 1) as it:
                for x in XS:
                    sp.wait_ge(img_used.of(x), img_used.done(it, x))
                    load(it + 1, x)
                for x in XS:
                    store(it, x)
            for x in XS:
                store(iters - 1, x)
            sp.wait_ge(stored, 16 * STREAMS * iters)

        @block.gpsimd
        def _(pool):
            with pool.Fori(0, iters) as it:
                for x in XS:
                    pool.wait_ge(z_ready.of(x), z_ready.done(it, x, 0))
                    nc.gpsimd.tensor_tensor(X[x][:], X[x][:], z[x][:], ALU.add).then_inc(Hz_ready.of(x), 1)
                for x in XS:
                    Xf = X[x][:].rearrange("p i t -> p (i t)")
                    for e in range(NE):
                        pool.wait_ge(ysel_ready.of(x), ysel_ready.done(it, x, e))
                        if e:
                            pool.wait_ge(Hy_ready.of(x), Hy_ready.done(it, x, e - 1))
                        nc.gpsimd.tensor_tensor(Xf, Xf, ysel[x][:, e], ALU.add).then_inc(Hy_ready.of(x), 1)

        @block.scalar
        def _(act):
            nc.scalar.preload_act_table_set(LNEXP)
            act.wait_ge(setup_d, 1)

            def rsqrt_of(it, x, k, src, eps, dims=(P, 1)):
                rows = dims[0]
                nc.scalar.activation(lnv[x][0:rows, 0, 0:src.shape[-1]], src, ACT.Ln, bias=eps).then_inc(ln_done.of(x), 1)
                act.wait_ge(ln_done.of(x), ln_done.done(it, x, k))
                nc.scalar.activation(rs[x][0:rows, 0, 0:src.shape[-1]], lnv[x][0:rows, 0, 0:src.shape[-1]],
                                     ACT.Exp, scale=-0.5).then_inc(rs_ready.of(x), 1)

            def rms(it, o, k):
                for x in XS:
                    act.wait_ge(x_ready.of(x), x_ready.done(it, x, o))
                    nc.scalar.activation(sq[x][:, 0:IMGS * T].rearrange("p (i t) -> p i t", i=IMGS),
                                         X[x][:, :, 1:L], ACT.Square).then_inc(sq_ready.of(x), 1)
                for x in XS:
                    act.wait_ge(ms_mm.of(x), ms_mm.done(it, x, o))
                    rsqrt_of(it, x, k, bank(x, 0, IMGS * T), 1e-6)

            def layernorm(it, o, k):
                for x in XS:
                    act.wait_ge(cen_mm.of(x), cen_mm.done(it, x, o))
                    nc.scalar.activation(sq[x][:, :], bank(x, 0), ACT.Square).then_inc(csq_ready.of(x), 1)
                for x in XS:
                    act.wait_ge(var_mm.of(x), var_mm.done(it, x, o))
                    rsqrt_of(it, x, k, bank(x, 1), 1e-5)

            with act.Fori(0, iters) as it:
                nc.scalar.preload_act_table_set(LNEXP)
                for l in range(2):
                    rms(it, 2 * l, 3 * l)
                    for x in XS:
                        act.wait_ge(qk_mm.of(x), qk_mm.done(it, x, l))
                        nc.scalar.copy(qS[x].rearrange("p i t -> p (i t)"), bank(x, 1, IMGS * T))
                        nc.scalar.copy(kS[x][:].rearrange("p i t -> p (i t)"), bank(x, 2, IMGS * T)).then_inc(qk_ready.of(x), 1)
                    for s in range(len(STEPS)):
                        for x in XS:
                            act.wait_ge(score_mm.of(x), score_mm.done(it, x, 8 * l + s))
                            for cc, (_, m) in enumerate(TC):
                                last = nc.scalar.activation(pt[x][0:m, cc].rearrange("p a t -> p (a t)"),
                                                            bank(x, cc, 2 * T, rows=m), ACT.Exp)
                            last.then_inc(exp_ready.of(x), 1)
                    for x in XS:
                        act.wait_ge(pv_mm.of(x), pv_mm.done(it, x, l))
                        nc.scalar.copy(oS[x], banks(x, 2, IMGS * T)).then_inc(o_ready.of(x), 1)
                    for x in XS:
                        act.wait_ge(sum_mm.of(x), sum_mm.done(it, x, l))
                        nc.scalar.activation(lnv[x][:, :, 0:IMGS * T], banks(x, 0, IMGS * T), ACT.Ln).then_inc(ln_done.of(x), 1)
                        act.wait_ge(ln_done.of(x), ln_done.done(it, x, 3 * l + 1))
                        nc.scalar.activation(rs[x][:, :, 0:IMGS * T], lnv[x][:, :, 0:IMGS * T], ACT.Exp,
                                             scale=-1.0).then_inc(rs_ready.of(x), 1)
                    rms(it, 2 * l + 1, 3 * l + 2)
                    for j, (_, m) in enumerate(FCH):
                        for x in XS:
                            act.wait_ge(gu_mm.of(x), gu_mm.done(it, x, 3 * l + j))
                            nc.scalar.activation(sil[x][0:m, j], bank(x, (2 * j) % 4, IMGS * T, rows=m),
                                                 ACT.Silu).then_inc(sil_ready.of(x), 1)
                    nc.scalar.preload_act_table_set(LNEXP)
                rms(it, 4, 6)
                layernorm(it, 0, 7)
                for x in XS:
                    act.wait_ge(kq1_mm.of(x), kq1_mm.done(it, x))
                    nc.scalar.activation(gel[x][:, 0], bank(x, 2), ACT.Gelu, bias=w("k_b1"))
                    nc.scalar.activation(gel[x][:, 1], bank(x, 3), ACT.Gelu, bias=w("q_b1")).then_inc(gel_ready.of(x), 1)
                nc.scalar.preload_act_table_set(LNEXP)
                for x in XS:
                    act.wait_ge(kq2_mm.of(x), kq2_mm.done(it, x))
                    for s, b in enumerate(("k_b2", "q_b2")):
                        last = nc.scalar.activation(kq[x][:, s].rearrange("p i t -> p (i t)"), bank(x, 2 + s, rows=KD),
                                                    ACT.Identity, bias=w(b, rows=KD))
                    last.then_inc(kq_ready.of(x), 1)
                for x in XS:
                    act.wait_ge(nmax_ready.of(x), nmax_ready.done(it, x))
                    nc.scalar.activation(lnv[x][0:KD], kqs[x], ACT.Ln, scale=TINY).then_inc(ln_done.of(x), 1)
                    act.wait_ge(ln_done.of(x), ln_done.done(it, x, 8))
                    nc.scalar.activation(rs[x][0:KD], lnv[x][0:KD], ACT.Exp, scale=-0.5).then_inc(rs_ready.of(x), 1)
                for x in XS:
                    act.wait_ge(r_mm.of(x), r_mm.done(it, x))
                    nc.scalar.copy(rS[x], bank(x, 0)).then_inc(r_ready.of(x), 1)
                layernorm(it, 1, 9)
                layernorm(it, 2, 10)
                for x in XS:
                    act.wait_ge(ohT_mm.of(x), ohT_mm.done(it, x))
                    nc.scalar.copy(ohT[x][:], bank(x, 3, rows=NE))
                    nc.scalar.copy(ohTb[x][:], bank(x, 3, rows=NE)).then_inc(ohT_ready.of(x), 1)
                for e in range(NE):
                    for x in XS:
                        act.wait_ge(mk_mm.of(x), mk_mm.done(it, x, e))
                        nc.scalar.copy(mk[x][:, e], bank(x, 2 + e % 2)).then_inc(mk_ready.of(x), 1)
                for x in XS:
                    for j in range(NJ):
                        act.wait_ge(hid_mm.of(x), hid_mm.done(it, x, j))
                        nc.scalar.activation(hid[x][:, j], bank(x, j), ACT.Relu).then_inc(hid_ready.of(x), 1)
                layernorm(it, 3, 11)
                for i in range(2):
                    for x in XS:
                        act.wait_ge(tc_mm.of(x), tc_mm.done(it, x, i))
                        if i:
                            act.wait_ge(xh_ready.of(x), xh_ready.done(it, x, 0))
                        nc.scalar.activation(tS[x], bank(x, 2 - 2 * i), ACT.Relu, bias=w("tb", i, i + 1))
                        nc.scalar.activation(cS[x], bank(x, 3 - 2 * i), ACT.Sigmoid, bias=w("cb", i, i + 1)).then_inc(tc_ready.of(x), 1)
                nc.scalar.preload_act_table_set(LNEXP)
                for x in XS:
                    act.wait_ge(xT_mm.of(x), xT_mm.done(it, x))
                    for cc, (_, m) in enumerate(LC):
                        last = nc.scalar.copy(xTS[x][0:m, :, cc],
                                              bank(x, 2, 512, rows=m).rearrange("p (i c d) -> p i c d", i=IMGS, c=2)[:, :, cc])
                    last.then_inc(xT_ready.of(x), 1)
                for x in XS:
                    act.wait_ge(am_ready.of(x), am_ready.done(it, x))
                    for i in range(IMGS):
                        for cc, (_, m) in enumerate(LC):
                            last = nc.scalar.activation(aS[x][0:m, i, cc], aS[x][0:m, i, cc], ACT.Exp,
                                                        bias=am[x][0:m, 0, i, cc:cc + 1],
                                                        accum_out=am[x][0:m, 1, i, cc:cc + 1])
                    last.then_inc(ex_ready.of(x), 1)
                for x in XS:
                    act.wait_ge(pT_mm.of(x), pT_mm.done(it, x))
                    for cc, (_, m) in enumerate(LC):
                        last = nc.scalar.copy(pTS[x][0:m, :, cc], banks(x, 0, L, rows=m, a=cc * L))
                    last.then_inc(pT_ready.of(x), 1)
                for x in XS:
                    act.wait_ge(att_mm.of(x), att_mm.done(it, x))
                    nc.scalar.copy(att[x], bank(x, 2)).then_inc(att_ready.of(x), 1)
                for x in XS:
                    act.wait_ge(gate_mm.of(x), gate_mm.done(it, x))
                    nc.scalar.activation(tS[x], bank(x, 0), ACT.Sigmoid, bias=w("ffb"))
                    nc.scalar.activation(cS[x], bank(x, 1), ACT.Sigmoid, bias=w("frb")).then_inc(gate_ready.of(x), 1)
                nc.scalar.preload_act_table_set(LNEXP)
                layernorm(it, 4, 12)
                for x in XS:
                    act.wait_ge(gd_ready.of(x), gd_ready.done(it, x))
                    nc.scalar.activation(gl[x][:, 1], gl[x][:, 0], ACT.Exp).then_inc(ge_ready.of(x), 1)
                    for e in range(E2):
                        act.wait_ge(h2_mm.of(x), h2_mm.done(it, x, e))
                        nc.scalar.activation(hid[x][:, e], bank(x, e % 2), ACT.Relu).then_inc(h2_ready.of(x), 1)
                for x in XS:
                    act.wait_ge(wr_mm.of(x), wr_mm.done(it, x))
                    nc.scalar.copy(wr[x], bank(x, 2, rows=E2 * R2)).then_inc(wr_ready.of(x), 1)

        @block.vector
        def _(dve):
            dve.wait_ge(loaded, LOADS)
            V = nc.vector
            V.tensor_copy(identb[:], c("ident"))
            V.tensor_copy(expselb[:].rearrange("p e n -> p (e n)"), c("expsel", rows=NE))
            for x in XS:
                V.memset(va[x][:], 1.0)
            V.tensor_scalar(w1row[:], c("one"), w("aw", 0, 1), None, ALU.mult)
            V.tensor_scalar(owg[:], w("o_w"), w("ln_g"), None, ALU.mult)
            for l in range(2):
                V.tensor_scalar(w(f"qkv{l}", 0, D), w(f"qkv{l}", 0, D), w(f"ln1_{l}"), DH ** -0.5, ALU.mult, ALU.mult)
                V.tensor_scalar(w(f"qkv{l}", D), w(f"qkv{l}", D), w(f"ln1_{l}"), None, ALU.mult)
                V.tensor_scalar(w(f"gate{l}"), w(f"gate{l}"), w(f"ln2_{l}"), None, ALU.mult)
                V.tensor_scalar(w(f"up{l}"), w(f"up{l}"), w(f"ln2_{l}"), None, ALU.mult)
            V.tensor_scalar(w("pos", 1), w("pos", 1), w("conv_b"), None, ALU.add)
            V.tensor_scalar(w("pos", 0, 1), w("pos", 0, 1), w("cls_token"), None, ALU.add).then_inc(setup_d, 1)
            dve.wait_ge(setup_p, 1)
            V.tensor_scalar(obp[:], bank(0, 0, 1), w("o_b"), None, ALU.add)
            V.tensor_copy(G[:], bank(0, 1, D, rows=E2 * R2)).then_inc(setup_d, 1)

            with dve.Fori(0, iters) as it:
                seen = [0] * STREAMS

                def then(x, ins):
                    ins.then_inc(own.of(x), 1)
                    dve.wait_ge(own.of(x), own.done(it, x, seen[x]))
                    seen[x] += 1

                def scale_h(o, k):
                    for x in XS:
                        dve.wait_ge(rs_ready.of(x), rs_ready.done(it, x, k))
                        V.tensor_tensor(h[x][:], X[x][:, :, 1:L],
                                        rs[x][:, 0, 0:IMGS * T].rearrange("p (i t) -> p i t", i=IMGS),
                                        ALU.mult).then_inc(h_ready.of(x), 1)

                def add_x(x, b, sig, k, r, at=1):
                    dve.wait_ge(sig.of(x), sig.done(it, x, k))
                    V.tensor_tensor(X[x][:, :, at:L], X[x][:, :, at:L],
                                    bank(x, b, IMGS * (L - at)).rearrange("p (i t) -> p i t", i=IMGS),
                                    ALU.add).then_inc(r[0].of(x), 1)

                def scale_z(o, k, dst):
                    for x in XS:
                        dve.wait_ge(rs_ready.of(x), rs_ready.done(it, x, k))
                        V.tensor_tensor(dst[x][:].rearrange("p i t -> p (i t)") if dst is z else dst[x][:],
                                        bank(x, 0), rs[x][:, 0], ALU.mult).then_inc(z_ready.of(x), 1)

                for x in XS:
                    dve.wait_ge(img_used.of(x), img_used.done(it, x))
                    V.tensor_tensor(X[x][:, :, 2:L], bank(x, 1, IMGS * NPATCH).rearrange("p (i t) -> p i t", i=IMGS),
                                    w("pos", 1).unsqueeze(1).broadcast_to([P, IMGS, NPATCH]), ALU.add)
                    V.tensor_copy(X[x][:, :, 1:2], w("pos", 0, 1).unsqueeze(1).broadcast_to([P, IMGS, 1])).then_inc(x_ready.of(x), 1)
                for l in range(2):
                    scale_h(2 * l, 3 * l)
                    for x in XS:
                        dve.wait_ge(v_mm.of(x), v_mm.done(it, x, l))
                        for cc, (_, m) in enumerate(TC):
                            src = bank(x, 3, 512, rows=m).rearrange("p (i c h d) -> p i c h d", i=IMGS, c=2, h=HEADS)
                            for i in range(IMGS):
                                last = V.tensor_copy(va[x][0:m, i, cc, :, 0:DH], src[:, i, cc])
                        last.then_inc(v_ready.of(x), 1)
                        dve.wait_ge(qk_ready.of(x), qk_ready.done(it, x, l))
                        for hd in range(HEADS):
                            last = V.tensor_scalar(qm[x][:, hd], qS[x], c("hmask", hd, hd + 1), None, ALU.mult)
                        last.then_inc(qm_ready.of(x), 1)
                    for s, (i, hp) in enumerate(STEPS):
                        for x in XS:
                            dve.wait_ge(max_mm.of(x), max_mm.done(it, x, 8 * l + s))
                            for cc, (_, m) in enumerate(TC):
                                last = V.tensor_reduce(nm[x][0:m, i, cc, 2 * hp:2 * hp + 2],
                                                       bank(x, 2 * (s % 2) + cc, 2 * T, rows=m).rearrange("p (a t) -> p a t", a=2),
                                                       AX.X, ALU.max, negate=True)
                            last.then_inc(max_ready.of(x), 1)
                    for x in XS:
                        dve.wait_ge(rs_ready.of(x), rs_ready.done(it, x, 3 * l + 1))
                        V.tensor_tensor(on[x], oS[x], rs[x][:, :, 0:IMGS * T], ALU.mult).then_inc(on_ready.of(x), 1)
                    for x in XS:
                        add_x(x, 2, wo_mm, l, (x_ready,))
                    scale_h(2 * l + 1, 3 * l + 2)
                    for j, (_, m) in enumerate(FCH):
                        for x in XS:
                            dve.wait_ge(sil_ready.of(x), sil_ready.done(it, x, 3 * l + j))
                            V.tensor_tensor(ff[x][0:m, j], sil[x][0:m, j], bank(x, (2 * j + 1) % 4, IMGS * T, rows=m),
                                            ALU.mult).then_inc(ff_ready.of(x), 1)
                    for x in XS:
                        add_x(x, 2, down_mm, l, (x_ready,))
                for x in XS:
                    dve.wait_ge(rs_ready.of(x), rs_ready.done(it, x, 6))
                    V.scalar_tensor_tensor(X[x][:, :, 1:L], X[x][:, :, 1:L], w("ln_f"),
                                           rs[x][:, 0, 0:IMGS * T].rearrange("p (i t) -> p i t", i=IMGS),
                                           ALU.mult, ALU.mult)
                    V.tensor_copy(X[x][:, :, 0:1], w("cls_tok").unsqueeze(1).broadcast_to([P, IMGS, 1])).then_inc(x_ready.of(x), 1)
                scale_z(0, 7, z)
                for x in XS:
                    dve.wait_ge(v0_mm.of(x), v0_mm.done(it, x))
                    for cc, (_, m) in enumerate(LC):
                        src = bank(x, 0, 512, rows=m).rearrange("p (i c d) -> p i c d", i=IMGS, c=2)
                        last = V.tensor_tensor(vS[x][0:m, :, cc], src[:, :, cc],
                                               w("v_b", rows=m).unsqueeze(1).broadcast_to([m, IMGS, D]), ALU.add)
                    last.then_inc(v0_ready.of(x), 1)
                for x in XS:
                    dve.wait_ge(kq_ready.of(x), kq_ready.done(it, x))
                    kqf = kq[x].rearrange("p s i t -> p s (i t)")
                    V.tensor_tensor(kqs[x], kqf, kqf, ALU.mult).then_inc(kqs_ready.of(x), 1)
                for x in XS:
                    dve.wait_ge(nn_mm.of(x), nn_mm.done(it, x))
                    V.tensor_scalar(kqs[x], banks(x, 0, N, rows=KD), 1e-24, None, ALU.max).then_inc(nmax_ready.of(x), 1)
                for x in XS:
                    dve.wait_ge(rs_ready.of(x), rs_ready.done(it, x, 8))
                    kqf = kq[x].rearrange("p s i t -> p s (i t)")
                    V.scalar_tensor_tensor(kqf, kqf, TINY ** 0.5, rs[x][0:KD], ALU.mult, ALU.mult).then_inc(kqn_ready.of(x), 1)
                for x in XS:
                    dve.wait_ge(sc_mm.of(x), sc_mm.done(it, x))
                    for a, n, m in ((0, L, P), (L, LC[1][1], LC[1][1])):
                        last = V.tensor_tensor(As[x][0:m, :, a:a + n], banks(x, 2, n, rows=m, a=a),
                                               c("causal", a, a + n, rows=m).unsqueeze(1).broadcast_to([m, IMGS, n]), ALU.mult)
                    last.then_inc(As_ready.of(x), 1)
                scale_z(1, 9, zn)
                for x in XS:
                    dve.wait_ge(ao_mm.of(x), ao_mm.done(it, x))
                    dve.wait_ge(Hz_ready.of(x), Hz_ready.done(it, x))
                    Xf = X[x][:].rearrange("p i t -> p (i t)")
                    V.scalar_tensor_tensor(Xf, bank(x, 2), obp[:], Xf, ALU.add, ALU.add).then_inc(H_ready.of(x), 1)
                scale_z(2, 10, z)
                for x in XS:
                    dve.wait_ge(rt_mm.of(x), rt_mm.done(it, x))
                    g = lg[x]

                    def flat(k):
                        return g[:, k].rearrange("p c e -> p (c e)")

                    def spread(k):
                        return lgs[x][:, k].unsqueeze(2).broadcast_to([TK, NTK, NE])
                    then(x, V.tensor_tensor(flat(0), bank(x, 2, NTK * NE, rows=TK), w("br", rows=TK), ALU.add))
                    then(x, V.tensor_reduce(lgs[x][:, 0], g[:, 0], AX.X, ALU.max))
                    then(x, V.tensor_tensor(g[:, 1], g[:, 0], spread(0), ALU.is_ge))
                    then(x, V.tensor_tensor(flat(2), flat(1), c("iota", rows=TK), ALU.mult))
                    then(x, V.tensor_reduce(lgs[x][:, 1], g[:, 2], AX.X, ALU.min))
                    V.tensor_tensor(g[:, 3], c("iota", rows=TK).rearrange("p (c e) -> p c e", e=NE),
                                    spread(1), ALU.is_equal).then_inc(oh_ready.of(x), 1)
                for e in range(NE):
                    for x in XS:
                        dve.wait_ge(mk_ready.of(x), mk_ready.done(it, x, e))
                        V.tensor_tensor(xe[x][:, e], z[x][:].rearrange("p i t -> p (i t)"), mk[x][:, e], ALU.mult).then_inc(xe_ready.of(x), 1)
                for x in XS:
                    for e in range(NE):
                        dve.wait_ge(y_mm.of(x), y_mm.done(it, x, e))
                        V.tensor_tensor(ysel[x][:, e], bank(x, e % 4), mk[x][:, e], ALU.mult).then_inc(ysel_ready.of(x), 1)
                for x in XS:
                    Xf = X[x][:].rearrange("p i t -> p (i t)")
                    dve.wait_ge(y_mm.of(x), y_mm.done(it, x, NE))
                    dve.wait_ge(Hy_ready.of(x), Hy_ready.done(it, x, NE - 1))
                    V.tensor_tensor(Xf, Xf, bank(x, 0), ALU.add).then_inc(H_ready.of(x), 1)
                scale_z(3, 11, z)
                for i in range(2):
                    for x in XS:
                        src = (z[x][:] if i == 0 else xh[x][:, 0]).rearrange("p i t -> p (i t)")
                        dve.wait_ge(tc_ready.of(x), tc_ready.done(it, x, i))
                        then(x, V.tensor_tensor(dS[x], tS[x], src, ALU.subtract))
                        then(x, V.tensor_tensor(dS[x], dS[x], cS[x], ALU.mult))
                        V.tensor_tensor(xh[x][:, i].rearrange("p i t -> p (i t)"), dS[x], src, ALU.add).then_inc(xh_ready.of(x), 1)
                for x in XS:
                    dve.wait_ge(xh_ready.of(x), xh_ready.done(it, x, 1))
                    V.tensor_scalar(xw[x], xh[x][:, 1], w("aw", 2, 3), w("aw", 1, 2), ALU.mult, ALU.add).then_inc(xw_ready.of(x), 1)
                for x in XS:
                    dve.wait_ge(pair_mm.of(x), pair_mm.done(it, x))
                    for cc, (_, m) in enumerate(LC):
                        last = V.tensor_scalar(aS[x][0:m, :, cc], banks(x, 0, L, rows=m, a=cc * L), w("ab", rows=m), 0.0, ALU.add, ALU.max)
                    then(x, last)
                    for cc, (_, m) in enumerate(LC):
                        last = V.tensor_reduce(am[x][0:m, 0, :, cc], aS[x][0:m, :, cc], AX.X, ALU.max, negate=True)
                    last.then_inc(am_ready.of(x), 1)
                for x in XS:
                    dve.wait_ge(ex_ready.of(x), ex_ready.done(it, x))
                    for cc, (_, m) in enumerate(LC):
                        last = V.reciprocal(am[x][0:m, 2, :, cc], am[x][0:m, 1, :, cc])
                    then(x, last)
                    for cc, (_, m) in enumerate(LC):
                        last = V.tensor_tensor(aS[x][0:m, :, cc], aS[x][0:m, :, cc],
                                               am[x][0:m, 2, :, cc].unsqueeze(2).broadcast_to([m, IMGS, L]), ALU.mult)
                    last.then_inc(p_ready.of(x), 1)
                for x in XS:
                    dve.wait_ge(gate_ready.of(x), gate_ready.done(it, x))
                    zf = z[x][:].rearrange("p i t -> p (i t)")
                    Xf = X[x][:].rearrange("p i t -> p (i t)")
                    V.tensor_tensor(cS[x], cS[x], zf, ALU.mult)
                    then(x, V.tensor_tensor(tS[x], tS[x], tS[x], ALU.mult))
                    then(x, V.tensor_tensor(tS[x], tS[x], cS[x], ALU.add))
                    V.tensor_tensor(Xf, Xf, tS[x], ALU.add).then_inc(H_ready.of(x), 1)
                scale_z(4, 12, z)
                for x in XS:
                    dve.wait_ge(gl_mm.of(x), gl_mm.done(it, x))
                    g, s = gl[x], gs[x]
                    lo = bank(x, 2, NTK * (E2 + 1), rows=TK).rearrange("p (c e) -> p c e", c=NTK)

                    def over(k, n=E2):
                        return s[:, k].unsqueeze(2).broadcast_to([TK, NTK, n])
                    V.tensor_scalar(g[:, 0, :, E2:], lo[:, :, E2:], -1.0, None, ALU.mult)
                    then(x, V.tensor_reduce(s[:, 0], lo[:, :, 0:E2], AX.X, ALU.max))
                    V.tensor_tensor(g[:, 0, :, 0:E2], lo[:, :, 0:E2], over(0), ALU.subtract).then_inc(gd_ready.of(x), 1)
                    dve.wait_ge(ge_ready.of(x), ge_ready.done(it, x))
                    V.tensor_reduce(s[:, 1], g[:, 1, :, 0:E2], AX.X, ALU.add)
                    then(x, V.tensor_scalar(s[:, 2], g[:, 1, :, E2], 1.0, None, ALU.add))
                    then(x, V.reciprocal(s[:, 3:5], s[:, 1:3]))
                    then(x, V.tensor_tensor(g[:, 2, :, 0:E2], g[:, 1, :, 0:E2], over(3), ALU.mult))
                    then(x, V.scalar_tensor_tensor(g[:, 2, :, 0:E2], over(4), -1.0 / E2, g[:, 2, :, 0:E2], ALU.mult, ALU.add))
                    then(x, V.tensor_scalar(g[:, 3, :, 0:E2], g[:, 2, :, 0:E2], 0.0, None, ALU.max))
                    then(x, V.tensor_reduce(s[:, 5], g[:, 3, :, 0:E2], AX.X, ALU.add))
                    then(x, V.scalar_tensor_tensor(s[:, 6], s[:, 5], 0.0, s[:, 5], ALU.is_equal, ALU.add))
                    then(x, V.reciprocal(s[:, 7], s[:, 6]))
                    V.tensor_tensor(wrep[x][:], g[:, 3, :, 0:E2].unsqueeze(3).broadcast_to([TK, NTK, E2, R2]),
                                    s[:, 7].unsqueeze(2).unsqueeze(3).broadcast_to([TK, NTK, E2, R2]),
                                    ALU.mult).then_inc(wv_ready.of(x), 1)
                for x in XS:
                    dve.wait_ge(wr_ready.of(x), wr_ready.done(it, x))
                    dve.wait_ge(lo_mm.of(x), lo_mm.done(it, x))
                    V.tensor_tensor(low[x], wr[x], bank(x, 3, rows=E2 * R2), ALU.mult).then_inc(low_ready.of(x), 1)
                for x in XS:
                    dve.wait_ge(ro_mm.of(x), ro_mm.done(it, x))
                    V.tensor_tensor(outS[x][:], X[x][:].rearrange("p i t -> p (i t)"), bank(x, 0), ALU.add).then_inc(out_ready.of(x), 1)
                dve.wait_ge(out_ready.of(STREAMS - 1), out_ready.done(it, STREAMS - 1))
                dve.wait_ge(stored, it * (16 * STREAMS) + 16 * STREAMS)
                assert seen == [CHAIN] * STREAMS, seen

        @block.tensor
        def _(pe):
            mm = nc.tensor.matmul

            def flat(t):
                return t.rearrange("p i t -> p (i t)")
            pe.wait_ge(setup_d, 1)
            mm(bank(0, 0, 1), w("o_w"), w("ln_b"), start=True, stop=True)
            for e in range(E2):
                last = mm(bank(0, 1, D, rows=E2 * R2), w("lB", 64 * e, 64 * e + 64), w("fc2", D * e, D * e + D),
                          start=(e == 0), stop=(e == E2 - 1))
            last.then_inc(setup_p, 1)
            pe.wait_ge(setup_d, 2)

            with pe.Fori(0, iters) as it:
                def wait(x, sig, k=0):
                    pe.wait_ge(sig.of(x), sig.done(it, x, k))

                def unit(x, b, lhsT, rhs, sig=None, rows=P, n=N):
                    r = mm(bank(x, b, n, rows=rows), lhsT, rhs, start=True, stop=True)
                    if sig is not None:
                        r.then_inc(sig.of(x), 1)

                def mean_square(o):
                    for x in XS:
                        wait(x, sq_ready, o)
                        unit(x, 0, c("mean"), sq[x][:, 0:IMGS * T], ms_mm, n=IMGS * T)

                def layernorm(o, src, sig, k):
                    for x in XS:
                        wait(x, sig, k)
                        unit(x, 0, c("centre"), src(x), cen_mm)
                    for x in XS:
                        wait(x, csq_ready, o)
                        unit(x, 1, c("mean"), sq[x][:], var_mm)

                for x in XS:
                    pe.wait_ge(img_loaded.of(x), img_loaded.done(it, x))
                    for k in range(KP):
                        last = mm(bank(x, 1, IMGS * NPATCH), w("conv", D * k, D * k + D), img[x][:, k],
                                  start=(k == 0), stop=(k == KP - 1))
                    last.then_inc(img_used.of(x), 1)
                for l in range(2):
                    mean_square(2 * l)
                    for x in XS:
                        wait(x, h_ready, 2 * l)
                        unit(x, 1, w(f"qkv{l}", 0, D), flat(h[x][:]), n=IMGS * T)
                        unit(x, 2, w(f"qkv{l}", D, 2 * D), flat(h[x][:]), qk_mm, n=IMGS * T)
                        for i in range(IMGS):
                            for cc, (t0, m) in enumerate(TC):
                                last = mm(bank(x, 3, D, rows=m, a=(2 * i + cc) * D), h[x][:, i, t0:t0 + m],
                                          w(f"qkv{l}", 2 * D), start=True, stop=True)
                        last.then_inc(v_mm.of(x), 1)

                    for s, (i, hp) in enumerate(STEPS):
                        for x in XS:
                            if s == 0:
                                wait(x, qm_ready, l)
                            elif s == 1:
                                wait(x, v_ready, l)
                            else:
                                wait(x, max_ready, 8 * l + s - 2)
                            for cc, (t0, m) in enumerate(TC):
                                for a in range(2):
                                    q = qm[x][:, 2 * hp + a, i, t0:t0 + m].bitcast(bf16)[:, 1::2]
                                    k = kS[x][:, i].bitcast(bf16)[:, 1::2]
                                    last = mm(bank(x, 2 * (s % 2) + cc, T, rows=m, a=a * T), q, k, start=True, stop=True)
                            last.then_inc(max_mm.of(x), 1)

                    def scores(x, s):
                        i, hp = STEPS[s]
                        if s == 0:
                            wait(x, max_ready, 8 * l + 7)
                        for cc, (s0, ms) in enumerate(TC):
                            mm(bank(x, cc, 2 * T, rows=ms), kS[x][:, i, s0:s0 + ms], qm[x][:, 2 * hp:2 * hp + 2, i],
                               start=True, stop=False)
                            for a in range(2):
                                for tc, (t0, mt) in enumerate(TC):
                                    last = mm(bank(x, cc, mt, rows=ms, a=a * T + t0),
                                              nm[x][0:mt, i, tc, 2 * hp + a:2 * hp + a + 1].broadcast_to([mt, ms]),
                                              identb[0:mt, 0:mt], start=False, stop=(a == 1 and tc == 1))
                        last.then_inc(score_mm.of(x), 1)

                    def values(x, s):
                        i, hp = STEPS[s]
                        wait(x, exp_ready, 8 * l + s)
                        for a in range(2):
                            hd = 2 * hp + a
                            g = BLK * (hd % 4)
                            for cc, (_, m) in enumerate(TC):
                                last = mm(bank(x, 2 + hd // 4, T, rows=BLK, a=i * T, row0=g), va[x][0:m, i, cc, hd],
                                          pt[x][0:m, cc, a], start=(cc == 0), stop=(cc == 1), tile_position=(0, g))
                        if s == len(STEPS) - 1:
                            last.then_inc(pv_mm.of(x), 1)

                    scores(0, 0)
                    for s in range(len(STEPS)):
                        scores(1, s)
                        values(0, s)
                        if s + 1 < len(STEPS):
                            scores(0, s + 1)
                        values(1, s)
                    for x in XS:
                        wait(x, o_ready, l)
                        for g in range(2):
                            unit(x, g, c("sel"), oS[x][:, g], sum_mm if g else None, n=IMGS * T)
                    for x in XS:
                        wait(x, on_ready, l)
                        for g in range(2):
                            last = mm(bank(x, 2, IMGS * T), w(f"wo{l}", D * g, D * g + D), on[x][:, g],
                                      start=(g == 0), stop=(g == 1))
                        last.then_inc(wo_mm.of(x), 1)
                    mean_square(2 * l + 1)
                    for j, (f0, m) in enumerate(FCH):
                        for x in XS:
                            if j == 0:
                                wait(x, h_ready, 2 * l + 1)
                            if j == 2:
                                wait(x, ff_ready, 3 * l)
                            b = (2 * j) % 4
                            unit(x, b, w(f"gate{l}", f0, f0 + m), flat(h[x][:]), None, m, IMGS * T)
                            unit(x, b + 1, w(f"up{l}", f0, f0 + m), flat(h[x][:]), gu_mm, m, IMGS * T)
                    for x in XS:
                        wait(x, ff_ready, 3 * l + 2)
                        for j, (_, m) in enumerate(FCH):
                            last = mm(bank(x, 2, IMGS * T), w(f"down{l}", D * j, D * j + D, rows=m), ff[x][0:m, j],
                                      start=(j == 0), stop=(j == 2))
                        last.then_inc(down_mm.of(x), 1)
                mean_square(4)

                layernorm(0, lambda x: flat(X[x][:]), x_ready, 5)
                for x in XS:
                    wait(x, z_ready, 0)
                    unit(x, 2, w("k_w1"), flat(z[x][:]))
                    unit(x, 3, w("q_w1"), flat(z[x][:]), kq1_mm)
                    for i in range(IMGS):
                        for cc, (t0, m) in enumerate(LC):
                            last = mm(bank(x, 0, D, rows=m, a=(2 * i + cc) * D), z[x][:, i, t0:t0 + m], w("v_w"),
                                      start=True, stop=True)
                    last.then_inc(v0_mm.of(x), 1)
                for x in XS:
                    wait(x, gel_ready)
                    unit(x, 2, w("k_w2"), gel[x][:, 0], rows=KD)
                    unit(x, 3, w("q_w2"), gel[x][:, 1], kq2_mm, rows=KD)
                for x in XS:
                    wait(x, kqs_ready)
                    wait(x, v0_ready)
                    for s in range(2):
                        unit(x, s, c("ones", rows=KD), kqs[x][:, s], nn_mm if s else None)
                for x in XS:
                    wait(x, kqn_ready)
                    for i in range(IMGS):
                        last = mm(bank(x, 2 + i, L, rows=P), kq[x][:, 0, i, 0:P], kq[x][:, 1, i, :], start=True, stop=True)
                        last = mm(bank(x, 2 + i, LC[1][1], rows=LC[1][1], a=L), kq[x][:, 0, i, P:L], kq[x][:, 1, i, P:L],
                                  start=True, stop=True)
                    last.then_inc(sc_mm.of(x), 1)
                for x in XS:
                    wait(x, As_ready)
                    for i in range(IMGS):
                        mm(bank(x, 0, L, a=i * L), vS[x][:, i, 0], As[x][:, i, 0:L], start=True, stop=False)
                        last = mm(bank(x, 0, LC[1][1], a=i * L + P), vS[x][0:LC[1][1], i, 1], As[x][0:LC[1][1], i, L:],
                                  start=False, stop=True)
                    last.then_inc(r_mm.of(x), 1)
                layernorm(1, lambda x: rS[x], r_ready, 0)
                for x in XS:
                    wait(x, z_ready, 1)
                    unit(x, 2, owg[:], zn[x], ao_mm)

                layernorm(2, lambda x: flat(X[x][:]), H_ready, 0)
                for x in XS:
                    wait(x, z_ready, 2)
                    zf = flat(z[x][:])
                    for k in range(NTK):
                        last = mm(bank(x, 2, NE, rows=TK, a=NE * k), zf[:, TK * k:TK * k + TK], w("Wr"), start=True, stop=True)
                    last.then_inc(rt_mm.of(x), 1)
                for x in XS:
                    wait(x, oh_ready)
                    for k in range(NTK):
                        last = mm(bank(x, 3, TK, rows=NE, a=TK * k), lg[x][:, 3, k], c("ident", 0, TK, rows=TK), start=True, stop=True)
                    last.then_inc(ohT_mm.of(x), 1)
                for e in range(NE):
                    for x in XS:
                        if e == 0:
                            wait(x, ohT_ready)
                        if e >= 2:
                            wait(x, mk_ready, e - 2)
                        unit(x, 2 + e % 2, expselb[:, e], ohTb[x][:], mk_mm)
                for x in XS:
                    wait(x, mk_ready, NE - 1)
                    for j in range(NJ):
                        mm(bank(x, j), w("b1", P * j, P * j + P, rows=NE), ohT[x][:], start=True, stop=False)
                        for e in range(NE):
                            if j == 0:
                                wait(x, xe_ready, e)
                            last = mm(bank(x, j), w("W1", HID * e + P * j, HID * e + P * j + P), xe[x][:, e],
                                      start=False, stop=(e == NE - 1))
                        last.then_inc(hid_mm.of(x), 1)
                for x in XS:
                    for e in range(NE):
                        if e >= 4:
                            wait(x, ysel_ready, e - 4)
                        for j in range(NJ):
                            if e == 0:
                                wait(x, hid_ready, j)
                            o = (e * NJ + j) * D
                            last = mm(bank(x, e % 4), w("W2", o, o + D), hid[x][:, j], start=(j == 0), stop=(j == NJ - 1))
                        last.then_inc(y_mm.of(x), 1)
                    wait(x, ysel_ready, 4)
                    unit(x, 0, w("b2", rows=NE), ohT[x][:], y_mm)

                layernorm(3, lambda x: flat(X[x][:]), H_ready, 1)
                for i in range(2):
                    for x in XS:
                        wait(x, z_ready if i == 0 else xh_ready, 3 if i == 0 else 0)
                        src = flat(z[x][:]) if i == 0 else flat(xh[x][:, 0])
                        unit(x, 2 - 2 * i, w("tW", D * i, D * i + D), src)
                        unit(x, 3 - 2 * i, w("cW", D * i, D * i + D), src, tc_mm)
                for x in XS:
                    wait(x, xh_ready, 1)
                    for i in range(IMGS):
                        for cc, (t0, m) in enumerate(LC):
                            last = nc.tensor.transpose(bank(x, 2, D, rows=m, a=(2 * i + cc) * D), xh[x][:, 1, i, t0:t0 + m], c("ident"))
                    last.then_inc(xT_mm.of(x), 1)
                for x in XS:
                    wait(x, xw_ready)
                    for i in range(IMGS):
                        for cc, (t0, m) in enumerate(LC):
                            mm(bank(x, i, L, rows=m, a=cc * L), xw[x][:, i, t0:t0 + m], xh[x][:, 1, i], start=True, stop=False)
                            last = mm(bank(x, i, L, rows=m, a=cc * L), xh[x][:, 1, i, t0:t0 + m], w1row[:], start=False, stop=True)
                    last.then_inc(pair_mm.of(x), 1)
                for x in XS:
                    wait(x, p_ready)
                    for i in range(IMGS):
                        for jc, (j0, mj) in enumerate(LC):
                            for cc, (t0, m) in enumerate(LC):
                                last = nc.tensor.transpose(bank(x, i, m, rows=mj, a=jc * L + t0), aS[x][0:m, i, cc, j0:j0 + mj],
                                                           c("ident", 0, m, rows=m))
                    last.then_inc(pT_mm.of(x), 1)
                for x in XS:
                    wait(x, xT_ready)
                    wait(x, pT_ready)
                    for i in range(IMGS):
                        for jc, (j0, mj) in enumerate(LC):
                            last = mm(bank(x, 2, L, a=i * L), xTS[x][0:mj, i, jc], pTS[x][0:mj, i, jc], start=(jc == 0), stop=(jc == 1))
                    last.then_inc(att_mm.of(x), 1)
                for x in XS:
                    wait(x, att_ready)
                    for b, name in ((0, "ffW"), (1, "frW")):
                        mm(bank(x, b), w(name, 0, D), flat(z[x][:]), start=True, stop=False)
                        last = mm(bank(x, b), w(name, D), att[x], start=False, stop=True)
                    last.then_inc(gate_mm.of(x), 1)

                layernorm(4, lambda x: flat(X[x][:]), H_ready, 2)
                for x in XS:
                    wait(x, z_ready, 4)
                    zf = flat(z[x][:])
                    for k in range(NTK):
                        last = mm(bank(x, 2, E2 + 1, rows=TK, a=(E2 + 1) * k), zf[:, TK * k:TK * k + TK], w("gt"), start=True, stop=True)
                    last.then_inc(gl_mm.of(x), 1)
                    for e in range(E2):
                        if e >= 2:
                            wait(x, h2_ready, e - 2)
                        unit(x, e % 2, w("fc1", D * e, D * e + D), zf, h2_mm)
                for x in XS:
                    wait(x, wv_ready)
                    for k in range(NTK):
                        last = mm(bank(x, 2, TK, rows=E2 * R2, a=TK * k),
                                  wrep[x][:, k].rearrange("p e r -> p (e r)"),
                                  c("ident", 0, TK, rows=TK), start=True, stop=True)
                    last.then_inc(wr_mm.of(x), 1)
                    for e in range(E2):
                        wait(x, h2_ready, e)
                        last = mm(bank(x, 3, rows=E2 * R2), w("lA", 64 * e, 64 * e + 64), hid[x][:, e], start=(e == 0), stop=(e == E2 - 1))
                    last.then_inc(lo_mm.of(x), 1)
                for x in XS:
                    wait(x, low_ready)
                    unit(x, 0, G[:], low[x], ro_mm)


def arrange(inp):
    b = inp["x"].shape[0]
    iters = b // (IMGS * STREAMS)
    pt = np.asarray(inp["x"]).reshape(iters, STREAMS, IMGS, 3, SIDE, PATCH, SIDE, PATCH)
    pt = pt.transpose(0, 1, 3, 5, 7, 2, 4, 6).reshape(iters, STREAMS, KP, P, IMGS * NPATCH)
    pt = np.ascontiguousarray(pt.transpose(0, 1, 3, 2, 4)).reshape(iters, STREAMS, P, KP, IMGS * NPATCH)
    a = {}

    def put(name, m):
        m = np.asarray(m)
        full = np.zeros((P, m.shape[1]), m.dtype)
        full[:m.shape[0]] = m
        a[name] = full

    def col(name, v):
        put(name, np.asarray(v).reshape(-1, 1))

    g = {k: np.asarray(v) for k, v in inp.items()}
    put("conv", g["L0_tok_conv_w"].reshape(D, KP, P).transpose(2, 1, 0).reshape(P, KP * D))
    for l in range(2):
        put(f"qkv{l}", g[f"L0_tok_qkv_{l}"].T)
        wo = np.zeros((2, 4, BLK, D), g[f"L0_tok_wo_{l}"].dtype)
        wo[:, :, 0:DH] = g[f"L0_tok_wo_{l}"].T.reshape(2, 4, DH, D)
        put(f"wo{l}", wo.reshape(2, P, D).transpose(1, 0, 2).reshape(P, 2 * D))
        put(f"gate{l}", g[f"L0_tok_gate_{l}"].T)
        put(f"up{l}", g[f"L0_tok_up_{l}"].T)
        dn = np.zeros((3 * P, D), np.float32)
        dn[0:DFF] = g[f"L0_tok_down_{l}"].T
        put(f"down{l}", dn.reshape(3, P, D).transpose(1, 0, 2).reshape(P, 3 * D))
        col(f"ln1_{l}", g[f"L0_tok_ln1_{l}"])
        col(f"ln2_{l}", g[f"L0_tok_ln2_{l}"])
    for n in ("k_w1", "q_w1", "k_w2", "q_w2", "v_w", "o_w"):
        put(n, g[f"L0_attn_{n}"])
    for n in ("k_b1", "q_b1", "k_b2", "q_b2", "ln_g", "ln_b", "o_b"):
        col(n, g[f"L0_attn_{n}"])
    put("v_b", np.broadcast_to(g["L0_attn_v_b"], (P, D)))
    put("Wr", g["L0_ffn_Wr"])
    put("W1", g["L0_ffn_W1"].transpose(1, 0, 2).reshape(D, NE * HID))
    put("W2", g["L0_ffn_W2"].reshape(NE, NJ, P, D).transpose(2, 0, 1, 3).reshape(P, NE * NJ * D))
    put("br", np.broadcast_to(np.tile(g["L0_ffn_br"], NTK), (P, NTK * NE)))
    put("b1", g["L0_ffn_b1"])
    put("b2", g["L0_ffn_b2"])
    for n in ("tW", "cW"):
        put(n, g[f"L1_attn_{n}"].transpose(1, 0, 2).reshape(D, 2 * D))
    for n in ("frW", "ffW"):
        put(n, g[f"L1_attn_{n}"].reshape(2, D, D).transpose(1, 0, 2).reshape(D, 2 * D))
    put("tb", g["L1_attn_tb"].T)
    put("cb", g["L1_attn_cb"].T)
    put("aw", g["L1_attn_aW"].reshape(3, D).T)
    put("ab", np.broadcast_to(g["L1_attn_ab"], (P, 1)))
    col("frb", g["L1_attn_frb"])
    col("ffb", g["L1_attn_ffb"])
    put("gt", np.concatenate([g["L1_ffn_gate_w"], g["L1_ffn_thr_w"]]).T)
    put("fc1", g["L1_ffn_fc1_w"].transpose(2, 0, 1).reshape(D, E2 * D))
    la = np.zeros((D, E2, E2, R2), np.float32)
    lb = np.zeros((D, E2, E2, R2), np.float32)
    for e in range(E2):
        la[:, e, e] = g["L1_ffn_lora_A"][e]
        lb[:, e, e] = g["L1_ffn_lora_B"][e].T
    put("lA", la.reshape(D, -1))
    put("lB", lb.reshape(D, -1))
    put("fc2", g["L1_ffn_fc2_w"].transpose(2, 0, 1).reshape(D, E2 * D))
    put("pos", g["L0_tok_pos_emb"].reshape(T, D).T)
    col("conv_b", g["L0_tok_conv_b"])
    col("cls_token", g["L0_tok_cls_token"])
    col("cls_tok", g["cls_tok"])
    col("ln_f", g["L0_tok_ln_f"])
    weights = np.concatenate([a[n] for n, _ in WSPEC], axis=1)
    assert weights.shape == (P, WTOT)

    k = {}
    k["ident"] = np.eye(P)
    k["centre"] = np.eye(P) - 1.0 / D
    k["mean"] = np.full((P, D), 1.0 / D)
    k["ones"] = np.ones((P, D))
    k["hmask"] = np.repeat(np.eye(HEADS), DH, axis=0)
    sel = np.zeros((P, P))
    for q in range(4):
        sel[BLK * q + DH, BLK * q:BLK * q + BLK] = 1.0
    k["sel"] = sel
    t = np.arange(L)
    full = (t[:, None] <= t[None, :]) / np.sqrt((t[None, :] + 1.0) * (KD // 2))
    causal = np.zeros((P, L + LC[1][1]))
    causal[:, 0:L] = full[0:P]
    causal[0:LC[1][1], L:] = full[P:L, P:L]
    k["causal"] = causal
    k["iota"] = np.broadcast_to(np.tile(np.arange(NE) - NE, NTK), (P, NTK * NE))
    es = np.zeros((P, NE, P))
    for e in range(NE):
        es[e, e] = 1.0
    k["expsel"] = es.reshape(P, NE * P)
    k["one"] = np.ones((P, L))
    consts = np.concatenate([k[n] for n, _ in CSPEC], axis=1).astype(np.float32)
    return iters, pt, weights, consts


def kernel(**inputs):
    import concourse.bacc as bacc
    from concourse.bass_utils import run_bass_kernel_spmd

    iters, patches, weights, consts = arrange(inputs)
    nc = bacc.Bacc("TRN2", target_bir_lowering=False, num_devices=1)
    arrays = {"patches": patches, "weights": weights, "consts": consts}
    args = [nc.dram_tensor(n, v.shape, mybir.dt.from_np(v.dtype), kind="ExternalInput").ap() for n, v in arrays.items()]
    out = nc.dram_tensor("out", (iters, STREAMS, P, N), mybir.dt.float32, kind="ExternalOutput").ap()
    build(nc, iters, *args, out)
    r = run_bass_kernel_spmd(nc, [arrays], core_ids=[0])
    got = r.results[0]["out"].reshape(iters, STREAMS, P, IMGS, L)
    return np.ascontiguousarray(got.transpose(0, 1, 3, 4, 2).reshape(iters * STREAMS * IMGS, L, D))
```

```python
import concourse.bass as bass
from concourse import mybir
from contextlib import ExitStack
import numpy as np

P = 128
D = 128
HEADS, DH = 8, 16
PATCH, SIDE = 16, 14
NPATCH = SIDE * SIDE
T = NPATCH + 1
L = T + 1
IMGS = 2
STREAMS = 2
KP = 3 * PATCH * PATCH // P
DFF = 344
FCH = [(0, 128), (128, 128), (256, 88)]
NE, HID = 8, 512
NJ = HID // P
E2, R2 = 4, 16
KD = 64
TC = [(0, 128), (128, T - 128)]
LC = [(0, 128), (128, L - 128)]
TK = 99
NTK = IMGS * L // TK
N = IMGS * L
BLK = 32
TINY = 2.0 ** 20
GH = HEADS // 2
HR = GH * DH
SC = 64.0

WSPEC = [("conv", KP * D), ("qkv0", 5 * D), ("qkv1", 5 * D), ("wo0", 2 * D), ("wo1", 2 * D),
         ("gate0", DFF), ("gate1", DFF), ("up0", DFF), ("up1", DFF),
         ("down0", 3 * D), ("down1", 3 * D),
         ("k_w1", D), ("q_w1", D), ("k_w2", KD), ("q_w2", KD), ("v_w", D), ("o_w", D), ("v_b", D),
         ("Wr", NE),
         ("tW", 2 * D), ("cW", 2 * D), ("frW", 2 * D), ("ffW", 2 * D),
         ("gt", E2 + 1), ("fc1", E2 * D), ("lA", E2 * E2 * R2), ("lB", E2 * E2 * R2), ("fc2", E2 * D),
         ("pos", T), ("br", NTK * NE), ("b1", HID), ("b2", D),
         ("conv_b", 1), ("cls_token", 1), ("cls_tok", 1), ("ln_f", 1), ("ln1_0", 1), ("ln1_1", 1),
         ("ln2_0", 1), ("ln2_1", 1), ("k_b1", 1), ("q_b1", 1), ("k_b2", 1), ("q_b2", 1),
         ("ln_g", 1), ("ln_b", 1), ("o_b", 1), ("tb", 2), ("cb", 2), ("aw", 3), ("ab", 1),
         ("frb", 1), ("ffb", 1)]
CSPEC = [("ident", P), ("centre", D), ("mean", D), ("ones", D), ("hmask", 4), ("smask", 4), ("lowrows", 2), ("sel", P),
         ("causal", L + LC[1][1]), ("iota", NTK * NE), ("expsel", NE * P)]


def offsets(spec):
    at, o = {}, 0
    for name, n in spec:
        at[name] = (o, n)
        o += n
    return at, o


WAT, WTOT = offsets(WSPEC)
CAT, CTOT = offsets(CSPEC)
PIECE = 2048
assert NE * HID == 2 * PIECE == NE * NJ * D


def build(nc, iters, patches, weights, experts, consts, out):
    f32, bf16, i32 = mybir.dt.float32, mybir.dt.bfloat16, mybir.dt.int32
    ALU, ACT, AX = mybir.AluOpType, mybir.ActivationFunctionType, mybir.AxisListType
    LNEXP = "natural_log_exp_and_others"
    ctx = ExitStack()
    with ctx:
        def sb(name, shape, dt=f32):
            return ctx.enter_context(nc.sbuf_tensor(name, shape, dt))

        W = sb("W", [P, WTOT])
        C = sb("C", [P, CTOT])

        def w(name, a=0, b=None, rows=P):
            o, n = WAT[name]
            return W[0:rows, o + a:o + (n if b is None else b)]

        def c(name, a=0, b=None, rows=P):
            o, n = CAT[name]
            return C[0:rows, o + a:o + (n if b is None else b)]

        f16 = mybir.dt.float16
        identb = sb("identb", [P, P], f16)
        expselb = sb("expselb", [NE, NE, P], f16)
        W1s = sb("W1s", [P, 2, NE * HID], f16)
        W2s = sb("W2s", [P, 2, NE * NJ * D], f16)
        b1s = sb("b1s", [2 * NE, HID], f16)
        b2s = sb("b2s", [2 * NE, D], f16)
        w1row = sb("w1row", [P, L])
        owg = sb("owg", [P, D])
        obp = sb("obp", [P, 1])
        G = sb("G", [E2 * R2, D])

        def per_stream(name, shape, dt=f32):
            return [sb(f"{name}{x}", shape, dt) for x in range(STREAMS)]

        img = per_stream("img", [P, KP, IMGS * NPATCH])
        X = per_stream("X", [P, IMGS, L])
        sq = per_stream("sq", [P, N])
        lnv = per_stream("lnv", [P, 2, N])
        rs = per_stream("rs", [P, 2, N])
        z = per_stream("z", [P, IMGS, L])
        h = [t[:].rearrange("p i t -> p (i t)")[:, 0:IMGS * T].rearrange("p (i t) -> p i t", i=IMGS) for t in z]
        ql = per_stream("ql", [HR + GH, 2, IMGS, T], f16)
        k1 = per_stream("k1", [P, 2, IMGS, T], f16)
        k2 = per_stream("k2", [HR + GH, 2, IMGS, T], f16)
        regA = per_stream("regA", [P, NE * N])
        regB = per_stream("regB", [P, NE * N])
        regC = per_stream("regC", [P, NJ * N])

        def view(reg, at, pattern, half=False, **dims):
            n = int(np.prod(list(dims.values())))
            if half:
                reg, at = [r[:, :].bitcast(f16) for r in reg], 2 * at
            if "one" in dims:
                return [r[:, at:at + n] for r in reg]
            return [r[:, at:at + n].rearrange(f"p ({pattern}) -> p {pattern}", **dims) for r in reg]

        IT = IMGS * T
        qmh = view(regA, 0, "h i t", half=True, h=HEADS, i=IMGS, t=T)
        qml = view(regA, HEADS * IT // 2, "h i t", half=True, h=HEADS, i=IMGS, t=T)
        xe = view(regA, 0, "e s n", half=True, e=NE, s=2, n=N)
        sil = view(regB, 0, "j n", j=3, n=IT)
        ff = view(regB, 3 * IT, "j n", j=3, n=IT)
        on = view(regB, 6 * IT, "g n", g=2, n=IT)
        mk = view(regB, 0, "e n", half=True, e=NE, n=N)
        zs = view(regB, NE * N // 2, "s n", half=True, s=2, n=N)
        pt = list(zip(view(regC, 0, "c a t", c=2, a=GH, t=T), view(regB, 2 * IT, "c a t", c=2, a=GH, t=T)))
        qh = view(regC, 2 * IT, "g i t", half=True, g=2, i=IMGS, t=T)
        kt = view(regC, 3 * IT, "g i t", half=True, g=2, i=IMGS, t=T)
        oS = view(regB, 0, "g n", g=2, n=IT)
        hid = view(regC, 0, "j n", j=NJ, n=N)
        hs = view(regC, 0, "j s n", half=True, j=NJ, s=2, n=N)
        ysel = view(regA, 0, "e n", e=NE, n=N)
        gel = view(regA, 0, "s n", s=2, n=N)
        kq = [v[0:KD] for v in view(regA, 2 * N, "s i t", s=2, i=IMGS, t=L)]
        kqs = [v[0:KD] for v in view(regA, 4 * N, "s n", s=2, n=N)]
        zn = view(regA, 6 * N, "one n", one=1, n=N)
        rS = view(regA, 7 * N, "one n", one=1, n=N)
        vS = view(regB, 0, "i c d", i=IMGS, c=2, d=D)
        As = view(regB, 4 * D, "i n", i=IMGS, n=L + LC[1][1])
        xh = view(regA, 0, "k i t", k=2, i=IMGS, t=L)
        xw = view(regA, 2 * N, "i t", i=IMGS, t=L)
        aS = view(regA, 3 * N, "i c t", i=IMGS, c=2, t=L)
        pTS = view(regA, 5 * N, "i c t", i=IMGS, c=2, t=L)
        att = view(regA, 7 * N, "one n", one=1, n=N)
        tS = view(regB, 0, "one n", one=1, n=N)
        cS = view(regB, N, "one n", one=1, n=N)
        dS = view(regB, 2 * N, "one n", one=1, n=N)
        xTS = view(regB, 3 * N, "i c d", i=IMGS, c=2, d=D)
        wr = [v[0:E2 * R2] for v in view(regB, 5 * N, "one n", one=1, n=N)]
        outS = view(regB, 7 * N, "one n", one=1, n=N)
        low = [v[0:E2 * R2] for v in view(regB, 6 * N, "one n", one=1, n=N)]
        va = per_stream("va", [P, IMGS, 2, HEADS, BLK])
        nm = per_stream("nm", [P, IMGS, 2, HEADS], f16)
        lg = per_stream("lg", [TK, 4, NTK, NE])
        oh = per_stream("oh", [TK, NTK, 2, NE], f16)
        lgs = per_stream("lgs", [TK, 2, NTK])
        ohT = per_stream("ohT", [2 * NE, N], f16)
        ohTs = per_stream("ohTs", [2 * NE, N], f16)
        am = per_stream("am", [P, 3, IMGS, 2])
        gl = per_stream("gl", [TK, 4, NTK, E2 + 1])
        wrep = per_stream("wrep", [TK, NTK, E2, R2])
        gs = per_stream("gs", [TK, 8, NTK])

        ps = [[ctx.enter_context(nc.psum_tensor(f"ps{x}", [P, 4, 512], f32))] for x in range(STREAMS)]

        def bank(x, b, n=N, rows=P, a=0, row0=0):
            return ps[x][0][row0:row0 + rows, b, a:a + n]

        def banks(x, b, n, rows=P, a=0):
            return ps[x][0][0:rows, b:b + 2, a:a + n]

        class Signal:

            def __init__(self, name, times=1, by=1, blocks=False, split=False):
                self.sems = [ctx.enter_context(nc.semaphore(f"{name}{x if split else ''}"))
                             for x in range(STREAMS if split else 1)]
                self.times, self.by, self.blocks = times, by, blocks

            def of(self, x):
                return self.sems[x % len(self.sems)]

            def done(self, it, x, k=0):
                if len(self.sems) > 1:
                    return it * (self.times * self.by) + (k + 1) * self.by
                at = x * self.times + k if self.blocks else k * STREAMS + x
                return it * (self.times * STREAMS * self.by) + (at + 1) * self.by

        loaded = ctx.enter_context(nc.semaphore("weights_loaded"))
        setup_d = ctx.enter_context(nc.semaphore("setup_vector"))
        setup_p = ctx.enter_context(nc.semaphore("setup_tensor"))
        stored = ctx.enter_context(nc.semaphore("stored"))
        img_loaded = Signal("img_loaded", 1, 16, split=True)
        img_used = Signal("img_used")
        STEPS = [(i, 2 * g + a) for g in range(2) for i in range(IMGS) for a in range(2)]
        GS = len(STEPS) // 2
        NMAX = GS + 2 * GS
        x_ready = Signal("x_ready", 1 + 4 + 1)
        sq_ready = Signal("sq_ready", 5)
        ms_mm = Signal("ms_mm", 5)
        ln_done = Signal("ln_done", 5 + 2 + 5 + 1)
        rs_ready = Signal("rs_ready", 5 + 2 + 5 + 1)
        h_ready = Signal("h_ready", 4)
        qk_mm = Signal("qk_mm", 2 * 4)
        v_mm = Signal("v_mm", 2)
        qk_ready = Signal("qk_ready", 2 * 4)
        k1_ready = Signal("k1_ready", 2)
        k2_ready = Signal("k2_ready", 2)
        nmT_mm = Signal("nmT_mm", 2 * 2)
        nmT_ready = Signal("nmT_ready", 2 * 2)
        qml_ready = Signal("qml_ready", 2 * 2)
        stage_loaded = ctx.enter_context(nc.semaphore("experts_loaded"))
        zh_ready = Signal("zh_ready")
        hh_ready = Signal("hh_ready", NJ, blocks=True)
        v_ready = Signal("v_ready", 2)
        qm_ready = Signal("qm_ready", 2)
        qm1_ready = Signal("qm1_ready", 2)
        max_mm = Signal("max_mm", 2 * NMAX)
        max_ready = Signal("max_ready", 2 * NMAX)
        score_mm = Signal("score_mm", 2 * 8)
        exp_ready = Signal("exp_ready", 2 * 8)
        pv_mm = Signal("pv_mm", 2)
        o_ready = Signal("o_ready", 2)
        sum_mm = Signal("sum_mm", 2)
        on_ready = Signal("on_ready", 2)
        wo_mm = Signal("wo_mm", 2)
        gu_mm = Signal("gu_mm", 2 * 3)
        sil_ready = Signal("sil_ready", 2 * 3)
        ff_ready = Signal("ff_ready", 2 * 3)
        down_mm = Signal("down_mm", 2)
        cen_mm = Signal("cen_mm", 5)
        csq_ready = Signal("csq_ready", 5)
        var_mm = Signal("var_mm", 5)
        z_ready = Signal("z_ready", 5)
        H_ready = Signal("H_ready", 3)
        Hy_ready = Signal("Hy_ready", NE, blocks=True)
        Hz_ready = Signal("Hz_ready")
        kq1_mm = Signal("kq1_mm")
        v0_mm = Signal("v0_mm")
        gel_ready = Signal("gel_ready")
        v0_ready = Signal("v0_ready")
        kq2_mm = Signal("kq2_mm")
        kq_ready = Signal("kq_ready")
        kqs_ready = Signal("kqs_ready")
        nn_mm = Signal("nn_mm")
        nmax_ready = Signal("nmax_ready")
        kqn_ready = Signal("kqn_ready")
        sc_mm = Signal("sc_mm")
        As_ready = Signal("As_ready")
        r_mm = Signal("r_mm")
        r_ready = Signal("r_ready")
        ao_mm = Signal("ao_mm")
        rt_mm = Signal("rt_mm")
        oh_ready = Signal("oh_ready")
        ohT_mm = Signal("ohT_mm")
        ohT_ready = Signal("ohT_ready")
        mk_mm = Signal("mk_mm", NE)
        mk_ready = Signal("mk_ready", NE)
        xe_ready = Signal("xe_ready", NE)
        hid_mm = Signal("hid_mm", NJ, blocks=True)
        hid_ready = Signal("hid_ready", NJ, blocks=True)
        y_mm = Signal("y_mm", NE + 1, blocks=True)
        ysel_ready = Signal("ysel_ready", NE, blocks=True)
        tc_mm = Signal("tc_mm", 2)
        tc_ready = Signal("tc_ready", 2)
        xh_ready = Signal("xh_ready", 2)
        xw_ready = Signal("xw_ready")
        xT_mm = Signal("xT_mm")
        xT_ready = Signal("xT_ready")
        pair_mm = Signal("pair_mm")
        am_ready = Signal("am_ready")
        ex_ready = Signal("ex_ready")
        p_ready = Signal("p_ready")
        pT_mm = Signal("pT_mm")
        pT_ready = Signal("pT_ready")
        att_mm = Signal("att_mm")
        att_ready = Signal("att_ready")
        gate_mm = Signal("gate_mm")
        gate_ready = Signal("gate_ready")
        gl_mm = Signal("gl_mm")
        gd_ready = Signal("gd_ready")
        ge_ready = Signal("ge_ready")
        wv_ready = Signal("wv_ready")
        h2_mm = Signal("h2_mm", E2, blocks=True)
        h2_ready = Signal("h2_ready", E2, blocks=True)
        wr_mm = Signal("wr_mm")
        wr_ready = Signal("wr_ready")
        lo_mm = Signal("lo_mm")
        low_ready = Signal("low_ready")
        ro_mm = Signal("ro_mm")
        out_ready = Signal("out_ready")
        CHAIN = 23
        own = Signal("vector_own", CHAIN, split=True)

        LOADS = 16 * (-(-WTOT // PIECE) - (-CTOT // PIECE))

        XS = range(STREAMS)
        STAGES = [regA[0], regB[0], regA[1], regB[1]]
        EXPERT_PIECES = [(STAGES[k], experts[k // 2, :, (k % 2) * PIECE:(k % 2 + 1) * PIECE]) for k in range(4)]
        block = ctx.enter_context(nc.Block())

        @block.sync
        def _(sp):
            for dst, src, n in ((W, weights, WTOT), (C, consts, CTOT)):
                for a in range(0, n, PIECE):
                    sp.dma_start(dst[:, a:min(a + PIECE, n)], src[:, a:min(a + PIECE, n)]).then_inc(loaded, 16)

            for k, (reg, src) in enumerate(EXPERT_PIECES):
                sp.dma_start(reg[:, 0:PIECE], src).then_inc(stage_loaded, 16)

            def load(it, x):
                sp.dma_start(img[x][:, :, :], patches[it, x]).then_inc(img_loaded.of(x), 16)

            def store(it, x):
                sp.wait_ge(out_ready.of(x), out_ready.done(it, x))
                sp.dma_start(out[it, x], outS[x]).then_inc(stored, 16)

            for x in XS:
                load(0, x)
            with sp.Fori(0, iters - 1) as it:
                for x in XS:
                    sp.wait_ge(img_used.of(x), img_used.done(it, x))
                    load(it + 1, x)
                for x in XS:
                    store(it, x)
            for x in XS:
                store(iters - 1, x)
            sp.wait_ge(stored, 16 * STREAMS * iters)

        @block.gpsimd
        def _(pool):
            with pool.Fori(0, iters) as it:
                for l in range(2):
                    for x in XS:
                        pool.wait_ge(qk_ready.of(x), qk_ready.done(it, x, 4 * l + 3))
                        k2f, ktf = (t[x][0:HR].rearrange("p g i t -> p (g i t)") for t in (k2, kt))
                        nc.gpsimd.tensor_tensor(k2f, ktf, c("ones", 0, 1, rows=HR).broadcast_to([HR, 2 * IT]),
                                                ALU.mult).then_inc(k2_ready.of(x), 1)
                for x in XS:
                    pool.wait_ge(z_ready.of(x), z_ready.done(it, x, 0))
                    nc.gpsimd.tensor_tensor(X[x][:], X[x][:], z[x][:], ALU.add).then_inc(Hz_ready.of(x), 1)
                for x in XS:
                    Xf = X[x][:].rearrange("p i t -> p (i t)")
                    for e in range(NE):
                        pool.wait_ge(ysel_ready.of(x), ysel_ready.done(it, x, e))
                        if e:
                            pool.wait_ge(Hy_ready.of(x), Hy_ready.done(it, x, e - 1))
                        nc.gpsimd.tensor_tensor(Xf, Xf, ysel[x][:, e], ALU.add).then_inc(Hy_ready.of(x), 1)

        @block.scalar
        def _(act):
            nc.scalar.preload_act_table_set(LNEXP)
            act.wait_ge(setup_d, 1)

            def rsqrt_of(it, x, k, src, eps, dims=(P, 1)):
                rows = dims[0]
                nc.scalar.activation(lnv[x][0:rows, 0, 0:src.shape[-1]], src, ACT.Ln, bias=eps).then_inc(ln_done.of(x), 1)
                act.wait_ge(ln_done.of(x), ln_done.done(it, x, k))
                nc.scalar.activation(rs[x][0:rows, 0, 0:src.shape[-1]], lnv[x][0:rows, 0, 0:src.shape[-1]],
                                     ACT.Exp, scale=-0.5).then_inc(rs_ready.of(x), 1)

            def rms(it, o, k):
                for x in XS:
                    act.wait_ge(x_ready.of(x), x_ready.done(it, x, o))
                    nc.scalar.activation(sq[x][:, 0:IMGS * T].rearrange("p (i t) -> p i t", i=IMGS),
                                         X[x][:, :, 1:L], ACT.Square).then_inc(sq_ready.of(x), 1)
                for x in XS:
                    act.wait_ge(ms_mm.of(x), ms_mm.done(it, x, o))
                    rsqrt_of(it, x, k, bank(x, 0, IMGS * T), 1e-6)

            def layernorm(it, o, k):
                for x in XS:
                    act.wait_ge(cen_mm.of(x), cen_mm.done(it, x, o))
                    nc.scalar.activation(sq[x][:, :], bank(x, 0), ACT.Square).then_inc(csq_ready.of(x), 1)
                for x in XS:
                    act.wait_ge(var_mm.of(x), var_mm.done(it, x, o))
                    rsqrt_of(it, x, k, bank(x, 1), 1e-5)

            with act.Fori(0, iters) as it:
                nc.scalar.preload_act_table_set(LNEXP)
                for l in range(2):
                    rms(it, 2 * l, 3 * l)
                    for k, (dst, g, b) in enumerate(((qh, 0, 1), (qh, 1, 2), (kt, 0, 3), (kt, 1, 0))):
                        for x in XS:
                            act.wait_ge(qk_mm.of(x), qk_mm.done(it, x, 4 * l + k))
                            nc.scalar.copy(dst[x][:, g].rearrange("p i t -> p (i t)"), bank(x, b, IT)).then_inc(qk_ready.of(x), 1)
                    for x in XS:
                        act.wait_ge(qk_ready.of(x), qk_ready.done(it, x, 4 * l + 3))
                        for a in range(GH):
                            last = nc.scalar.activation(qmh[x][:, GH + a], qh[x][:, 1], ACT.Copy, scale=c("hmask", a, a + 1))
                        last.then_inc(qm1_ready.of(x), 1)
                    for g in range(2):
                        for x in XS:
                            act.wait_ge(nmT_mm.of(x), nmT_mm.done(it, x, 2 * l + g))
                            nc.scalar.copy(ql[x][HR:HR + GH, g].rearrange("p i t -> p (i t)"),
                                           bank(x, 3 * g, IT, rows=GH, row0=HR)).then_inc(nmT_ready.of(x), 1)
                        for s in range(GS * g, GS * g + GS):
                            for x in XS:
                                act.wait_ge(score_mm.of(x), score_mm.done(it, x, 8 * l + s))
                                for cc, (_, m) in enumerate(TC):
                                    last = nc.scalar.activation(pt[x][s // 2 % 2][0:m, cc, 2 * (s % 2):2 * (s % 2) + 2].rearrange("p a t -> p (a t)"),
                                                                bank(x, cc, 2 * T, rows=m), ACT.Exp)
                                last.then_inc(exp_ready.of(x), 1)
                    for x in XS:
                        act.wait_ge(pv_mm.of(x), pv_mm.done(it, x, l))
                        nc.scalar.copy(oS[x], banks(x, 2, IMGS * T)).then_inc(o_ready.of(x), 1)
                    for x in XS:
                        act.wait_ge(sum_mm.of(x), sum_mm.done(it, x, l))
                        nc.scalar.activation(lnv[x][:, :, 0:IMGS * T], banks(x, 0, IMGS * T), ACT.Ln).then_inc(ln_done.of(x), 1)
                        act.wait_ge(ln_done.of(x), ln_done.done(it, x, 3 * l + 1))
                        nc.scalar.activation(rs[x][:, :, 0:IMGS * T], lnv[x][:, :, 0:IMGS * T], ACT.Exp,
                                             scale=-1.0).then_inc(rs_ready.of(x), 1)
                    rms(it, 2 * l + 1, 3 * l + 2)
                    for j, (_, m) in enumerate(FCH):
                        for x in XS:
                            act.wait_ge(gu_mm.of(x), gu_mm.done(it, x, 3 * l + j))
                            nc.scalar.activation(sil[x][0:m, j], bank(x, (2 * j) % 4, IMGS * T, rows=m),
                                                 ACT.Silu).then_inc(sil_ready.of(x), 1)
                    nc.scalar.preload_act_table_set(LNEXP)
                rms(it, 4, 6)
                layernorm(it, 0, 7)
                for x in XS:
                    act.wait_ge(kq1_mm.of(x), kq1_mm.done(it, x))
                    nc.scalar.activation(gel[x][:, 0], bank(x, 2), ACT.Gelu, bias=w("k_b1"))
                    nc.scalar.activation(gel[x][:, 1], bank(x, 3), ACT.Gelu, bias=w("q_b1")).then_inc(gel_ready.of(x), 1)
                nc.scalar.preload_act_table_set(LNEXP)
                for x in XS:
                    act.wait_ge(kq2_mm.of(x), kq2_mm.done(it, x))
                    for s, b in enumerate(("k_b2", "q_b2")):
                        last = nc.scalar.activation(kq[x][:, s].rearrange("p i t -> p (i t)"), bank(x, 2 + s, rows=KD),
                                                    ACT.Identity, bias=w(b, rows=KD))
                    last.then_inc(kq_ready.of(x), 1)
                for x in XS:
                    act.wait_ge(nmax_ready.of(x), nmax_ready.done(it, x))
                    nc.scalar.activation(lnv[x][0:KD], kqs[x], ACT.Ln, scale=TINY).then_inc(ln_done.of(x), 1)
                    act.wait_ge(ln_done.of(x), ln_done.done(it, x, 8))
                    nc.scalar.activation(rs[x][0:KD], lnv[x][0:KD], ACT.Exp, scale=-0.5).then_inc(rs_ready.of(x), 1)
                for x in XS:
                    act.wait_ge(r_mm.of(x), r_mm.done(it, x))
                    nc.scalar.copy(rS[x], bank(x, 0)).then_inc(r_ready.of(x), 1)
                layernorm(it, 1, 9)
                layernorm(it, 2, 10)
                for x in XS:
                    act.wait_ge(z_ready.of(x), z_ready.done(it, x, 2))
                    nc.scalar.copy(zs[x][:, 0], z[x][:].rearrange("p i t -> p (i t)")).then_inc(zh_ready.of(x), 1)
                for x in XS:
                    act.wait_ge(ohT_mm.of(x), ohT_mm.done(it, x))
                    nc.scalar.copy(ohT[x][:], bank(x, 3, rows=2 * NE))
                    nc.scalar.mul(ohTs[x][:], bank(x, 3, rows=2 * NE), SC).then_inc(ohT_ready.of(x), 1)
                for e in range(NE):
                    for x in XS:
                        act.wait_ge(mk_mm.of(x), mk_mm.done(it, x, e))
                        nc.scalar.copy(mk[x][:, e], bank(x, 2 + e % 2)).then_inc(mk_ready.of(x), 1)
                for x in XS:
                    for j in range(NJ):
                        act.wait_ge(hid_mm.of(x), hid_mm.done(it, x, j))
                        nc.scalar.activation(hs[x][:, j, 0], bank(x, j), ACT.Relu).then_inc(hh_ready.of(x), 1)
                layernorm(it, 3, 11)
                for i in range(2):
                    for x in XS:
                        act.wait_ge(tc_mm.of(x), tc_mm.done(it, x, i))
                        if i:
                            act.wait_ge(xh_ready.of(x), xh_ready.done(it, x, 0))
                        nc.scalar.activation(tS[x], bank(x, 2 - 2 * i), ACT.Relu, bias=w("tb", i, i + 1))
                        nc.scalar.activation(cS[x], bank(x, 3 - 2 * i), ACT.Sigmoid, bias=w("cb", i, i + 1)).then_inc(tc_ready.of(x), 1)
                nc.scalar.preload_act_table_set(LNEXP)
                for x in XS:
                    act.wait_ge(xT_mm.of(x), xT_mm.done(it, x))
                    for cc, (_, m) in enumerate(LC):
                        last = nc.scalar.copy(xTS[x][0:m, :, cc],
                                              bank(x, 2, 512, rows=m).rearrange("p (i c d) -> p i c d", i=IMGS, c=2)[:, :, cc])
                    last.then_inc(xT_ready.of(x), 1)
                for x in XS:
                    act.wait_ge(am_ready.of(x), am_ready.done(it, x))
                    for i in range(IMGS):
                        for cc, (_, m) in enumerate(LC):
                            last = nc.scalar.activation(aS[x][0:m, i, cc], aS[x][0:m, i, cc], ACT.Exp,
                                                        bias=am[x][0:m, 0, i, cc:cc + 1],
                                                        accum_out=am[x][0:m, 1, i, cc:cc + 1])
                    last.then_inc(ex_ready.of(x), 1)
                for x in XS:
                    act.wait_ge(pT_mm.of(x), pT_mm.done(it, x))
                    for cc, (_, m) in enumerate(LC):
                        last = nc.scalar.copy(pTS[x][0:m, :, cc], banks(x, 0, L, rows=m, a=cc * L))
                    last.then_inc(pT_ready.of(x), 1)
                for x in XS:
                    act.wait_ge(att_mm.of(x), att_mm.done(it, x))
                    nc.scalar.copy(att[x], bank(x, 2)).then_inc(att_ready.of(x), 1)
                for x in XS:
                    act.wait_ge(gate_mm.of(x), gate_mm.done(it, x))
                    nc.scalar.activation(tS[x], bank(x, 0), ACT.Sigmoid, bias=w("ffb"))
                    nc.scalar.activation(cS[x], bank(x, 1), ACT.Sigmoid, bias=w("frb")).then_inc(gate_ready.of(x), 1)
                nc.scalar.preload_act_table_set(LNEXP)
                layernorm(it, 4, 12)
                for x in XS:
                    act.wait_ge(gd_ready.of(x), gd_ready.done(it, x))
                    nc.scalar.activation(gl[x][:, 1], gl[x][:, 0], ACT.Exp).then_inc(ge_ready.of(x), 1)
                    for e in range(E2):
                        act.wait_ge(h2_mm.of(x), h2_mm.done(it, x, e))
                        nc.scalar.activation(hid[x][:, e], bank(x, e % 2), ACT.Relu).then_inc(h2_ready.of(x), 1)
                for x in XS:
                    act.wait_ge(wr_mm.of(x), wr_mm.done(it, x))
                    nc.scalar.copy(wr[x], bank(x, 2, rows=E2 * R2)).then_inc(wr_ready.of(x), 1)

        @block.vector
        def _(dve):
            dve.wait_ge(loaded, LOADS)
            V = nc.vector
            V.tensor_copy(identb[:], c("ident"))
            V.tensor_copy(expselb[:].rearrange("p e n -> p (e n)"), c("expsel", rows=NE))
            for x in XS:
                V.memset(va[x][:], 1.0)
                V.memset(k2[x][HR:], 1.0)
            V.tensor_scalar(w1row[:], c("ones", 0, 1).broadcast_to([P, L]), w("aw", 0, 1), None, ALU.mult)
            V.tensor_scalar(owg[:], w("o_w"), w("ln_g"), None, ALU.mult)
            for l in range(2):
                V.tensor_scalar(w(f"qkv{l}", 0, 2 * D), w(f"qkv{l}", 0, 2 * D), w(f"ln1_{l}"), DH ** -0.5, ALU.mult, ALU.mult)
                V.tensor_scalar(w(f"qkv{l}", 2 * D), w(f"qkv{l}", 2 * D), w(f"ln1_{l}"), None, ALU.mult)
                V.tensor_scalar(w(f"gate{l}"), w(f"gate{l}"), w(f"ln2_{l}"), None, ALU.mult)
                V.tensor_scalar(w(f"up{l}"), w(f"up{l}"), w(f"ln2_{l}"), None, ALU.mult)
            V.tensor_scalar(w("pos", 1), w("pos", 1), w("conv_b"), None, ALU.add)
            V.tensor_scalar(w("pos", 0, 1), w("pos", 0, 1), w("cls_token"), None, ALU.add)
            for k, (reg, _) in enumerate(EXPERT_PIECES):
                dst, a = (W1s, W2s)[k // 2], (k % 2) * PIECE
                dve.wait_ge(stage_loaded, 16 * len(EXPERT_PIECES))
                V.tensor_scalar(dst[:, 0, a:a + PIECE], reg[:, 0:PIECE], SC, None, ALU.mult)
            V.tensor_scalar(b1s[:], w("b1", rows=2 * NE), SC, None, ALU.mult)
            V.tensor_scalar(b2s[:], w("b2", rows=2 * NE), SC, None, ALU.mult)
            for name in ("b1", "b2"):
                last = V.tensor_scalar(w(name, rows=2 * NE), w(name, rows=2 * NE), SC, None, ALU.mult)
            last.then_inc(setup_d, 1)
            dve.wait_ge(setup_d, 1)
            for k, (reg, _) in enumerate(EXPERT_PIECES):
                dst, a = (W1s, W2s)[k // 2], (k % 2) * PIECE
                V.scalar_tensor_tensor(dst[:, 1, a:a + PIECE], reg[:, 0:PIECE], SC, dst[:, 0, a:a + PIECE],
                                       ALU.mult, ALU.subtract)
            V.scalar_tensor_tensor(b1s[:], b1s[:], c("lowrows", 1, 2, rows=2 * NE), w("b1", rows=2 * NE), ALU.mult, ALU.add)
            V.scalar_tensor_tensor(b2s[:], b2s[:], c("lowrows", 1, 2, rows=2 * NE), w("b2", rows=2 * NE), ALU.mult, ALU.add)
            dve.wait_ge(setup_p, 1)
            V.tensor_scalar(obp[:], bank(0, 0, 1), w("o_b"), None, ALU.add)
            V.tensor_copy(G[:], bank(0, 1, D, rows=E2 * R2)).then_inc(setup_d, 1)

            with dve.Fori(0, iters) as it:
                seen = [0] * STREAMS

                def then(x, ins):
                    ins.then_inc(own.of(x), 1)
                    dve.wait_ge(own.of(x), own.done(it, x, seen[x]))
                    seen[x] += 1

                def scale_h(o, k):
                    for x in XS:
                        dve.wait_ge(rs_ready.of(x), rs_ready.done(it, x, k))
                        V.tensor_tensor(h[x], X[x][:, :, 1:L],
                                        rs[x][:, 0, 0:IMGS * T].rearrange("p (i t) -> p i t", i=IMGS),
                                        ALU.mult).then_inc(h_ready.of(x), 1)

                def add_x(x, b, sig, k, r, at=1):
                    dve.wait_ge(sig.of(x), sig.done(it, x, k))
                    V.tensor_tensor(X[x][:, :, at:L], X[x][:, :, at:L],
                                    bank(x, b, IMGS * (L - at)).rearrange("p (i t) -> p i t", i=IMGS),
                                    ALU.add).then_inc(r[0].of(x), 1)

                def scale_z(o, k, dst):
                    for x in XS:
                        dve.wait_ge(rs_ready.of(x), rs_ready.done(it, x, k))
                        V.tensor_tensor(dst[x][:].rearrange("p i t -> p (i t)") if dst is z else dst[x][:],
                                        bank(x, 0), rs[x][:, 0], ALU.mult).then_inc(z_ready.of(x), 1)

                for x in XS:
                    dve.wait_ge(img_used.of(x), img_used.done(it, x))
                    V.tensor_tensor(X[x][:, :, 2:L], bank(x, 1, IMGS * NPATCH).rearrange("p (i t) -> p i t", i=IMGS),
                                    w("pos", 1).unsqueeze(1).broadcast_to([P, IMGS, NPATCH]), ALU.add)
                    V.tensor_copy(X[x][:, :, 1:2], w("pos", 0, 1).unsqueeze(1).broadcast_to([P, IMGS, 1])).then_inc(x_ready.of(x), 1)
                for l in range(2):
                    scale_h(2 * l, 3 * l)
                    for x in XS:
                        dve.wait_ge(v_mm.of(x), v_mm.done(it, x, l))
                        for cc, (_, m) in enumerate(TC):
                            src = bank(x, 0, 512, rows=m).rearrange("p (i c h d) -> p i c h d", i=IMGS, c=2, h=HEADS)
                            for i in range(IMGS):
                                last = V.tensor_copy(va[x][0:m, i, cc, :, 0:DH], src[:, i, cc])
                        last.then_inc(v_ready.of(x), 1)
                    for g in range(2):
                        for x in XS:
                            dve.wait_ge(qk_ready.of(x), qk_ready.done(it, x, 4 * l + g))
                            qlg, qhg = (t[x][0:HR, g].rearrange("p i t -> p (i t)") for t in (ql, qh))
                            V.tensor_tensor(qlg, bank(x, 1 + g, IT, rows=HR), qhg, ALU.subtract)
                            if g == 0:
                                for a in range(GH):
                                    last = V.tensor_scalar(qmh[x][:, a], qh[x][:, 0], c("hmask", a, a + 1), None, ALU.mult)
                                last.then_inc(qm_ready.of(x), 1)
                    for g in range(2):
                        for x in XS:
                            dve.wait_ge(qk_ready.of(x), qk_ready.done(it, x, 4 * l + 2 + g))
                            k1g, ktg = (t[x][:, g].rearrange("p i t -> p (i t)") for t in (k1, kt))
                            last = V.scalar_tensor_tensor(k1g, ktg, c("lowrows", 0, 1), bank(x, 3 - 3 * g, IT), ALU.mult, ALU.add)
                            if g:
                                last.then_inc(k1_ready.of(x), 1)

                    def maxima(x, s, b, cc):
                        (i, hp), m = STEPS[s], TC[cc][1]
                        return V.tensor_reduce(nm[x][0:m, i, cc, 2 * hp:2 * hp + 2],
                                               bank(x, b, 2 * T, rows=m).rearrange("p (a t) -> p a t", a=2),
                                               AX.X, ALU.max, negate=True)

                    def masked_low(x, g):
                        dve.wait_ge(nmT_ready.of(x), nmT_ready.done(it, x, 2 * l + g))
                        for a in range(GH):
                            last = V.tensor_scalar(qml[x][0:HR + GH, GH * g + a], ql[x][:, g],
                                                   c("smask", a, a + 1, rows=HR + GH), None, ALU.mult)
                        last.then_inc(qml_ready.of(x), 1)

                    for s in range(GS):
                        for x in XS:
                            dve.wait_ge(max_mm.of(x), max_mm.done(it, x, NMAX * l + s))
                            for cc in range(2):
                                last = maxima(x, s, 2 * (s % 2) + cc, cc)
                            last.then_inc(max_ready.of(x), 1)
                    for x in XS:
                        masked_low(x, 0)
                    for s in range(GS):
                        for cc in range(2):
                            k = NMAX * l + GS + 2 * s + cc
                            for x in XS:
                                dve.wait_ge(max_mm.of(x), max_mm.done(it, x, k))
                                maxima(x, GS + s, 3, cc).then_inc(max_ready.of(x), 1)
                    for x in XS:
                        masked_low(x, 1)
                    for x in XS:
                        dve.wait_ge(rs_ready.of(x), rs_ready.done(it, x, 3 * l + 1))
                        V.tensor_tensor(on[x], oS[x], rs[x][:, :, 0:IMGS * T], ALU.mult).then_inc(on_ready.of(x), 1)
                    for x in XS:
                        add_x(x, 2, wo_mm, l, (x_ready,))
                    scale_h(2 * l + 1, 3 * l + 2)
                    for j, (_, m) in enumerate(FCH):
                        for x in XS:
                            dve.wait_ge(sil_ready.of(x), sil_ready.done(it, x, 3 * l + j))
                            V.tensor_tensor(ff[x][0:m, j], sil[x][0:m, j], bank(x, (2 * j + 1) % 4, IMGS * T, rows=m),
                                            ALU.mult).then_inc(ff_ready.of(x), 1)
                    for x in XS:
                        add_x(x, 2, down_mm, l, (x_ready,))
                for x in XS:
                    dve.wait_ge(rs_ready.of(x), rs_ready.done(it, x, 6))
                    V.scalar_tensor_tensor(X[x][:, :, 1:L], X[x][:, :, 1:L], w("ln_f"),
                                           rs[x][:, 0, 0:IMGS * T].rearrange("p (i t) -> p i t", i=IMGS),
                                           ALU.mult, ALU.mult)
                    V.tensor_copy(X[x][:, :, 0:1], w("cls_tok").unsqueeze(1).broadcast_to([P, IMGS, 1])).then_inc(x_ready.of(x), 1)
                scale_z(0, 7, z)
                for x in XS:
                    dve.wait_ge(v0_mm.of(x), v0_mm.done(it, x))
                    for cc, (_, m) in enumerate(LC):
                        src = bank(x, 0, 512, rows=m).rearrange("p (i c d) -> p i c d", i=IMGS, c=2)
                        last = V.tensor_tensor(vS[x][0:m, :, cc], src[:, :, cc],
                                               w("v_b", rows=m).unsqueeze(1).broadcast_to([m, IMGS, D]), ALU.add)
                    last.then_inc(v0_ready.of(x), 1)
                for x in XS:
                    dve.wait_ge(kq_ready.of(x), kq_ready.done(it, x))
                    kqf = kq[x].rearrange("p s i t -> p s (i t)")
                    V.tensor_tensor(kqs[x], kqf, kqf, ALU.mult).then_inc(kqs_ready.of(x), 1)
                for x in XS:
                    dve.wait_ge(nn_mm.of(x), nn_mm.done(it, x))
                    V.tensor_scalar(kqs[x], banks(x, 0, N, rows=KD), 1e-24, None, ALU.max).then_inc(nmax_ready.of(x), 1)
                for x in XS:
                    dve.wait_ge(rs_ready.of(x), rs_ready.done(it, x, 8))
                    kqf = kq[x].rearrange("p s i t -> p s (i t)")
                    V.scalar_tensor_tensor(kqf, kqf, TINY ** 0.5, rs[x][0:KD], ALU.mult, ALU.mult).then_inc(kqn_ready.of(x), 1)
                for x in XS:
                    dve.wait_ge(sc_mm.of(x), sc_mm.done(it, x))
                    for a, n, m in ((0, L, P), (L, LC[1][1], LC[1][1])):
                        last = V.tensor_tensor(As[x][0:m, :, a:a + n], banks(x, 2, n, rows=m, a=a),
                                               c("causal", a, a + n, rows=m).unsqueeze(1).broadcast_to([m, IMGS, n]), ALU.mult)
                    last.then_inc(As_ready.of(x), 1)
                scale_z(1, 9, zn)
                for x in XS:
                    dve.wait_ge(ao_mm.of(x), ao_mm.done(it, x))
                    dve.wait_ge(Hz_ready.of(x), Hz_ready.done(it, x))
                    Xf = X[x][:].rearrange("p i t -> p (i t)")
                    V.scalar_tensor_tensor(Xf, bank(x, 2), obp[:], Xf, ALU.add, ALU.add).then_inc(H_ready.of(x), 1)
                scale_z(2, 10, z)
                for x in XS:
                    dve.wait_ge(rt_mm.of(x), rt_mm.done(it, x))
                    g = lg[x]

                    def flat(k):
                        return g[:, k].rearrange("p c e -> p (c e)")

                    def spread(k):
                        return lgs[x][:, k].unsqueeze(2).broadcast_to([TK, NTK, NE])
                    then(x, V.tensor_tensor(flat(0), bank(x, 2, NTK * NE, rows=TK), w("br", rows=TK), ALU.add))
                    then(x, V.tensor_reduce(lgs[x][:, 0], g[:, 0], AX.X, ALU.max))
                    then(x, V.tensor_tensor(g[:, 1], g[:, 0], spread(0), ALU.is_ge))
                    then(x, V.tensor_tensor(flat(2), flat(1), c("iota", rows=TK), ALU.mult))
                    then(x, V.tensor_reduce(lgs[x][:, 1], g[:, 2], AX.X, ALU.min))
                    for s in range(2):
                        last = V.tensor_tensor(oh[x][:, :, s], c("iota", rows=TK).rearrange("p (c e) -> p c e", e=NE),
                                               spread(1), ALU.is_equal)
                    last.then_inc(oh_ready.of(x), 1)
                for x in XS:
                    dve.wait_ge(zh_ready.of(x), zh_ready.done(it, x))
                    then(x, V.tensor_tensor(zs[x][:, 1], z[x][:].rearrange("p i t -> p (i t)"), zs[x][:, 0], ALU.subtract))
                for e in range(NE):
                    for x in XS:
                        dve.wait_ge(mk_ready.of(x), mk_ready.done(it, x, e))
                        V.tensor_tensor(xe[x][:, e], zs[x], mk[x][:, e].unsqueeze(1).broadcast_to([P, 2, N]), ALU.mult).then_inc(xe_ready.of(x), 1)
                for x in XS:
                    for j in range(NJ):
                        dve.wait_ge(hh_ready.of(x), hh_ready.done(it, x, j))
                        V.scalar_tensor_tensor(hs[x][:, j, 1], bank(x, j), 0.0, hs[x][:, j, 0], ALU.max, ALU.subtract).then_inc(hid_ready.of(x), 1)
                for x in XS:
                    for e in range(NE):
                        dve.wait_ge(y_mm.of(x), y_mm.done(it, x, e))
                        V.scalar_tensor_tensor(ysel[x][:, e], bank(x, e % 4), SC ** -2, mk[x][:, e], ALU.mult, ALU.mult).then_inc(ysel_ready.of(x), 1)
                for x in XS:
                    Xf = X[x][:].rearrange("p i t -> p (i t)")
                    dve.wait_ge(y_mm.of(x), y_mm.done(it, x, NE))
                    dve.wait_ge(Hy_ready.of(x), Hy_ready.done(it, x, NE - 1))
                    V.scalar_tensor_tensor(Xf, bank(x, 0), SC ** -2, Xf, ALU.mult, ALU.add).then_inc(H_ready.of(x), 1)
                scale_z(3, 11, z)
                for i in range(2):
                    for x in XS:
                        src = (z[x][:] if i == 0 else xh[x][:, 0]).rearrange("p i t -> p (i t)")
                        dve.wait_ge(tc_ready.of(x), tc_ready.done(it, x, i))
                        then(x, V.tensor_tensor(dS[x], tS[x], src, ALU.subtract))
                        then(x, V.tensor_tensor(dS[x], dS[x], cS[x], ALU.mult))
                        V.tensor_tensor(xh[x][:, i].rearrange("p i t -> p (i t)"), dS[x], src, ALU.add).then_inc(xh_ready.of(x), 1)
                for x in XS:
                    dve.wait_ge(xh_ready.of(x), xh_ready.done(it, x, 1))
                    V.tensor_scalar(xw[x], xh[x][:, 1], w("aw", 2, 3), w("aw", 1, 2), ALU.mult, ALU.add).then_inc(xw_ready.of(x), 1)
                for x in XS:
                    dve.wait_ge(pair_mm.of(x), pair_mm.done(it, x))
                    for cc, (_, m) in enumerate(LC):
                        last = V.tensor_scalar(aS[x][0:m, :, cc], banks(x, 0, L, rows=m, a=cc * L), w("ab", rows=m), 0.0, ALU.add, ALU.max)
                    then(x, last)
                    for cc, (_, m) in enumerate(LC):
                        last = V.tensor_reduce(am[x][0:m, 0, :, cc], aS[x][0:m, :, cc], AX.X, ALU.max, negate=True)
                    last.then_inc(am_ready.of(x), 1)
                for x in XS:
                    dve.wait_ge(ex_ready.of(x), ex_ready.done(it, x))
                    for cc, (_, m) in enumerate(LC):
                        last = V.reciprocal(am[x][0:m, 2, :, cc], am[x][0:m, 1, :, cc])
                    then(x, last)
                    for cc, (_, m) in enumerate(LC):
                        last = V.tensor_tensor(aS[x][0:m, :, cc], aS[x][0:m, :, cc],
                                               am[x][0:m, 2, :, cc].unsqueeze(2).broadcast_to([m, IMGS, L]), ALU.mult)
                    last.then_inc(p_ready.of(x), 1)
                for x in XS:
                    dve.wait_ge(gate_ready.of(x), gate_ready.done(it, x))
                    zf = z[x][:].rearrange("p i t -> p (i t)")
                    Xf = X[x][:].rearrange("p i t -> p (i t)")
                    V.tensor_tensor(cS[x], cS[x], zf, ALU.mult)
                    then(x, V.tensor_tensor(tS[x], tS[x], tS[x], ALU.mult))
                    then(x, V.tensor_tensor(tS[x], tS[x], cS[x], ALU.add))
                    V.tensor_tensor(Xf, Xf, tS[x], ALU.add).then_inc(H_ready.of(x), 1)
                scale_z(4, 12, z)
                for x in XS:
                    dve.wait_ge(gl_mm.of(x), gl_mm.done(it, x))
                    g, s = gl[x], gs[x]
                    lo = bank(x, 2, NTK * (E2 + 1), rows=TK).rearrange("p (c e) -> p c e", c=NTK)

                    def over(k, n=E2):
                        return s[:, k].unsqueeze(2).broadcast_to([TK, NTK, n])
                    V.tensor_scalar(g[:, 0, :, E2:], lo[:, :, E2:], -1.0, None, ALU.mult)
                    then(x, V.tensor_reduce(s[:, 0], lo[:, :, 0:E2], AX.X, ALU.max))
                    V.tensor_tensor(g[:, 0, :, 0:E2], lo[:, :, 0:E2], over(0), ALU.subtract).then_inc(gd_ready.of(x), 1)
                    dve.wait_ge(ge_ready.of(x), ge_ready.done(it, x))
                    V.tensor_reduce(s[:, 1], g[:, 1, :, 0:E2], AX.X, ALU.add)
                    then(x, V.tensor_scalar(s[:, 2], g[:, 1, :, E2], 1.0, None, ALU.add))
                    then(x, V.reciprocal(s[:, 3:5], s[:, 1:3]))
                    then(x, V.tensor_tensor(g[:, 2, :, 0:E2], g[:, 1, :, 0:E2], over(3), ALU.mult))
                    then(x, V.scalar_tensor_tensor(g[:, 2, :, 0:E2], over(4), -1.0 / E2, g[:, 2, :, 0:E2], ALU.mult, ALU.add))
                    then(x, V.tensor_scalar(g[:, 3, :, 0:E2], g[:, 2, :, 0:E2], 0.0, None, ALU.max))
                    then(x, V.tensor_reduce(s[:, 5], g[:, 3, :, 0:E2], AX.X, ALU.add))
                    then(x, V.scalar_tensor_tensor(s[:, 6], s[:, 5], 0.0, s[:, 5], ALU.is_equal, ALU.add))
                    then(x, V.reciprocal(s[:, 7], s[:, 6]))
                    V.tensor_tensor(wrep[x][:], g[:, 3, :, 0:E2].unsqueeze(3).broadcast_to([TK, NTK, E2, R2]),
                                    s[:, 7].unsqueeze(2).unsqueeze(3).broadcast_to([TK, NTK, E2, R2]),
                                    ALU.mult).then_inc(wv_ready.of(x), 1)
                for x in XS:
                    dve.wait_ge(wr_ready.of(x), wr_ready.done(it, x))
                    dve.wait_ge(lo_mm.of(x), lo_mm.done(it, x))
                    V.tensor_tensor(low[x], wr[x], bank(x, 3, rows=E2 * R2), ALU.mult).then_inc(low_ready.of(x), 1)
                for x in XS:
                    dve.wait_ge(ro_mm.of(x), ro_mm.done(it, x))
                    V.tensor_tensor(outS[x], X[x][:].rearrange("p i t -> p (i t)"), bank(x, 0), ALU.add).then_inc(out_ready.of(x), 1)
                dve.wait_ge(out_ready.of(STREAMS - 1), out_ready.done(it, STREAMS - 1))
                dve.wait_ge(stored, it * (16 * STREAMS) + 16 * STREAMS)
                assert seen == [CHAIN] * STREAMS, seen

        @block.tensor
        def _(pe):
            mm = nc.tensor.matmul

            def flat(t):
                return t.rearrange("p i t -> p (i t)")
            pe.wait_ge(setup_d, 1)
            mm(bank(0, 0, 1), w("o_w"), w("ln_b"), start=True, stop=True)
            for e in range(E2):
                last = mm(bank(0, 1, D, rows=E2 * R2), w("lB", 64 * e, 64 * e + 64), w("fc2", D * e, D * e + D),
                          start=(e == 0), stop=(e == E2 - 1))
            last.then_inc(setup_p, 1)
            pe.wait_ge(setup_d, 2)

            with pe.Fori(0, iters) as it:
                def wait(x, sig, k=0):
                    pe.wait_ge(sig.of(x), sig.done(it, x, k))

                def unit(x, b, lhsT, rhs, sig=None, rows=P, n=N):
                    r = mm(bank(x, b, n, rows=rows), lhsT, rhs, start=True, stop=True)
                    if sig is not None:
                        r.then_inc(sig.of(x), 1)

                def mean_square(o):
                    for x in XS:
                        wait(x, sq_ready, o)
                        unit(x, 0, c("mean"), sq[x][:, 0:IMGS * T], ms_mm, n=IMGS * T)

                def layernorm(o, src, sig, k):
                    for x in XS:
                        wait(x, sig, k)
                        unit(x, 0, c("centre"), src(x), cen_mm)
                    for x in XS:
                        wait(x, csq_ready, o)
                        unit(x, 1, c("mean"), sq[x][:], var_mm)

                for x in XS:
                    pe.wait_ge(img_loaded.of(x), img_loaded.done(it, x))
                    for k in range(KP):
                        last = mm(bank(x, 1, IMGS * NPATCH), w("conv", D * k, D * k + D), img[x][:, k],
                                  start=(k == 0), stop=(k == KP - 1))
                    last.then_inc(img_used.of(x), 1)
                for l in range(2):
                    mean_square(2 * l)
                    for x in XS:
                        wait(x, h_ready, 2 * l)
                        for i in range(IMGS):
                            for cc, (t0, m) in enumerate(TC):
                                last = mm(bank(x, 0, D, rows=m, a=(2 * i + cc) * D), h[x][:, i, t0:t0 + m],
                                          w(f"qkv{l}", 4 * D), start=True, stop=True)
                        last.then_inc(v_mm.of(x), 1)
                    for k, b in enumerate((1, 2, 3, 0)):
                        for x in XS:
                            if k == 3:
                                wait(x, v_ready, l)
                            unit(x, b, w(f"qkv{l}", D * k, D * k + D), flat(h[x]), qk_mm, n=IT)

                    def row_scores(x, s, b, cc):
                        (i, hp), (t0, m) = STEPS[s], TC[cc]
                        for a in range(2):
                            last = mm(bank(x, b, T, rows=m, a=a * T), qmh[x][:, 2 * hp + a, i, t0:t0 + m], k1[x][:, hp // 2, i],
                                      start=True, stop=True)
                        return last

                    def second_maxima(x, s, cc):
                        k = NMAX * l + GS + 2 * s + cc
                        if s == 0 and cc == 0:
                            wait(x, qm1_ready, l)
                        wait(x, max_ready, k - 1)
                        row_scores(x, GS + s, 3, cc).then_inc(max_mm.of(x), 1)

                    def as_rows(x, g):
                        wait(x, max_ready, NMAX * l + (GS - 1 if g == 0 else NMAX - 1))
                        for i in range(IMGS):
                            for tc, (t0, m) in enumerate(TC):
                                last = mm(bank(x, 3 * g, m, rows=GH, a=i * T + t0, row0=HR), nm[x][0:m, i, tc, GH * g:GH * g + GH],
                                          identb[0:m, 0:m], start=True, stop=True, tile_position=(0, HR))
                        last.then_inc(nmT_mm.of(x), 1)

                    for s in range(GS):
                        for x in XS:
                            if s == 0:
                                wait(x, qm_ready, l)
                                wait(x, k1_ready, l)
                            elif s >= 2:
                                wait(x, max_ready, NMAX * l + s - 2)
                            for cc in range(2):
                                last = row_scores(x, s, 2 * (s % 2) + cc, cc)
                            last.then_inc(max_mm.of(x), 1)
                    for x in XS:
                        as_rows(x, 0)

                    def scores(x, s):
                        i, hp = STEPS[s]
                        if s == 0:
                            wait(x, k2_ready, l)
                        if s % GS == 0:
                            wait(x, qml_ready, 2 * l + s // GS)
                        if s:
                            wait(x, exp_ready, 8 * l + s - 1)
                        for cc, (s0, ms) in enumerate(TC):
                            mm(bank(x, cc, 2 * T, rows=ms), k1[x][:, hp // 2, i, s0:s0 + ms], qmh[x][:, 2 * hp:2 * hp + 2, i],
                               start=True, stop=False)
                            last = mm(bank(x, cc, 2 * T, rows=ms), k2[x][:, hp // 2, i, s0:s0 + ms],
                                      qml[x][0:HR + GH, 2 * hp:2 * hp + 2, i], start=False, stop=True)
                        last.then_inc(score_mm.of(x), 1)

                    def values(x, s):
                        i, g = STEPS[s][0], STEPS[s][1] // 2
                        wait(x, exp_ready, 8 * l + s)
                        for cc, (_, m) in enumerate(TC):
                            for a in range(GH):
                                last = mm(bank(x, 2 + g, T, rows=BLK, a=i * T, row0=BLK * a), va[x][0:m, i, cc, GH * g + a],
                                          pt[x][s // 2 % 2][0:m, cc, a], start=(cc == 0), stop=(cc == 1), tile_position=(0, BLK * a))
                        if s == len(STEPS) - 1:
                            last.then_inc(pv_mm.of(x), 1)

                    for g in range(2):
                        scores(0, GS * g)
                        for s in range(GS * g, GS * g + GS):
                            end = s == GS * g + GS - 1
                            scores(1, s)
                            if g == 0:
                                second_maxima(0, s, 0)
                            if not end:
                                scores(0, s + 1)
                            if s % 2 and not end:
                                values(0, s)
                            if g == 0:
                                second_maxima(1, s, 0)
                                second_maxima(0, s, 1)
                            if s % 2 and not end:
                                values(1, s)
                            if g == 0:
                                second_maxima(1, s, 1)
                            if end:
                                values(0, s)
                                if g == 0:
                                    for x in XS:
                                        as_rows(x, 1)
                                values(1, s)
                    for x in XS:
                        wait(x, o_ready, l)
                        for g in range(2):
                            unit(x, g, c("sel"), oS[x][:, g], sum_mm if g else None, n=IMGS * T)
                    for x in XS:
                        wait(x, on_ready, l)
                        for g in range(2):
                            last = mm(bank(x, 2, IMGS * T), w(f"wo{l}", D * g, D * g + D), on[x][:, g],
                                      start=(g == 0), stop=(g == 1))
                        last.then_inc(wo_mm.of(x), 1)
                    mean_square(2 * l + 1)
                    for j, (f0, m) in enumerate(FCH):
                        for x in XS:
                            if j == 0:
                                wait(x, h_ready, 2 * l + 1)
                            if j == 2:
                                wait(x, ff_ready, 3 * l)
                            b = (2 * j) % 4
                            unit(x, b, w(f"gate{l}", f0, f0 + m), flat(h[x]), None, m, IMGS * T)
                            unit(x, b + 1, w(f"up{l}", f0, f0 + m), flat(h[x]), gu_mm, m, IMGS * T)
                    for x in XS:
                        wait(x, ff_ready, 3 * l + 2)
                        for j, (_, m) in enumerate(FCH):
                            last = mm(bank(x, 2, IMGS * T), w(f"down{l}", D * j, D * j + D, rows=m), ff[x][0:m, j],
                                      start=(j == 0), stop=(j == 2))
                        last.then_inc(down_mm.of(x), 1)
                mean_square(4)

                layernorm(0, lambda x: flat(X[x][:]), x_ready, 5)
                for x in XS:
                    wait(x, z_ready, 0)
                    unit(x, 2, w("k_w1"), flat(z[x][:]))
                    unit(x, 3, w("q_w1"), flat(z[x][:]), kq1_mm)
                    for i in range(IMGS):
                        for cc, (t0, m) in enumerate(LC):
                            last = mm(bank(x, 0, D, rows=m, a=(2 * i + cc) * D), z[x][:, i, t0:t0 + m], w("v_w"),
                                      start=True, stop=True)
                    last.then_inc(v0_mm.of(x), 1)
                for x in XS:
                    wait(x, gel_ready)
                    unit(x, 2, w("k_w2"), gel[x][:, 0], rows=KD)
                    unit(x, 3, w("q_w2"), gel[x][:, 1], kq2_mm, rows=KD)
                for x in XS:
                    wait(x, kqs_ready)
                    wait(x, v0_ready)
                    for s in range(2):
                        unit(x, s, c("ones", rows=KD), kqs[x][:, s], nn_mm if s else None)
                for x in XS:
                    wait(x, kqn_ready)
                    for i in range(IMGS):
                        last = mm(bank(x, 2 + i, L, rows=P), kq[x][:, 0, i, 0:P], kq[x][:, 1, i, :], start=True, stop=True)
                        last = mm(bank(x, 2 + i, LC[1][1], rows=LC[1][1], a=L), kq[x][:, 0, i, P:L], kq[x][:, 1, i, P:L],
                                  start=True, stop=True)
                    last.then_inc(sc_mm.of(x), 1)
                for x in XS:
                    wait(x, As_ready)
                    for i in range(IMGS):
                        mm(bank(x, 0, L, a=i * L), vS[x][:, i, 0], As[x][:, i, 0:L], start=True, stop=False)
                        last = mm(bank(x, 0, LC[1][1], a=i * L + P), vS[x][0:LC[1][1], i, 1], As[x][0:LC[1][1], i, L:],
                                  start=False, stop=True)
                    last.then_inc(r_mm.of(x), 1)
                layernorm(1, lambda x: rS[x], r_ready, 0)
                for x in XS:
                    wait(x, z_ready, 1)
                    unit(x, 2, owg[:], zn[x], ao_mm)

                layernorm(2, lambda x: flat(X[x][:]), H_ready, 0)
                for x in XS:
                    wait(x, z_ready, 2)
                    zf = flat(z[x][:])
                    for k in range(NTK):
                        last = mm(bank(x, 2, NE, rows=TK, a=NE * k), zf[:, TK * k:TK * k + TK], w("Wr"), start=True, stop=True)
                    last.then_inc(rt_mm.of(x), 1)
                for x in XS:
                    wait(x, oh_ready)
                    for k in range(NTK):
                        last = mm(bank(x, 3, TK, rows=2 * NE, a=TK * k), oh[x][:, k].rearrange("p s e -> p (s e)"),
                                  identb[0:TK, 0:TK], start=True, stop=True)
                    last.then_inc(ohT_mm.of(x), 1)
                for e in range(NE):
                    for x in XS:
                        if e == 0:
                            wait(x, ohT_ready)
                        if e >= 2:
                            wait(x, mk_ready, e - 2)
                        unit(x, 2 + e % 2, expselb[:, e], ohT[x][0:NE], mk_mm)
                for x in XS:
                    wait(x, mk_ready, NE - 1)
                    for j in range(NJ):
                        mm(bank(x, j), b1s[:, P * j:P * j + P], ohT[x][:], start=True, stop=False)
                        for e in range(NE):
                            if j == 0:
                                wait(x, xe_ready, e)
                            o = HID * e + P * j
                            for ws, zp in ((0, 0), (0, 1), (1, 0)):
                                last = mm(bank(x, j), W1s[:, ws, o:o + P], xe[x][:, e, zp],
                                          start=False, stop=(e == NE - 1 and ws == 1))
                        last.then_inc(hid_mm.of(x), 1)
                for x in XS:
                    for e in range(NE):
                        if e >= 4:
                            wait(x, ysel_ready, e - 4)
                        for j in range(NJ):
                            if e == 0:
                                wait(x, hid_ready, j)
                            o = (e * NJ + j) * D
                            for ws, hp in ((0, 0), (0, 1), (1, 0)):
                                last = mm(bank(x, e % 4), W2s[:, ws, o:o + D], hs[x][:, j, hp],
                                          start=(j == 0 and ws == 0 and hp == 0), stop=(j == NJ - 1 and ws == 1))
                        last.then_inc(y_mm.of(x), 1)
                    wait(x, ysel_ready, 4)
                    unit(x, 0, b2s[:], ohTs[x][:], y_mm)

                layernorm(3, lambda x: flat(X[x][:]), H_ready, 1)
                for i in range(2):
                    for x in XS:
                        wait(x, z_ready if i == 0 else xh_ready, 3 if i == 0 else 0)
                        src = flat(z[x][:]) if i == 0 else flat(xh[x][:, 0])
                        unit(x, 2 - 2 * i, w("tW", D * i, D * i + D), src)
                        unit(x, 3 - 2 * i, w("cW", D * i, D * i + D), src, tc_mm)
                for x in XS:
                    wait(x, xh_ready, 1)
                    for i in range(IMGS):
                        for cc, (t0, m) in enumerate(LC):
                            last = nc.tensor.transpose(bank(x, 2, D, rows=m, a=(2 * i + cc) * D), xh[x][:, 1, i, t0:t0 + m], c("ident"))
                    last.then_inc(xT_mm.of(x), 1)
                for x in XS:
                    wait(x, xw_ready)
                    for i in range(IMGS):
                        for cc, (t0, m) in enumerate(LC):
                            mm(bank(x, i, L, rows=m, a=cc * L), xw[x][:, i, t0:t0 + m], xh[x][:, 1, i], start=True, stop=False)
                            last = mm(bank(x, i, L, rows=m, a=cc * L), xh[x][:, 1, i, t0:t0 + m], w1row[:], start=False, stop=True)
                    last.then_inc(pair_mm.of(x), 1)
                for x in XS:
                    wait(x, p_ready)
                    for i in range(IMGS):
                        for jc, (j0, mj) in enumerate(LC):
                            for cc, (t0, m) in enumerate(LC):
                                last = nc.tensor.transpose(bank(x, i, m, rows=mj, a=jc * L + t0), aS[x][0:m, i, cc, j0:j0 + mj],
                                                           c("ident", 0, m, rows=m))
                    last.then_inc(pT_mm.of(x), 1)
                for x in XS:
                    wait(x, xT_ready)
                    wait(x, pT_ready)
                    for i in range(IMGS):
                        for jc, (j0, mj) in enumerate(LC):
                            last = mm(bank(x, 2, L, a=i * L), xTS[x][0:mj, i, jc], pTS[x][0:mj, i, jc], start=(jc == 0), stop=(jc == 1))
                    last.then_inc(att_mm.of(x), 1)
                for x in XS:
                    wait(x, att_ready)
                    for b, name in ((0, "ffW"), (1, "frW")):
                        mm(bank(x, b), w(name, 0, D), flat(z[x][:]), start=True, stop=False)
                        last = mm(bank(x, b), w(name, D), att[x], start=False, stop=True)
                    last.then_inc(gate_mm.of(x), 1)

                layernorm(4, lambda x: flat(X[x][:]), H_ready, 2)
                for x in XS:
                    wait(x, z_ready, 4)
                    zf = flat(z[x][:])
                    for k in range(NTK):
                        last = mm(bank(x, 2, E2 + 1, rows=TK, a=(E2 + 1) * k), zf[:, TK * k:TK * k + TK], w("gt"), start=True, stop=True)
                    last.then_inc(gl_mm.of(x), 1)
                    for e in range(E2):
                        if e >= 2:
                            wait(x, h2_ready, e - 2)
                        unit(x, e % 2, w("fc1", D * e, D * e + D), zf, h2_mm)
                for x in XS:
                    wait(x, wv_ready)
                    for k in range(NTK):
                        last = mm(bank(x, 2, TK, rows=E2 * R2, a=TK * k),
                                  wrep[x][:, k].rearrange("p e r -> p (e r)"),
                                  c("ident", 0, TK, rows=TK), start=True, stop=True)
                    last.then_inc(wr_mm.of(x), 1)
                    for e in range(E2):
                        wait(x, h2_ready, e)
                        last = mm(bank(x, 3, rows=E2 * R2), w("lA", 64 * e, 64 * e + 64), hid[x][:, e], start=(e == 0), stop=(e == E2 - 1))
                    last.then_inc(lo_mm.of(x), 1)
                for x in XS:
                    wait(x, low_ready)
                    unit(x, 0, G[:], low[x], ro_mm)


def arrange(inp):
    b = inp["x"].shape[0]
    iters = b // (IMGS * STREAMS)
    pt = np.asarray(inp["x"]).reshape(iters, STREAMS, IMGS, 3, SIDE, PATCH, SIDE, PATCH)
    pt = pt.transpose(0, 1, 3, 5, 7, 2, 4, 6).reshape(iters, STREAMS, KP, P, IMGS * NPATCH)
    pt = np.ascontiguousarray(pt.transpose(0, 1, 3, 2, 4)).reshape(iters, STREAMS, P, KP, IMGS * NPATCH)
    a = {}

    def put(name, m):
        m = np.asarray(m)
        full = np.zeros((P, m.shape[1]), m.dtype)
        full[:m.shape[0]] = m
        a[name] = full

    def col(name, v):
        put(name, np.asarray(v).reshape(-1, 1))

    g = {k: np.asarray(v) for k, v in inp.items()}
    put("conv", g["L0_tok_conv_w"].reshape(D, KP, P).transpose(2, 1, 0).reshape(P, KP * D))
    for l in range(2):
        qkv = g[f"L0_tok_qkv_{l}"].T
        put(f"qkv{l}", np.concatenate([qkv[:, HR * k:HR * k + HR] for k in range(4) for _ in range(2)] + [qkv[:, 2 * D:]], axis=1))
        wo = np.zeros((2, 4, BLK, D), g[f"L0_tok_wo_{l}"].dtype)
        wo[:, :, 0:DH] = g[f"L0_tok_wo_{l}"].T.reshape(2, 4, DH, D)
        put(f"wo{l}", wo.reshape(2, P, D).transpose(1, 0, 2).reshape(P, 2 * D))
        put(f"gate{l}", g[f"L0_tok_gate_{l}"].T)
        put(f"up{l}", g[f"L0_tok_up_{l}"].T)
        dn = np.zeros((3 * P, D), np.float32)
        dn[0:DFF] = g[f"L0_tok_down_{l}"].T
        put(f"down{l}", dn.reshape(3, P, D).transpose(1, 0, 2).reshape(P, 3 * D))
        col(f"ln1_{l}", g[f"L0_tok_ln1_{l}"])
        col(f"ln2_{l}", g[f"L0_tok_ln2_{l}"])
    for n in ("k_w1", "q_w1", "k_w2", "q_w2", "v_w", "o_w"):
        put(n, g[f"L0_attn_{n}"])
    for n in ("k_b1", "q_b1", "k_b2", "q_b2", "ln_g", "ln_b", "o_b"):
        col(n, g[f"L0_attn_{n}"])
    put("v_b", np.broadcast_to(g["L0_attn_v_b"], (P, D)))
    put("Wr", g["L0_ffn_Wr"])
    experts = np.stack([g["L0_ffn_W1"].transpose(1, 0, 2).reshape(D, NE * HID),
                        g["L0_ffn_W2"].reshape(NE, NJ, P, D).transpose(2, 0, 1, 3).reshape(P, NE * NJ * D)])
    put("br", np.broadcast_to(np.tile(g["L0_ffn_br"], NTK), (P, NTK * NE)))
    put("b1", np.concatenate([g["L0_ffn_b1"]] * 2))
    put("b2", np.concatenate([g["L0_ffn_b2"]] * 2))
    for n in ("tW", "cW"):
        put(n, g[f"L1_attn_{n}"].transpose(1, 0, 2).reshape(D, 2 * D))
    for n in ("frW", "ffW"):
        put(n, g[f"L1_attn_{n}"].reshape(2, D, D).transpose(1, 0, 2).reshape(D, 2 * D))
    put("tb", g["L1_attn_tb"].T)
    put("cb", g["L1_attn_cb"].T)
    put("aw", g["L1_attn_aW"].reshape(3, D).T)
    put("ab", np.broadcast_to(g["L1_attn_ab"], (P, 1)))
    col("frb", g["L1_attn_frb"])
    col("ffb", g["L1_attn_ffb"])
    put("gt", np.concatenate([g["L1_ffn_gate_w"], g["L1_ffn_thr_w"]]).T)
    put("fc1", g["L1_ffn_fc1_w"].transpose(2, 0, 1).reshape(D, E2 * D))
    la = np.zeros((D, E2, E2, R2), np.float32)
    lb = np.zeros((D, E2, E2, R2), np.float32)
    for e in range(E2):
        la[:, e, e] = g["L1_ffn_lora_A"][e]
        lb[:, e, e] = g["L1_ffn_lora_B"][e].T
    put("lA", la.reshape(D, -1))
    put("lB", lb.reshape(D, -1))
    put("fc2", g["L1_ffn_fc2_w"].transpose(2, 0, 1).reshape(D, E2 * D))
    put("pos", g["L0_tok_pos_emb"].reshape(T, D).T)
    col("conv_b", g["L0_tok_conv_b"])
    col("cls_token", g["L0_tok_cls_token"])
    col("cls_tok", g["cls_tok"])
    col("ln_f", g["L0_tok_ln_f"])
    weights = np.concatenate([a[n] for n, _ in WSPEC], axis=1)
    assert weights.shape == (P, WTOT)

    k = {}
    k["ident"] = np.eye(P)
    k["centre"] = np.eye(P) - 1.0 / D
    k["mean"] = np.full((P, D), 1.0 / D)
    k["ones"] = np.ones((P, D))
    k["hmask"] = np.tile(np.repeat(np.eye(GH), DH, axis=0), (2, 1))
    k["smask"] = np.zeros((P, GH))
    k["smask"][0:HR] = k["hmask"][0:HR]
    k["smask"][HR:HR + GH] = np.eye(GH)
    k["lowrows"] = np.zeros((P, 2))
    k["lowrows"][HR:, 0] = -1.0
    k["lowrows"][NE:2 * NE, 1] = -1.0
    sel = np.zeros((P, P))
    for q in range(4):
        sel[BLK * q + DH, BLK * q:BLK * q + BLK] = 1.0
    k["sel"] = sel
    t = np.arange(L)
    full = (t[:, None] <= t[None, :]) / np.sqrt((t[None, :] + 1.0) * (KD // 2))
    causal = np.zeros((P, L + LC[1][1]))
    causal[:, 0:L] = full[0:P]
    causal[0:LC[1][1], L:] = full[P:L, P:L]
    k["causal"] = causal
    k["iota"] = np.broadcast_to(np.tile(np.arange(NE) - NE, NTK), (P, NTK * NE))
    es = np.zeros((P, NE, P))
    for e in range(NE):
        es[e, e] = 1.0
    k["expsel"] = es.reshape(P, NE * P)
    consts = np.concatenate([k[n] for n, _ in CSPEC], axis=1).astype(np.float32)
    return iters, pt, weights, experts, consts


def kernel(**inputs):
    import concourse.bacc as bacc
    from concourse.bass_utils import run_bass_kernel_spmd

    iters, patches, weights, experts, consts = arrange(inputs)
    nc = bacc.Bacc("TRN2", target_bir_lowering=False, num_devices=1)
    arrays = {"patches": patches, "weights": weights, "experts": experts, "consts": consts}
    args = [nc.dram_tensor(n, v.shape, mybir.dt.from_np(v.dtype), kind="ExternalInput").ap() for n, v in arrays.items()]
    out = nc.dram_tensor("out", (iters, STREAMS, P, N), mybir.dt.float32, kind="ExternalOutput").ap()
    build(nc, iters, *args, out)
    r = run_bass_kernel_spmd(nc, [arrays], core_ids=[0])
    got = r.results[0]["out"].reshape(iters, STREAMS, P, IMGS, L)
    return np.ascontiguousarray(got.transpose(0, 1, 3, 4, 2).reshape(iters * STREAMS * IMGS, L, D))
```

```python
import concourse.bass as bass
from concourse import mybir
from contextlib import ExitStack
import numpy as np

P = 128
D = 128
HEADS, DH = 8, 16
PATCH, SIDE = 16, 14
NPATCH = SIDE * SIDE
T = NPATCH + 1
L = T + 1
IMGS = 2
STREAMS = 2
KP = 3 * PATCH * PATCH // P
DFF = 344
FCH = [(0, 128), (128, 128), (256, 88)]
NE, HID = 8, 512
NJ = HID // P
E2, R2 = 4, 16
KD = 64
TC = [(0, 128), (128, T - 128)]
LC = [(0, 128), (128, L - 128)]
TK = 99
NTK = IMGS * L // TK
N = IMGS * L
BLK = 32
TINY = 2.0 ** 20
GH = HEADS // 2
HR = GH * DH
SC = 64.0

WSPEC = [("conv", KP * D), ("qkv0", 5 * D), ("qkv1", 5 * D), ("wo0", 2 * D), ("wo1", 2 * D),
         ("gate0", DFF), ("gate1", DFF), ("up0", DFF), ("up1", DFF),
         ("down0", 3 * D), ("down1", 3 * D),
         ("k_w1", D), ("q_w1", D), ("k_w2", KD), ("q_w2", KD), ("v_w", D), ("o_w", D), ("v_b", D),
         ("Wr", NE),
         ("tW", 2 * D), ("cW", 2 * D), ("frW", 2 * D), ("ffW", 2 * D),
         ("gt", E2 + 1), ("fc1", E2 * D), ("lA", E2 * BLK), ("lB", E2 * BLK), ("fc2", E2 * D),
         ("pos", T), ("br", NTK * NE), ("b1", HID), ("b2", D),
         ("conv_b", 1), ("cls_token", 1), ("cls_tok", 1), ("ln_f", 1), ("ln1_0", 1), ("ln1_1", 1),
         ("ln2_0", 1), ("ln2_1", 1), ("k_b1", 1), ("q_b1", 1), ("k_b2", 1), ("q_b2", 1),
         ("ln_g", 1), ("ln_b", 1), ("o_b", 1), ("tb", 2), ("cb", 2), ("aw", 3), ("ab", 1),
         ("frb", 1), ("ffb", 1)]
CSPEC = [("ident", P), ("centre", D), ("mean", D), ("ones", D), ("hmask", 4), ("smask", 4), ("lowrows", 2), ("sel", P),
         ("causal", L + LC[1][1]), ("iota", NTK * NE), ("expsel", NE * P)]


def offsets(spec):
    at, o = {}, 0
    for name, n in spec:
        at[name] = (o, n)
        o += n
    return at, o


WAT, WTOT = offsets(WSPEC)
CAT, CTOT = offsets(CSPEC)
PIECE = 2048
assert NE * HID == 2 * PIECE == NE * NJ * D


def build(nc, iters, patches, weights, experts, consts, out):
    f32, bf16, i32 = mybir.dt.float32, mybir.dt.bfloat16, mybir.dt.int32
    ALU, ACT, AX = mybir.AluOpType, mybir.ActivationFunctionType, mybir.AxisListType
    LNEXP = "natural_log_exp_and_others"
    ctx = ExitStack()
    with ctx:
        def sb(name, shape, dt=f32):
            return ctx.enter_context(nc.sbuf_tensor(name, shape, dt))

        W = sb("W", [P, WTOT])
        C = sb("C", [P, CTOT])

        def w(name, a=0, b=None, rows=P):
            o, n = WAT[name]
            return W[0:rows, o + a:o + (n if b is None else b)]

        def c(name, a=0, b=None, rows=P):
            o, n = CAT[name]
            return C[0:rows, o + a:o + (n if b is None else b)]

        f16 = mybir.dt.float16
        identb = sb("identb", [P, P], f16)
        expselb = sb("expselb", [NE, NE, P], f16)
        W1s = sb("W1s", [P, 2, NE * HID], f16)
        W2s = sb("W2s", [P, 2, NE * NJ * D], f16)
        b1s = sb("b1s", [2 * NE, HID], f16)
        b2s = sb("b2s", [2 * NE, D], f16)
        w1row = sb("w1row", [P, L])
        owg = sb("owg", [P, D])
        obp = sb("obp", [P, 1])
        G = sb("G", [P, D])

        def per_stream(name, shape, dt=f32):
            return [sb(f"{name}{x}", shape, dt) for x in range(STREAMS)]

        img = per_stream("img", [P, KP, IMGS * NPATCH])
        X = per_stream("X", [P, IMGS, L])
        sq = per_stream("sq", [P, N])
        lnv = per_stream("lnv", [P, 2, N])
        rs = per_stream("rs", [P, 2, N])
        z = per_stream("z", [P, IMGS, L])
        h = [t[:].rearrange("p i t -> p (i t)")[:, 0:IMGS * T].rearrange("p (i t) -> p i t", i=IMGS) for t in z]
        ql = per_stream("ql", [HR + GH, 2, IMGS, T], f16)
        k1 = per_stream("k1", [P, 2, IMGS, T], f16)
        k2 = per_stream("k2", [HR + GH, 2, IMGS, T], f16)
        regA = per_stream("regA", [P, NE * N])
        regB = per_stream("regB", [P, NE * N])
        regC = per_stream("regC", [P, NJ * N])

        def view(reg, at, pattern, half=False, **dims):
            n = int(np.prod(list(dims.values())))
            if half:
                reg, at = [r[:, :].bitcast(f16) for r in reg], 2 * at
            if "one" in dims:
                return [r[:, at:at + n] for r in reg]
            return [r[:, at:at + n].rearrange(f"p ({pattern}) -> p {pattern}", **dims) for r in reg]

        IT = IMGS * T
        qmh = view(regA, 0, "h i t", half=True, h=HEADS, i=IMGS, t=T)
        qml = view(regA, HEADS * IT // 2, "h i t", half=True, h=HEADS, i=IMGS, t=T)
        xe = view(regA, 0, "e s n", half=True, e=NE, s=2, n=N)
        sil = view(regB, 0, "j n", j=3, n=IT)
        ff = view(regB, 3 * IT, "j n", j=3, n=IT)
        on = view(regB, 6 * IT, "g n", g=2, n=IT)
        mk = view(regB, 0, "e n", half=True, e=NE, n=N)
        zs = view(regB, NE * N // 2, "s n", half=True, s=2, n=N)
        pt = list(zip(view(regC, 0, "c a t", c=2, a=GH, t=T), view(regB, 2 * IT, "c a t", c=2, a=GH, t=T)))
        qh = view(regC, 2 * IT, "g i t", half=True, g=2, i=IMGS, t=T)
        kt = view(regC, 3 * IT, "g i t", half=True, g=2, i=IMGS, t=T)
        oS = view(regB, 0, "g n", g=2, n=IT)
        hid = view(regC, 0, "j n", j=NJ, n=N)
        hs = view(regC, 0, "j s n", half=True, j=NJ, s=2, n=N)
        ysel = view(regA, 0, "e n", e=NE, n=N)
        gel = view(regA, 0, "s n", s=2, n=N)
        kq = [v[0:KD] for v in view(regA, 2 * N, "s i t", s=2, i=IMGS, t=L)]
        kqs = [v[0:KD] for v in view(regA, 4 * N, "s n", s=2, n=N)]
        zn = view(regA, 6 * N, "one n", one=1, n=N)
        rS = view(regA, 7 * N, "one n", one=1, n=N)
        vS = view(regB, 0, "i c d", i=IMGS, c=2, d=D)
        As = view(regB, 4 * D, "i n", i=IMGS, n=L + LC[1][1])
        xh = view(regA, 0, "k i t", k=2, i=IMGS, t=L)
        xw = view(regA, 2 * N, "i t", i=IMGS, t=L)
        aS = view(regA, 3 * N, "i c t", i=IMGS, c=2, t=L)
        pTS = view(regA, 5 * N, "i c t", i=IMGS, c=2, t=L)
        att = view(regA, 7 * N, "one n", one=1, n=N)
        tS = view(regB, 0, "one n", one=1, n=N)
        cS = view(regB, N, "one n", one=1, n=N)
        dS = view(regB, 2 * N, "one n", one=1, n=N)
        xTS = view(regB, 3 * N, "i c d", i=IMGS, c=2, d=D)
        wr = view(regB, 5 * N, "one n", one=1, n=N)
        outS = view(regB, 7 * N, "one n", one=1, n=N)
        low = view(regB, 6 * N, "one n", one=1, n=N)
        va = per_stream("va", [P, IMGS, 2, HEADS, BLK])
        nm = per_stream("nm", [P, IMGS, 2, HEADS], f16)
        lg = per_stream("lg", [TK, 3, NTK, NE])
        oh = per_stream("oh", [TK, NTK, 2, NE], f16)
        lgs = per_stream("lgs", [TK, 2, NTK])
        ohT = per_stream("ohT", [2 * NE, N], f16)
        ohTs = per_stream("ohTs", [2 * NE, N], f16)
        am = per_stream("am", [P, 3, IMGS, 2])
        gl = per_stream("gl", [TK, 4, NTK, E2 + 1])
        wrep = per_stream("wrep", [TK, NTK, E2, BLK])
        gs = per_stream("gs", [TK, 8, NTK])

        ps = [[ctx.enter_context(nc.psum_tensor(f"ps{x}", [P, 4, 512], f32))] for x in range(STREAMS)]

        def bank(x, b, n=N, rows=P, a=0, row0=0):
            return ps[x][0][row0:row0 + rows, b, a:a + n]

        def banks(x, b, n, rows=P, a=0):
            return ps[x][0][0:rows, b:b + 2, a:a + n]

        class Signal:

            def __init__(self, name, times=1, by=1, blocks=False, split=False):
                self.sems = [ctx.enter_context(nc.semaphore(f"{name}{x if split else ''}"))
                             for x in range(STREAMS if split else 1)]
                self.times, self.by, self.blocks = times, by, blocks

            def of(self, x):
                return self.sems[x % len(self.sems)]

            def done(self, it, x, k=0):
                if len(self.sems) > 1:
                    return it * (self.times * self.by) + (k + 1) * self.by
                at = x * self.times + k if self.blocks else k * STREAMS + x
                return it * (self.times * STREAMS * self.by) + (at + 1) * self.by

        loaded = ctx.enter_context(nc.semaphore("weights_loaded"))
        setup_d = ctx.enter_context(nc.semaphore("setup_vector"))
        setup_p = ctx.enter_context(nc.semaphore("setup_tensor"))
        stored = ctx.enter_context(nc.semaphore("stored"))
        img_loaded = Signal("img_loaded", 1, 16, split=True)
        emb_mm = Signal("emb_mm")
        emb_ready = Signal("emb_ready")
        img_used = Signal("img_used")
        STEPS = [(i, 2 * g + a) for g in range(2) for i in range(IMGS) for a in range(2)]
        GS = len(STEPS) // 2
        NMAX = 2 * len(STEPS)
        x_ready = Signal("x_ready", 1 + 4 + 1)
        sq_ready = Signal("sq_ready", 5)
        ms_mm = Signal("ms_mm", 5)
        ln_done = Signal("ln_done", 5 + 5 + 1)
        rs_ready = Signal("rs_ready", 5 + 5 + 1)
        h_ready = Signal("h_ready", 4)
        qk_mm = Signal("qk_mm", 2 * 4)
        v_mm = Signal("v_mm", 2)
        qk_ready = Signal("qk_ready", 2 * 4)
        k1_ready = Signal("k1_ready", 2 * 2)
        k2_ready = Signal("k2_ready", 2)
        nmT_mm = Signal("nmT_mm", 2 * 2)
        nmT_ready = Signal("nmT_ready", 2 * 2)
        qml_ready = Signal("qml_ready", 2 * 4)
        stage_loaded = ctx.enter_context(nc.semaphore("experts_loaded"))
        zh_ready = Signal("zh_ready")
        hh_ready = Signal("hh_ready", NJ, blocks=True)
        v_ready = Signal("v_ready", 2)
        qm_ready = Signal("qm_ready", 2)
        qm1_ready = Signal("qm1_ready", 2 * 2)
        max_mm = Signal("max_mm", 2 * NMAX)
        max_ready = Signal("max_ready", 2 * NMAX)
        score_mm = Signal("score_mm", 2 * 8)
        exp_ready = Signal("exp_ready", 2 * 8)
        pv_mm = Signal("pv_mm", 2 * 2)
        o_ready = Signal("o_ready", 2 * 2)
        sum_mm = Signal("sum_mm", 2 * 2)
        lsum_ready = Signal("lsum_ready", 2 * 2, split=True)
        rsum_ready = Signal("rsum_ready", 2 * 2, split=True)
        on_ready = Signal("on_ready", 2 * 2, split=True)
        wo_mm = Signal("wo_mm", 2)
        gu_mm = Signal("gu_mm", 2 * 3)
        sil_ready = Signal("sil_ready", 2 * 3)
        ff_ready = Signal("ff_ready", 2 * 3)
        down_mm = Signal("down_mm", 2)
        cen_mm = Signal("cen_mm", 5)
        csq_ready = Signal("csq_ready", 5)
        var_mm = Signal("var_mm", 5)
        z_ready = Signal("z_ready", 5)
        H_ready = Signal("H_ready", 3)
        Hy_ready = Signal("Hy_ready", NE, blocks=True)
        Hz_ready = Signal("Hz_ready")
        kq1_mm = Signal("kq1_mm")
        v0_mm = Signal("v0_mm")
        gel_ready = Signal("gel_ready")
        v0_ready = Signal("v0_ready")
        kq2_mm = Signal("kq2_mm")
        kq_ready = Signal("kq_ready")
        kqs_ready = Signal("kqs_ready")
        nn_mm = Signal("nn_mm")
        nmax_ready = Signal("nmax_ready")
        kqn_ready = Signal("kqn_ready")
        sc_mm = Signal("sc_mm")
        As_ready = Signal("As_ready")
        r_mm = Signal("r_mm")
        r_ready = Signal("r_ready")
        ao_mm = Signal("ao_mm")
        rt_mm = Signal("rt_mm")
        oh_ready = Signal("oh_ready")
        ohT_mm = Signal("ohT_mm")
        ohT_ready = Signal("ohT_ready")
        mk_mm = Signal("mk_mm", NE)
        mk_ready = Signal("mk_ready", NE)
        xe_ready = Signal("xe_ready", NE)
        hid_mm = Signal("hid_mm", NJ, blocks=True)
        hid_ready = Signal("hid_ready", NJ, blocks=True)
        y_mm = Signal("y_mm", NE + 1, blocks=True)
        ysel_ready = Signal("ysel_ready", NE, blocks=True)
        tc_mm = Signal("tc_mm", 2)
        tc_ready = Signal("tc_ready", 2)
        xh_ready = Signal("xh_ready", 2)
        xw_ready = Signal("xw_ready")
        xT_mm = Signal("xT_mm")
        xT_ready = Signal("xT_ready")
        pair_mm = Signal("pair_mm", IMGS)
        am_ready = Signal("am_ready", IMGS)
        ex_ready = Signal("ex_ready", IMGS)
        p_ready = Signal("p_ready", IMGS)
        pT_mm = Signal("pT_mm", IMGS)
        pT_ready = Signal("pT_ready", IMGS)
        att_mm = Signal("att_mm")
        att_ready = Signal("att_ready")
        gate_mm = Signal("gate_mm")
        gate_ready = Signal("gate_ready")
        gl_mm = Signal("gl_mm")
        gd_ready = Signal("gd_ready")
        ge_ready = Signal("ge_ready")
        wv_ready = Signal("wv_ready")
        h2_mm = Signal("h2_mm", E2, blocks=True)
        h2_ready = Signal("h2_ready", E2, blocks=True)
        wr_mm = Signal("wr_mm")
        wr_ready = Signal("wr_ready")
        lo_mm = Signal("lo_mm")
        low_ready = Signal("low_ready")
        ro_mm = Signal("ro_mm")
        out_ready = Signal("out_ready")
        CHAIN = 25
        own = Signal("vector_own", CHAIN, split=True)

        LAG = 1
        EMB0 = 4
        EMB1 = 5

        LOADS = 16 * (-(-WTOT // PIECE) - (-CTOT // PIECE))

        XS = range(STREAMS)
        STAGES = [regA[0], regB[0], regA[1], regB[1]]
        EXPERT_PIECES = [(STAGES[k], experts[k // 2, :, (k % 2) * PIECE:(k % 2 + 1) * PIECE]) for k in range(4)]
        block = ctx.enter_context(nc.Block())

        @block.sync
        def _(sp):
            for dst, src, n in ((W, weights, WTOT), (C, consts, CTOT)):
                for a in range(0, n, PIECE):
                    sp.dma_start(dst[:, a:min(a + PIECE, n)], src[:, a:min(a + PIECE, n)]).then_inc(loaded, 16)

            for k, (reg, src) in enumerate(EXPERT_PIECES):
                sp.dma_start(reg[:, 0:PIECE], src).then_inc(stage_loaded, 16)

            def load(it, x):
                sp.dma_start(img[x][:, :, :], patches[it, x]).then_inc(img_loaded.of(x), 16)

            def store(it, x):
                sp.wait_ge(out_ready.of(x), out_ready.done(it, x))
                sp.dma_start(out[it, x], outS[x]).then_inc(stored, 16)

            for x in XS:
                load(0, x)
            with sp.Fori(0, iters - 1) as it:
                for x in XS:
                    sp.wait_ge(img_used.of(x), img_used.done(it, x))
                    load(it + 1, x)
                for x in XS:
                    store(it, x)
            for x in XS:
                sp.wait_ge(img_used.of(x), img_used.done(iters - 1, x))
                load(0, x)
            for x in XS:
                store(iters - 1, x)
            sp.wait_ge(stored, 16 * STREAMS * (iters + 1))
            for x in XS:
                sp.wait_ge(img_loaded.of(x), img_loaded.done(iters, x))

        @block.gpsimd
        def _(pool):
            with pool.Fori(0, iters) as it:
                for l in range(2):
                    for x in XS:
                        pool.wait_ge(qk_ready.of(x), qk_ready.done(it, x, 4 * l + 3))
                        k2f, ktf = (t[x][0:HR].rearrange("p g i t -> p (g i t)") for t in (k2, kt))
                        nc.gpsimd.tensor_tensor(k2f, ktf, c("ones", 0, 1, rows=HR).broadcast_to([HR, 2 * IT]),
                                                ALU.mult).then_inc(k2_ready.of(x), 1)
                for x in XS:
                    pool.wait_ge(z_ready.of(x), z_ready.done(it, x, 0))
                    nc.gpsimd.tensor_tensor(X[x][:], X[x][:], z[x][:], ALU.add).then_inc(Hz_ready.of(x), 1)
                for x in XS:
                    Xf = X[x][:].rearrange("p i t -> p (i t)")
                    for e in range(NE):
                        pool.wait_ge(ysel_ready.of(x), ysel_ready.done(it, x, e))
                        if e:
                            pool.wait_ge(Hy_ready.of(x), Hy_ready.done(it, x, e - 1))
                        nc.gpsimd.tensor_tensor(Xf, Xf, ysel[x][:, e], ALU.add).then_inc(Hy_ready.of(x), 1)

        @block.scalar
        def _(act):
            nc.scalar.preload_act_table_set(LNEXP)
            act.wait_ge(setup_d, 1)

            def rsqrt_of(it, x, k, src, eps, dims=(P, 1)):
                rows = dims[0]
                nc.scalar.activation(lnv[x][0:rows, 0, 0:src.shape[-1]], src, ACT.Ln, bias=eps).then_inc(ln_done.of(x), 1)
                act.wait_ge(ln_done.of(x), ln_done.done(it, x, k))
                nc.scalar.activation(rs[x][0:rows, 0, 0:src.shape[-1]], lnv[x][0:rows, 0, 0:src.shape[-1]],
                                     ACT.Exp, scale=-0.5).then_inc(rs_ready.of(x), 1)

            def rms(it, o, k):
                for x in XS:
                    act.wait_ge(x_ready.of(x), x_ready.done(it, x, o))
                    nc.scalar.activation(sq[x][:, 0:IMGS * T].rearrange("p (i t) -> p i t", i=IMGS),
                                         X[x][:, :, 1:L], ACT.Square).then_inc(sq_ready.of(x), 1)
                for x in XS:
                    act.wait_ge(ms_mm.of(x), ms_mm.done(it, x, o))
                    rsqrt_of(it, x, k, bank(x, 0, IMGS * T), 1e-6)

            def layernorm(it, o, k):
                for x in XS:
                    act.wait_ge(cen_mm.of(x), cen_mm.done(it, x, o))
                    nc.scalar.activation(sq[x][:, :], bank(x, 0), ACT.Square).then_inc(csq_ready.of(x), 1)
                for x in XS:
                    act.wait_ge(var_mm.of(x), var_mm.done(it, x, o))
                    rsqrt_of(it, x, k, bank(x, 1), 1e-5)

            with act.Fori(0, iters) as it:
                nc.scalar.preload_act_table_set(LNEXP)
                for l in range(2):
                    rms(it, 2 * l, 2 * l)
                    for k, (dst, g, b) in enumerate(((qh, 0, 1), (qh, 1, 2), (kt, 0, 3), (kt, 1, 0))):
                        for x in XS:
                            act.wait_ge(qk_mm.of(x), qk_mm.done(it, x, 4 * l + k))
                            nc.scalar.copy(dst[x][:, g].rearrange("p i t -> p (i t)"), bank(x, b, IT)).then_inc(qk_ready.of(x), 1)
                    for x in XS:
                        act.wait_ge(qk_ready.of(x), qk_ready.done(it, x, 4 * l + 3))
                        for a in range(2, GH):
                            last = nc.scalar.activation(qmh[x][:, a], qh[x][:, 0], ACT.Copy, scale=c("hmask", a, a + 1))
                        last.then_inc(qm1_ready.of(x), 1)
                    for x in XS:
                        for a in range(GH):
                            last = nc.scalar.activation(qmh[x][:, GH + a], qh[x][:, 1], ACT.Copy, scale=c("hmask", a, a + 1))
                        last.then_inc(qm1_ready.of(x), 1)
                        act.wait_ge(v_mm.of(x), v_mm.done(it, x, l))
                        for cc, (_, m) in enumerate(TC):
                            last = nc.scalar.copy(va[x][0:m, :, cc, :, 0:DH],
                                                  bank(x, 3, 512, rows=m).rearrange("p (i c h d) -> p i c h d", i=IMGS, c=2, h=HEADS)[:, :, cc])
                        last.then_inc(v_ready.of(x), 1)
                    for g in range(2):
                        for x in XS:
                            act.wait_ge(nmT_mm.of(x), nmT_mm.done(it, x, 2 * l + g))
                            nc.scalar.copy(ql[x][HR:HR + GH, g].rearrange("p i t -> p (i t)"),
                                           bank(x, 3 * g, IT, rows=GH, row0=HR)).then_inc(nmT_ready.of(x), 1)
                        for s in range(GS * g, GS * g + GS):
                            if s == GS + 1:
                                for x in XS:
                                    act.wait_ge(pv_mm.of(x), pv_mm.done(it, x, 2 * l))
                                    nc.scalar.copy(oS[x][:, 0], bank(x, 2, IT)).then_inc(o_ready.of(x), 1)
                            for x in XS:
                                act.wait_ge(score_mm.of(x), score_mm.done(it, x, 8 * l + s))
                                for cc, (_, m) in enumerate(TC):
                                    last = nc.scalar.activation(pt[x][s // 2 % 2][0:m, cc, 2 * (s % 2):2 * (s % 2) + 2].rearrange("p a t -> p (a t)"),
                                                                bank(x, cc, 2 * T, rows=m), ACT.Exp)
                                last.then_inc(exp_ready.of(x), 1)
                    for x in XS:
                        act.wait_ge(pv_mm.of(x), pv_mm.done(it, x, 2 * l + 1))
                        nc.scalar.copy(oS[x][:, 1], bank(x, 3, IT)).then_inc(o_ready.of(x), 1)
                    for x in XS:
                        for g in range(2):
                            act.wait_ge(sum_mm.of(x), sum_mm.done(it, x, 2 * l + g))
                            nc.scalar.activation(lnv[x][:, g, 0:IT], bank(x, g, IT), ACT.Ln).then_inc(lsum_ready.of(x), 1)
                        for g in range(2):
                            act.wait_ge(lsum_ready.of(x), lsum_ready.done(it, x, 2 * l + g))
                            nc.scalar.activation(rs[x][:, g, 0:IT], lnv[x][:, g, 0:IT], ACT.Exp,
                                                 scale=-1.0).then_inc(rsum_ready.of(x), 1)
                    rms(it, 2 * l + 1, 2 * l + 1)
                    nc.scalar.preload_act_table(ACT.Silu)
                    for j, (_, m) in enumerate(FCH):
                        for x in XS:
                            act.wait_ge(gu_mm.of(x), gu_mm.done(it, x, 3 * l + j))
                            nc.scalar.activation(sil[x][0:m, j], bank(x, (2 * j) % 4, IMGS * T, rows=m),
                                                 ACT.Silu).then_inc(sil_ready.of(x), 1)
                    nc.scalar.preload_act_table_set(LNEXP)
                rms(it, 4, 4)
                layernorm(it, 0, 5)
                nc.scalar.preload_act_table(ACT.Gelu)
                for x in XS:
                    act.wait_ge(kq1_mm.of(x), kq1_mm.done(it, x))
                    nc.scalar.activation(gel[x][:, 0], bank(x, 2), ACT.Gelu, bias=w("k_b1"))
                    nc.scalar.activation(gel[x][:, 1], bank(x, 3), ACT.Gelu, bias=w("q_b1")).then_inc(gel_ready.of(x), 1)
                nc.scalar.preload_act_table_set(LNEXP)
                for x in XS:
                    act.wait_ge(kq2_mm.of(x), kq2_mm.done(it, x))
                    for s, b in enumerate(("k_b2", "q_b2")):
                        last = nc.scalar.activation(kq[x][:, s].rearrange("p i t -> p (i t)"), bank(x, 2 + s, rows=KD),
                                                    ACT.Identity, bias=w(b, rows=KD))
                    last.then_inc(kq_ready.of(x), 1)
                for x in XS:
                    act.wait_ge(nmax_ready.of(x), nmax_ready.done(it, x))
                    nc.scalar.activation(lnv[x][0:KD], kqs[x], ACT.Ln, scale=TINY).then_inc(ln_done.of(x), 1)
                    act.wait_ge(ln_done.of(x), ln_done.done(it, x, 6))
                    nc.scalar.activation(rs[x][0:KD], lnv[x][0:KD], ACT.Exp, scale=-0.5).then_inc(rs_ready.of(x), 1)
                for x in XS:
                    act.wait_ge(r_mm.of(x), r_mm.done(it, x))
                    nc.scalar.copy(rS[x], bank(x, 0)).then_inc(r_ready.of(x), 1)
                layernorm(it, 1, 7)
                layernorm(it, 2, 8)
                for x in XS:
                    act.wait_ge(z_ready.of(x), z_ready.done(it, x, 2))
                    nc.scalar.copy(zs[x][:, 0], z[x][:].rearrange("p i t -> p (i t)")).then_inc(zh_ready.of(x), 1)
                for x in XS:
                    act.wait_ge(ohT_mm.of(x), ohT_mm.done(it, x))
                    nc.scalar.copy(ohT[x][:], bank(x, 2, rows=2 * NE))
                    nc.scalar.mul(ohTs[x][:], bank(x, 2, rows=2 * NE), SC).then_inc(ohT_ready.of(x), 1)
                for e in range(NE):
                    for x in XS:
                        act.wait_ge(mk_mm.of(x), mk_mm.done(it, x, e))
                        nc.scalar.copy(mk[x][:, e], bank(x, 2 - e % 2)).then_inc(mk_ready.of(x), 1)
                for x in XS:
                    for j in range(NJ):
                        act.wait_ge(hid_mm.of(x), hid_mm.done(it, x, j))
                        nc.scalar.activation(hs[x][:, j, 0], bank(x, j), ACT.Relu).then_inc(hh_ready.of(x), 1)
                layernorm(it, 3, 9)
                nc.scalar.preload_act_table(ACT.Sigmoid)
                for i in range(2):
                    for x in XS:
                        act.wait_ge(tc_mm.of(x), tc_mm.done(it, x, i))
                        if i:
                            act.wait_ge(xh_ready.of(x), xh_ready.done(it, x, 0))
                        nc.scalar.activation(tS[x], bank(x, 2 - 2 * i), ACT.Relu, bias=w("tb", i, i + 1))
                        nc.scalar.activation(cS[x], bank(x, 3 - 2 * i), ACT.Sigmoid, bias=w("cb", i, i + 1)).then_inc(tc_ready.of(x), 1)
                nc.scalar.preload_act_table_set(LNEXP)
                for x in XS:
                    act.wait_ge(xT_mm.of(x), xT_mm.done(it, x))
                    for cc, (_, m) in enumerate(LC):
                        last = nc.scalar.copy(xTS[x][0:m, :, cc],
                                              bank(x, 2, 512, rows=m).rearrange("p (i c d) -> p i c d", i=IMGS, c=2)[:, :, cc])
                    last.then_inc(xT_ready.of(x), 1)
                for i in range(IMGS):
                    for x in XS:
                        act.wait_ge(am_ready.of(x), am_ready.done(it, x, i))
                        for cc, (_, m) in enumerate(LC):
                            last = nc.scalar.activation(aS[x][0:m, i, cc], aS[x][0:m, i, cc], ACT.Exp,
                                                        bias=am[x][0:m, 0, i, cc:cc + 1],
                                                        accum_out=am[x][0:m, 1, i, cc:cc + 1])
                        last.then_inc(ex_ready.of(x), 1)
                for i in range(IMGS):
                    for x in XS:
                        act.wait_ge(pT_mm.of(x), pT_mm.done(it, x, i))
                        for cc, (_, m) in enumerate(LC):
                            last = nc.scalar.copy(pTS[x][0:m, i, cc], bank(x, i, L, rows=m, a=cc * L))
                        last.then_inc(pT_ready.of(x), 1)
                for x in XS:
                    act.wait_ge(att_mm.of(x), att_mm.done(it, x))
                    nc.scalar.copy(att[x], bank(x, 3)).then_inc(att_ready.of(x), 1)
                nc.scalar.preload_act_table(ACT.Sigmoid)
                for x in XS:
                    act.wait_ge(gate_mm.of(x), gate_mm.done(it, x))
                    nc.scalar.activation(tS[x], bank(x, 2), ACT.Sigmoid, bias=w("ffb"))
                    nc.scalar.activation(cS[x], bank(x, 0), ACT.Sigmoid, bias=w("frb")).then_inc(gate_ready.of(x), 1)
                nc.scalar.preload_act_table_set(LNEXP)
                layernorm(it, 4, 10)
                for x in XS:
                    act.wait_ge(gd_ready.of(x), gd_ready.done(it, x))
                    nc.scalar.activation(gl[x][:, 1], gl[x][:, 0], ACT.Exp).then_inc(ge_ready.of(x), 1)
                    for e in range(E2):
                        act.wait_ge(h2_mm.of(x), h2_mm.done(it, x, e))
                        nc.scalar.activation(hid[x][:, e], bank(x, e % 2), ACT.Relu).then_inc(h2_ready.of(x), 1)
                for x in XS:
                    act.wait_ge(wr_mm.of(x), wr_mm.done(it, x))
                    nc.scalar.copy(wr[x], bank(x, 2)).then_inc(wr_ready.of(x), 1)

        @block.vector
        def _(dve):
            dve.wait_ge(loaded, LOADS)
            V = nc.vector
            V.tensor_copy(identb[:], c("ident"))
            V.tensor_copy(expselb[:].rearrange("p e n -> p (e n)"), c("expsel", rows=NE))
            for x in XS:
                V.memset(va[x][:], 1.0)
                V.memset(k2[x][HR:], 1.0)
            V.tensor_scalar(w1row[:], c("ones", 0, 1).broadcast_to([P, L]), w("aw", 0, 1), None, ALU.mult)
            V.tensor_scalar(owg[:], w("o_w"), w("ln_g"), None, ALU.mult)
            for l in range(2):
                V.tensor_scalar(w(f"qkv{l}", 0, 2 * D), w(f"qkv{l}", 0, 2 * D), w(f"ln1_{l}"), DH ** -0.5, ALU.mult, ALU.mult)
                V.tensor_scalar(w(f"qkv{l}", 2 * D), w(f"qkv{l}", 2 * D), w(f"ln1_{l}"), None, ALU.mult)
                V.tensor_scalar(w(f"gate{l}"), w(f"gate{l}"), w(f"ln2_{l}"), None, ALU.mult)
                V.tensor_scalar(w(f"up{l}"), w(f"up{l}"), w(f"ln2_{l}"), None, ALU.mult)
            V.tensor_scalar(w("pos", 1), w("pos", 1), w("conv_b"), None, ALU.add)
            V.tensor_scalar(w("pos", 0, 1), w("pos", 0, 1), w("cls_token"), None, ALU.add)
            for k, (reg, _) in enumerate(EXPERT_PIECES):
                dst, a = (W1s, W2s)[k // 2], (k % 2) * PIECE
                dve.wait_ge(stage_loaded, 16 * len(EXPERT_PIECES))
                V.tensor_scalar(dst[:, 0, a:a + PIECE], reg[:, 0:PIECE], SC, None, ALU.mult)
            V.tensor_scalar(b1s[:], w("b1", rows=2 * NE), SC, None, ALU.mult)
            V.tensor_scalar(b2s[:], w("b2", rows=2 * NE), SC, None, ALU.mult)
            for name in ("b1", "b2"):
                last = V.tensor_scalar(w(name, rows=2 * NE), w(name, rows=2 * NE), SC, None, ALU.mult)
            last.then_inc(setup_d, 1)
            dve.wait_ge(setup_d, 1)
            for k, (reg, _) in enumerate(EXPERT_PIECES):
                dst, a = (W1s, W2s)[k // 2], (k % 2) * PIECE
                V.scalar_tensor_tensor(dst[:, 1, a:a + PIECE], reg[:, 0:PIECE], SC, dst[:, 0, a:a + PIECE],
                                       ALU.mult, ALU.subtract)
            V.scalar_tensor_tensor(b1s[:], b1s[:], c("lowrows", 1, 2, rows=2 * NE), w("b1", rows=2 * NE), ALU.mult, ALU.add)
            V.scalar_tensor_tensor(b2s[:], b2s[:], c("lowrows", 1, 2, rows=2 * NE), w("b2", rows=2 * NE), ALU.mult, ALU.add)
            dve.wait_ge(setup_p, 1)
            for x in XS:
                V.memset(outS[x][:, 0:1], 0.0).then_inc(stored, 16)
            V.tensor_scalar(obp[:], bank(0, 0, 1), w("o_b"), None, ALU.add)
            V.tensor_copy(G[:], bank(0, 1, D)).then_inc(setup_d, 1)

            def embed(it, x):
                dve.wait_ge(emb_mm.of(x), emb_mm.done(it, x))
                V.tensor_tensor(img[x][:, 0].rearrange("p (i t) -> p i t", i=IMGS),
                                bank(x, 3, IMGS * NPATCH).rearrange("p (i t) -> p i t", i=IMGS),
                                w("pos", 1).unsqueeze(1).broadcast_to([P, IMGS, NPATCH]), ALU.add).then_inc(emb_ready.of(x), 1)

            for x in XS:
                embed(0, x)
            with dve.Fori(0, iters) as it:
                seen = [0] * STREAMS

                def then(x, ins):
                    ins.then_inc(own.of(x), 1)
                    dve.wait_ge(own.of(x), own.done(it, x, seen[x]))
                    seen[x] += 1

                def scale_h(o, k):
                    for x in XS:
                        dve.wait_ge(rs_ready.of(x), rs_ready.done(it, x, k))
                        V.tensor_tensor(h[x], X[x][:, :, 1:L],
                                        rs[x][:, 0, 0:IMGS * T].rearrange("p (i t) -> p i t", i=IMGS),
                                        ALU.mult).then_inc(h_ready.of(x), 1)

                def add_x(x, b, sig, k, r, at=1):
                    dve.wait_ge(sig.of(x), sig.done(it, x, k))
                    V.tensor_tensor(X[x][:, :, at:L], X[x][:, :, at:L],
                                    bank(x, b, IMGS * (L - at)).rearrange("p (i t) -> p i t", i=IMGS),
                                    ALU.add).then_inc(r[0].of(x), 1)

                def scale_z(o, k, dst):
                    for x in XS:
                        dve.wait_ge(rs_ready.of(x), rs_ready.done(it, x, k))
                        V.tensor_tensor(dst[x][:].rearrange("p i t -> p (i t)") if dst is z else dst[x][:],
                                        bank(x, 0), rs[x][:, 0], ALU.mult).then_inc(z_ready.of(x), 1)

                for x in XS:
                    dve.wait_ge(emb_ready.of(x), emb_ready.done(it, x))
                    V.tensor_copy(X[x][:, :, 2:L], img[x][:, 0].rearrange("p (i t) -> p i t", i=IMGS)).then_inc(img_used.of(x), 1)
                    V.tensor_copy(X[x][:, :, 1:2], w("pos", 0, 1).unsqueeze(1).broadcast_to([P, IMGS, 1])).then_inc(x_ready.of(x), 1)
                for l in range(2):
                    scale_h(2 * l, 2 * l)
                    for g in range(2):
                        for x in XS:
                            dve.wait_ge(qk_ready.of(x), qk_ready.done(it, x, 4 * l + g))
                            qlg, qhg = (t[x][0:HR, g].rearrange("p i t -> p (i t)") for t in (ql, qh))
                            V.tensor_tensor(qlg, bank(x, 1 + g, IT, rows=HR), qhg, ALU.subtract)
                            if g == 0:
                                for a in range(2):
                                    last = V.tensor_scalar(qmh[x][:, a], qh[x][:, 0], c("hmask", a, a + 1), None, ALU.mult)
                                last.then_inc(qm_ready.of(x), 1)
                    for g in range(2):
                        for x in XS:
                            dve.wait_ge(qk_ready.of(x), qk_ready.done(it, x, 4 * l + 2 + g))
                            k1g, ktg = (t[x][:, g].rearrange("p i t -> p (i t)") for t in (k1, kt))
                            V.scalar_tensor_tensor(k1g, ktg, c("lowrows", 0, 1), bank(x, 3 - 3 * g, IT),
                                                   ALU.mult, ALU.add).then_inc(k1_ready.of(x), 1)

                    def maxima(x, s, b, cc):
                        (i, hp), m = STEPS[s], TC[cc][1]
                        return V.tensor_reduce(nm[x][0:m, i, cc, 2 * hp:2 * hp + 2],
                                               bank(x, b, 2 * T, rows=m).rearrange("p (a t) -> p a t", a=2),
                                               AX.X, ALU.max, negate=True)

                    def masked_low(g):
                        for pair in range(2):
                            for x in XS:
                                if pair == 0:
                                    dve.wait_ge(nmT_ready.of(x), nmT_ready.done(it, x, 2 * l + g))
                                for a in (2 * pair, 2 * pair + 1):
                                    last = V.tensor_scalar(qml[x][0:HR + GH, GH * g + a], ql[x][:, g],
                                                           c("smask", a, a + 1, rows=HR + GH), None, ALU.mult)
                                last.then_inc(qml_ready.of(x), 1)

                    for n in range(NMAX):
                        if n == NMAX // 2 + 1:
                            masked_low(0)
                        for x in XS:
                            dve.wait_ge(max_mm.of(x), max_mm.done(it, x, NMAX * l + n))
                            maxima(x, n // 2, (n + 1) % 3 if n < NMAX // 2 else 3, n % 2).then_inc(max_ready.of(x), 1)
                    masked_low(1)
                    if l == 0:
                        dve.wait_ge(stored, it * (16 * STREAMS) + 16 * STREAMS)
                    for x in XS:
                        for g in range(2):
                            dve.wait_ge(rsum_ready.of(x), rsum_ready.done(it, x, 2 * l + g))
                            V.tensor_tensor(on[x][:, g], oS[x][:, g], rs[x][:, g, 0:IT], ALU.mult).then_inc(on_ready.of(x), 1)
                    for x in XS:
                        add_x(x, 2, wo_mm, l, (x_ready,))
                    scale_h(2 * l + 1, 2 * l + 1)
                    for j, (_, m) in enumerate(FCH):
                        for x in XS:
                            dve.wait_ge(sil_ready.of(x), sil_ready.done(it, x, 3 * l + j))
                            V.tensor_tensor(ff[x][0:m, j], sil[x][0:m, j], bank(x, (2 * j + 1) % 4, IMGS * T, rows=m),
                                            ALU.mult).then_inc(ff_ready.of(x), 1)
                    for x in XS:
                        add_x(x, 2, down_mm, l, (x_ready,))
                for x in XS:
                    dve.wait_ge(rs_ready.of(x), rs_ready.done(it, x, 4))
                    V.scalar_tensor_tensor(X[x][:, :, 1:L], X[x][:, :, 1:L], w("ln_f"),
                                           rs[x][:, 0, 0:IMGS * T].rearrange("p (i t) -> p i t", i=IMGS),
                                           ALU.mult, ALU.mult)
                    V.tensor_copy(X[x][:, :, 0:1], w("cls_tok").unsqueeze(1).broadcast_to([P, IMGS, 1])).then_inc(x_ready.of(x), 1)
                scale_z(0, 5, z)
                for x in XS:
                    dve.wait_ge(v0_mm.of(x), v0_mm.done(it, x))
                    for cc, (_, m) in enumerate(LC):
                        src = bank(x, 0, 512, rows=m).rearrange("p (i c d) -> p i c d", i=IMGS, c=2)
                        last = V.tensor_tensor(vS[x][0:m, :, cc], src[:, :, cc],
                                               w("v_b", rows=m).unsqueeze(1).broadcast_to([m, IMGS, D]), ALU.add)
                    last.then_inc(v0_ready.of(x), 1)
                for x in XS:
                    dve.wait_ge(kq_ready.of(x), kq_ready.done(it, x))
                    kqf = kq[x].rearrange("p s i t -> p s (i t)")
                    V.tensor_tensor(kqs[x], kqf, kqf, ALU.mult).then_inc(kqs_ready.of(x), 1)
                for x in XS:
                    dve.wait_ge(nn_mm.of(x), nn_mm.done(it, x))
                    V.tensor_scalar(kqs[x], banks(x, 0, N, rows=KD), 1e-24, None, ALU.max).then_inc(nmax_ready.of(x), 1)
                for x in XS:
                    dve.wait_ge(rs_ready.of(x), rs_ready.done(it, x, 6))
                    kqf = kq[x].rearrange("p s i t -> p s (i t)")
                    V.scalar_tensor_tensor(kqf, kqf, TINY ** 0.5, rs[x][0:KD], ALU.mult, ALU.mult).then_inc(kqn_ready.of(x), 1)
                for x in XS:
                    dve.wait_ge(sc_mm.of(x), sc_mm.done(it, x))
                    for a, n, m in ((0, L, P), (L, LC[1][1], LC[1][1])):
                        last = V.tensor_tensor(As[x][0:m, :, a:a + n], banks(x, 2, n, rows=m, a=a),
                                               c("causal", a, a + n, rows=m).unsqueeze(1).broadcast_to([m, IMGS, n]), ALU.mult)
                    last.then_inc(As_ready.of(x), 1)
                scale_z(1, 7, zn)
                for x in XS:
                    dve.wait_ge(ao_mm.of(x), ao_mm.done(it, x))
                    dve.wait_ge(Hz_ready.of(x), Hz_ready.done(it, x))
                    Xf = X[x][:].rearrange("p i t -> p (i t)")
                    V.scalar_tensor_tensor(Xf, bank(x, 2), obp[:], Xf, ALU.add, ALU.add).then_inc(H_ready.of(x), 1)
                scale_z(2, 8, z)
                for x in XS:
                    dve.wait_ge(rt_mm.of(x), rt_mm.done(it, x))
                    g = lg[x]

                    def flat(k):
                        return g[:, k].rearrange("p c e -> p (c e)")

                    def spread(k):
                        return lgs[x][:, k].unsqueeze(2).broadcast_to([TK, NTK, NE])
                    then(x, V.tensor_tensor(flat(0), bank(x, 2, NTK * NE, rows=TK), w("br", rows=TK), ALU.add))
                    then(x, V.tensor_reduce(lgs[x][:, 0], g[:, 0], AX.X, ALU.max))
                    then(x, V.tensor_tensor(g[:, 1], g[:, 0], spread(0), ALU.is_ge))
                    then(x, V.tensor_tensor(flat(2), flat(1), c("iota", rows=TK), ALU.mult))
                    then(x, V.tensor_reduce(lgs[x][:, 1], g[:, 2], AX.X, ALU.min))
                    for s in range(2):
                        last = V.tensor_tensor(oh[x][:, :, s], c("iota", rows=TK).rearrange("p (c e) -> p c e", e=NE),
                                               spread(1), ALU.is_equal)
                    last.then_inc(oh_ready.of(x), 1)
                embed(it + 1, 0)
                for x in XS:
                    dve.wait_ge(zh_ready.of(x), zh_ready.done(it, x))
                    then(x, V.tensor_tensor(zs[x][:, 1], z[x][:].rearrange("p i t -> p (i t)"), zs[x][:, 0], ALU.subtract))
                for e in range(NE):
                    for x in XS:
                        dve.wait_ge(mk_ready.of(x), mk_ready.done(it, x, e))
                        V.tensor_tensor(xe[x][:, e], zs[x], mk[x][:, e].unsqueeze(1).broadcast_to([P, 2, N]), ALU.mult).then_inc(xe_ready.of(x), 1)
                for x in XS:
                    for j in range(NJ):
                        dve.wait_ge(hh_ready.of(x), hh_ready.done(it, x, j))
                        V.scalar_tensor_tensor(hs[x][:, j, 1], bank(x, j), 0.0, hs[x][:, j, 0], ALU.max, ALU.subtract).then_inc(hid_ready.of(x), 1)
                for x in XS:
                    for e in range(NE):
                        dve.wait_ge(y_mm.of(x), y_mm.done(it, x, e))
                        V.scalar_tensor_tensor(ysel[x][:, e], bank(x, e % 4), SC ** -2, mk[x][:, e], ALU.mult, ALU.mult).then_inc(ysel_ready.of(x), 1)
                for x in XS:
                    Xf = X[x][:].rearrange("p i t -> p (i t)")
                    dve.wait_ge(y_mm.of(x), y_mm.done(it, x, NE))
                    dve.wait_ge(Hy_ready.of(x), Hy_ready.done(it, x, NE - 1))
                    V.scalar_tensor_tensor(Xf, bank(x, 0), SC ** -2, Xf, ALU.mult, ALU.add).then_inc(H_ready.of(x), 1)
                scale_z(3, 9, z)
                for i in range(2):
                    for x in XS:
                        src = (z[x][:] if i == 0 else xh[x][:, 0]).rearrange("p i t -> p (i t)")
                        dve.wait_ge(tc_ready.of(x), tc_ready.done(it, x, i))
                        then(x, V.tensor_tensor(dS[x], tS[x], src, ALU.subtract))
                        then(x, V.tensor_tensor(dS[x], dS[x], cS[x], ALU.mult))
                        V.tensor_tensor(xh[x][:, i].rearrange("p i t -> p (i t)"), dS[x], src, ALU.add).then_inc(xh_ready.of(x), 1)
                for x in XS:
                    dve.wait_ge(xh_ready.of(x), xh_ready.done(it, x, 1))
                    V.tensor_scalar(xw[x], xh[x][:, 1], w("aw", 2, 3), w("aw", 1, 2), ALU.mult, ALU.add).then_inc(xw_ready.of(x), 1)
                for i in range(IMGS):
                    for x in XS:
                        dve.wait_ge(pair_mm.of(x), pair_mm.done(it, x, i))
                        for cc, (_, m) in enumerate(LC):
                            last = V.tensor_scalar(aS[x][0:m, i, cc], bank(x, i, L, rows=m, a=cc * L), w("ab", rows=m), 0.0, ALU.add, ALU.max)
                        then(x, last)
                        for cc, (_, m) in enumerate(LC):
                            last = V.tensor_reduce(am[x][0:m, 0, i, cc:cc + 1], aS[x][0:m, i, cc], AX.X, ALU.max, negate=True)
                        last.then_inc(am_ready.of(x), 1)
                for i in range(IMGS):
                    for x in XS:
                        dve.wait_ge(ex_ready.of(x), ex_ready.done(it, x, i))
                        for cc, (_, m) in enumerate(LC):
                            last = V.reciprocal(am[x][0:m, 2, i, cc:cc + 1], am[x][0:m, 1, i, cc:cc + 1])
                        then(x, last)
                        for cc, (_, m) in enumerate(LC):
                            last = V.tensor_scalar(aS[x][0:m, i, cc], aS[x][0:m, i, cc], am[x][0:m, 2, i, cc:cc + 1], None, ALU.mult)
                        last.then_inc(p_ready.of(x), 1)
                for x in XS:
                    dve.wait_ge(gate_ready.of(x), gate_ready.done(it, x))
                    zf = z[x][:].rearrange("p i t -> p (i t)")
                    Xf = X[x][:].rearrange("p i t -> p (i t)")
                    V.tensor_tensor(cS[x], cS[x], zf, ALU.mult)
                    then(x, V.tensor_tensor(tS[x], tS[x], tS[x], ALU.mult))
                    then(x, V.tensor_tensor(tS[x], tS[x], cS[x], ALU.add))
                    V.tensor_tensor(Xf, Xf, tS[x], ALU.add).then_inc(H_ready.of(x), 1)
                scale_z(4, 10, z)
                embed(it + 1, 1)
                for x in XS:
                    dve.wait_ge(gl_mm.of(x), gl_mm.done(it, x))
                    g, s = gl[x], gs[x]
                    lo = bank(x, 2, NTK * (E2 + 1), rows=TK).rearrange("p (c e) -> p c e", c=NTK)

                    def over(k, n=E2):
                        return s[:, k].unsqueeze(2).broadcast_to([TK, NTK, n])
                    V.tensor_scalar(g[:, 0, :, E2:], lo[:, :, E2:], -1.0, None, ALU.mult)
                    then(x, V.tensor_reduce(s[:, 0], lo[:, :, 0:E2], AX.X, ALU.max))
                    V.tensor_tensor(g[:, 0, :, 0:E2], lo[:, :, 0:E2], over(0), ALU.subtract).then_inc(gd_ready.of(x), 1)
                    dve.wait_ge(ge_ready.of(x), ge_ready.done(it, x))
                    V.tensor_reduce(s[:, 1], g[:, 1, :, 0:E2], AX.X, ALU.add)
                    then(x, V.tensor_scalar(s[:, 2], g[:, 1, :, E2], 1.0, None, ALU.add))
                    then(x, V.reciprocal(s[:, 3:5], s[:, 1:3]))
                    then(x, V.tensor_tensor(g[:, 2, :, 0:E2], g[:, 1, :, 0:E2], over(3), ALU.mult))
                    then(x, V.scalar_tensor_tensor(g[:, 2, :, 0:E2], over(4), -1.0 / E2, g[:, 2, :, 0:E2], ALU.mult, ALU.add))
                    then(x, V.tensor_scalar(g[:, 3, :, 0:E2], g[:, 2, :, 0:E2], 0.0, None, ALU.max))
                    then(x, V.tensor_reduce(s[:, 5], g[:, 3, :, 0:E2], AX.X, ALU.add))
                    then(x, V.scalar_tensor_tensor(s[:, 6], s[:, 5], 0.0, s[:, 5], ALU.is_equal, ALU.add))
                    then(x, V.reciprocal(s[:, 7], s[:, 6]))
                    V.tensor_tensor(wrep[x][:], g[:, 3, :, 0:E2].unsqueeze(3).broadcast_to([TK, NTK, E2, BLK]),
                                    s[:, 7].unsqueeze(2).unsqueeze(3).broadcast_to([TK, NTK, E2, BLK]),
                                    ALU.mult).then_inc(wv_ready.of(x), 1)
                for x in XS:
                    dve.wait_ge(wr_ready.of(x), wr_ready.done(it, x))
                    dve.wait_ge(lo_mm.of(x), lo_mm.done(it, x))
                    V.tensor_tensor(low[x], wr[x], bank(x, 3), ALU.mult).then_inc(low_ready.of(x), 1)
                for x in XS:
                    dve.wait_ge(ro_mm.of(x), ro_mm.done(it, x))
                    V.tensor_tensor(outS[x], X[x][:].rearrange("p i t -> p (i t)"), bank(x, 0), ALU.add).then_inc(out_ready.of(x), 1)
                dve.wait_ge(out_ready.of(STREAMS - 1), out_ready.done(it, STREAMS - 1))
                assert seen == [CHAIN] * STREAMS, seen

        @block.tensor
        def _(pe):
            mm = nc.tensor.matmul

            def flat(t):
                return t.rearrange("p i t -> p (i t)")
            pe.wait_ge(setup_d, 1)
            mm(bank(0, 0, 1), w("o_w"), w("ln_b"), start=True, stop=True)
            for e in range(E2):
                last = mm(bank(0, 1, D, rows=BLK, row0=BLK * e), w("lB", BLK * e, BLK * e + BLK), w("fc2", D * e, D * e + D),
                          start=True, stop=True, tile_position=(0, BLK * e))
            last.then_inc(setup_p, 1)

            def embed(it, x, chunks):
                if chunks[0] == 0:
                    pe.wait_ge(img_loaded.of(x), img_loaded.done(it, x))
                for k in chunks:
                    last = mm(bank(x, 3, IMGS * NPATCH), w("conv", D * k, D * k + D), img[x][:, k],
                              start=(k == 0), stop=(k == KP - 1))
                if chunks[-1] == KP - 1:
                    last.then_inc(emb_mm.of(x), 1)

            for x in XS:
                embed(0, x, range(KP))
            pe.wait_ge(setup_d, 2)
            with pe.Fori(0, iters) as it:
                def wait(x, sig, k=0):
                    pe.wait_ge(sig.of(x), sig.done(it, x, k))

                def unit(x, b, lhsT, rhs, sig=None, rows=P, n=N):
                    r = mm(bank(x, b, n, rows=rows), lhsT, rhs, start=True, stop=True)
                    if sig is not None:
                        r.then_inc(sig.of(x), 1)

                def mean_square(o):
                    for x in XS:
                        wait(x, sq_ready, o)
                        unit(x, 0, c("mean"), sq[x][:, 0:IMGS * T], ms_mm, n=IMGS * T)

                def layernorm(o, src, sig, k):
                    for x in XS:
                        wait(x, sig, k)
                        unit(x, 0, c("centre"), src(x), cen_mm)
                    for x in XS:
                        wait(x, csq_ready, o)
                        unit(x, 1, c("mean"), sq[x][:], var_mm)

                for l in range(2):
                    mean_square(2 * l)
                    for k, b in enumerate((1, 2, 3, 0)):
                        for x in XS:
                            if k == 0:
                                wait(x, h_ready, 2 * l)
                            unit(x, b, w(f"qkv{l}", D * k, D * k + D), flat(h[x]), qk_mm, n=IT)

                    def values_in(x):
                        for i in range(IMGS):
                            for cc, (t0, m) in enumerate(TC):
                                last = mm(bank(x, 3, D, rows=m, a=(2 * i + cc) * D), h[x][:, i, t0:t0 + m],
                                          w(f"qkv{l}", 4 * D), start=True, stop=True)
                        last.then_inc(v_mm.of(x), 1)

                    def row_scores(x, s, b, cc):
                        (i, hp), (t0, m) = STEPS[s], TC[cc]
                        for a in range(2):
                            last = mm(bank(x, b, T, rows=m, a=a * T), qmh[x][:, 2 * hp + a, i, t0:t0 + m], k1[x][:, hp // 2, i],
                                      start=True, stop=True)
                        return last

                    def second_maxima(x, s, cc):
                        n = NMAX // 2 + 2 * s + cc
                        if s == 0 and cc == 0:
                            wait(x, qm1_ready, 2 * l + 1)
                            wait(x, v_ready, l)
                        wait(x, max_ready, NMAX * l + n - 1)
                        row_scores(x, GS + s, 3, cc).then_inc(max_mm.of(x), 1)

                    def as_rows(x, g):
                        wait(x, max_ready, NMAX * l + (NMAX // 2 - 1 if g == 0 else NMAX - 1))
                        for i in range(IMGS):
                            for tc, (t0, m) in enumerate(TC):
                                last = mm(bank(x, 3 * g, m, rows=GH, a=i * T + t0, row0=HR), nm[x][0:m, i, tc, GH * g:GH * g + GH],
                                          identb[0:m, 0:m], start=True, stop=True, tile_position=(0, HR))
                        last.then_inc(nmT_mm.of(x), 1)

                    for n in range(NMAX // 2):
                        for x in XS:
                            if n == 0:
                                wait(x, qm_ready, l)
                                wait(x, k1_ready, 2 * l)
                            elif n == 2:
                                wait(x, qm1_ready, 2 * l)
                                wait(x, k1_ready, 2 * l + 1)
                            elif n >= 3:
                                wait(x, max_ready, NMAX * l + n - 3)
                            row_scores(x, n // 2, (n + 1) % 3, n % 2).then_inc(max_mm.of(x), 1)
                            if n == 2:
                                values_in(x)
                    for x in XS:
                        as_rows(x, 0)
                    for x in XS:
                        second_maxima(x, 0, 0)

                    def scores(x, s):
                        i, hp = STEPS[s]
                        if s == 0:
                            wait(x, k2_ready, l)
                        if s % GS < 2:
                            wait(x, qml_ready, 4 * l + hp)
                        if s:
                            wait(x, exp_ready, 8 * l + s - 1)
                        for cc, (s0, ms) in enumerate(TC):
                            mm(bank(x, cc, 2 * T, rows=ms), k1[x][:, hp // 2, i, s0:s0 + ms], qmh[x][:, 2 * hp:2 * hp + 2, i],
                               start=True, stop=False)
                            last = mm(bank(x, cc, 2 * T, rows=ms), k2[x][:, hp // 2, i, s0:s0 + ms],
                                      qml[x][0:HR + GH, 2 * hp:2 * hp + 2, i], start=False, stop=True)
                        last.then_inc(score_mm.of(x), 1)

                    def values(x, s):
                        i, g = STEPS[s][0], STEPS[s][1] // 2
                        wait(x, exp_ready, 8 * l + s)
                        for cc, (_, m) in enumerate(TC):
                            for a in range(GH):
                                last = mm(bank(x, 2 + g, T, rows=BLK, a=i * T, row0=BLK * a), va[x][0:m, i, cc, GH * g + a],
                                          pt[x][s // 2 % 2][0:m, cc, a], start=(cc == 0), stop=(cc == 1), tile_position=(0, BLK * a))
                        if s % GS == GS - 1:
                            last.then_inc(pv_mm.of(x), 1)

                    for g in range(2):
                        scores(0, GS * g)
                        for s in range(GS * g, GS * g + GS):
                            end = s == GS * g + GS - 1
                            scores(1, s)
                            if g == 0 and s:
                                second_maxima(0, s, 0)
                            if not end:
                                scores(0, s + 1)
                            if s % 2 and not end:
                                values(0, s)
                            if g == 0 and s:
                                second_maxima(1, s, 0)
                            if g == 0:
                                second_maxima(0, s, 1)
                            if s % 2 and not end:
                                values(1, s)
                            if g == 0:
                                second_maxima(1, s, 1)
                            if end:
                                values(0, s)
                                if g == 0:
                                    for x in XS:
                                        as_rows(x, 1)
                                values(1, s)
                    for g in range(2):
                        for x in XS:
                            if g == 0:
                                wait(x, exp_ready, 8 * l + 7)
                            wait(x, o_ready, 2 * l + g)
                            unit(x, g, c("sel"), oS[x][:, g], sum_mm, n=IMGS * T)
                    for x in XS:
                        for g in range(2):
                            wait(x, on_ready, 2 * l + g)
                            last = mm(bank(x, 2, IMGS * T), w(f"wo{l}", D * g, D * g + D), on[x][:, g],
                                      start=(g == 0), stop=(g == 1))
                        last.then_inc(wo_mm.of(x), 1)
                    mean_square(2 * l + 1)
                    for j, (f0, m) in enumerate(FCH):
                        for x in XS:
                            if j == 0:
                                wait(x, h_ready, 2 * l + 1)
                            if j == 2:
                                wait(x, ff_ready, 3 * l)
                            b = (2 * j) % 4
                            unit(x, b, w(f"gate{l}", f0, f0 + m), flat(h[x]), None, m, IMGS * T)
                            unit(x, b + 1, w(f"up{l}", f0, f0 + m), flat(h[x]), gu_mm, m, IMGS * T)
                    for x in XS:
                        wait(x, ff_ready, 3 * l + 2)
                        for j, (_, m) in enumerate(FCH):
                            last = mm(bank(x, 2, IMGS * T), w(f"down{l}", D * j, D * j + D, rows=m), ff[x][0:m, j],
                                      start=(j == 0), stop=(j == 2))
                        last.then_inc(down_mm.of(x), 1)
                mean_square(4)

                layernorm(0, lambda x: flat(X[x][:]), x_ready, 5)
                for x in XS:
                    wait(x, z_ready, 0)
                    unit(x, 2, w("k_w1"), flat(z[x][:]))
                    unit(x, 3, w("q_w1"), flat(z[x][:]), kq1_mm)
                    for i in range(IMGS):
                        for cc, (t0, m) in enumerate(LC):
                            last = mm(bank(x, 0, D, rows=m, a=(2 * i + cc) * D), z[x][:, i, t0:t0 + m], w("v_w"),
                                      start=True, stop=True)
                    last.then_inc(v0_mm.of(x), 1)
                for x in XS:
                    wait(x, gel_ready)
                    unit(x, 2, w("k_w2"), gel[x][:, 0], rows=KD)
                    unit(x, 3, w("q_w2"), gel[x][:, 1], kq2_mm, rows=KD)
                for x in XS:
                    wait(x, kqs_ready)
                    wait(x, v0_ready)
                    for s in range(2):
                        unit(x, s, c("ones", rows=KD), kqs[x][:, s], nn_mm if s else None)
                for x in XS:
                    wait(x, kqn_ready)
                    for i in range(IMGS):
                        last = mm(bank(x, 2 + i, L, rows=P), kq[x][:, 0, i, 0:P], kq[x][:, 1, i, :], start=True, stop=True)
                        last = mm(bank(x, 2 + i, LC[1][1], rows=LC[1][1], a=L), kq[x][:, 0, i, P:L], kq[x][:, 1, i, P:L],
                                  start=True, stop=True)
                    last.then_inc(sc_mm.of(x), 1)
                for x in XS:
                    wait(x, As_ready)
                    for i in range(IMGS):
                        mm(bank(x, 0, L, a=i * L), vS[x][:, i, 0], As[x][:, i, 0:L], start=True, stop=False)
                        last = mm(bank(x, 0, LC[1][1], a=i * L + P), vS[x][0:LC[1][1], i, 1], As[x][0:LC[1][1], i, L:],
                                  start=False, stop=True)
                    last.then_inc(r_mm.of(x), 1)
                layernorm(1, lambda x: rS[x], r_ready, 0)
                for x in XS:
                    wait(x, z_ready, 1)
                    unit(x, 2, owg[:], zn[x], ao_mm)

                layernorm(2, lambda x: flat(X[x][:]), H_ready, 0)
                embed(it + 1, 0, range(EMB0))
                for x in XS:
                    wait(x, z_ready, 2)
                    zf = flat(z[x][:])
                    for k in range(NTK):
                        last = mm(bank(x, 2, NE, rows=TK, a=NE * k), zf[:, TK * k:TK * k + TK], w("Wr"), start=True, stop=True)
                    last.then_inc(rt_mm.of(x), 1)
                embed(it + 1, 0, range(EMB0, KP))
                for x in XS:
                    wait(x, oh_ready)
                    for k in range(NTK):
                        last = mm(bank(x, 2, TK, rows=2 * NE, a=TK * k), oh[x][:, k].rearrange("p s e -> p (s e)"),
                                  identb[0:TK, 0:TK], start=True, stop=True)
                    last.then_inc(ohT_mm.of(x), 1)

                def hidden(x, j, es):
                    if es[0] == 0:
                        mm(bank(x, j), b1s[:, P * j:P * j + P], ohT[x][:], start=True, stop=False)
                    for e in es:
                        if j == 0:
                            wait(x, xe_ready, e)
                        o = HID * e + P * j
                        for ws, zp in ((0, 0), (0, 1), (1, 0)):
                            last = mm(bank(x, j), W1s[:, ws, o:o + P], xe[x][:, e, zp],
                                      start=False, stop=(e == NE - 1 and ws == 1))
                    if es[-1] == NE - 1:
                        last.then_inc(hid_mm.of(x), 1)

                for e in range(NE):
                    for x in XS:
                        if e == 0:
                            wait(x, ohT_ready)
                        if e >= 2:
                            wait(x, mk_ready, e - 2)
                        unit(x, 2 - e % 2, expselb[:, e], ohT[x][0:NE], mk_mm)
                    for x in XS:
                        if e >= LAG:
                            hidden(x, 0, range(e - LAG, e - LAG + 1))
                for x in XS:
                    wait(x, mk_ready, NE - 1)
                    for j in range(NJ):
                        if j == 3 and x == 0:
                            pe.wait_ge(emb_ready.of(x), emb_ready.done(it + 1, x))
                        hidden(x, j, range(0 if j else NE - LAG, NE))
                for x in XS:
                    for e in range(NE):
                        if e >= 4:
                            wait(x, ysel_ready, e - 4)
                        for j in range(NJ):
                            if e == 0:
                                wait(x, hid_ready, j)
                            o = (e * NJ + j) * D
                            for ws, hp in ((0, 0), (0, 1), (1, 0)):
                                last = mm(bank(x, e % 4), W2s[:, ws, o:o + D], hs[x][:, j, hp],
                                          start=(j == 0 and ws == 0 and hp == 0), stop=(j == NJ - 1 and ws == 1))
                        last.then_inc(y_mm.of(x), 1)
                    wait(x, ysel_ready, 4)
                    unit(x, 0, b2s[:], ohTs[x][:], y_mm)

                layernorm(3, lambda x: flat(X[x][:]), H_ready, 1)
                for i in range(2):
                    for x in XS:
                        wait(x, z_ready if i == 0 else xh_ready, 3 if i == 0 else 0)
                        src = flat(z[x][:]) if i == 0 else flat(xh[x][:, 0])
                        unit(x, 2 - 2 * i, w("tW", D * i, D * i + D), src)
                        unit(x, 3 - 2 * i, w("cW", D * i, D * i + D), src, tc_mm)
                for x in XS:
                    wait(x, xh_ready, 1)
                    for i in range(IMGS):
                        for cc, (t0, m) in enumerate(LC):
                            last = nc.tensor.transpose(bank(x, 2, D, rows=m, a=(2 * i + cc) * D), xh[x][:, 1, i, t0:t0 + m], c("ident"))
                    last.then_inc(xT_mm.of(x), 1)
                for i in range(IMGS):
                    for x in XS:
                        if i == 0:
                            wait(x, xw_ready)
                        for cc, (t0, m) in enumerate(LC):
                            mm(bank(x, i, L, rows=m, a=cc * L), xw[x][:, i, t0:t0 + m], xh[x][:, 1, i], start=True, stop=False)
                            last = mm(bank(x, i, L, rows=m, a=cc * L), xh[x][:, 1, i, t0:t0 + m], w1row[:], start=False, stop=True)
                        last.then_inc(pair_mm.of(x), 1)
                for x in XS:
                    wait(x, xT_ready)
                    mm(bank(x, 2), w("ffW", 0, D), flat(z[x][:]), start=True, stop=False)
                for i in range(IMGS):
                    for x in XS:
                        wait(x, p_ready, i)
                        for jc, (j0, mj) in enumerate(LC):
                            for cc, (t0, m) in enumerate(LC):
                                last = nc.tensor.transpose(bank(x, i, m, rows=mj, a=jc * L + t0), aS[x][0:m, i, cc, j0:j0 + mj],
                                                           c("ident", 0, m, rows=m))
                        last.then_inc(pT_mm.of(x), 1)
                for i in range(IMGS):
                    for x in XS:
                        wait(x, pT_ready, i)
                        for jc, (j0, mj) in enumerate(LC):
                            last = mm(bank(x, 3, L, a=i * L), xTS[x][0:mj, i, jc], pTS[x][0:mj, i, jc], start=(jc == 0), stop=(jc == 1))
                        if i == IMGS - 1:
                            last.then_inc(att_mm.of(x), 1)
                for x in XS:
                    mm(bank(x, 0), w("frW", 0, D), flat(z[x][:]), start=True, stop=False)
                for x in XS:
                    wait(x, att_ready)
                    for b, name in ((2, "ffW"), (0, "frW")):
                        last = mm(bank(x, b), w(name, D), att[x], start=False, stop=True)
                    last.then_inc(gate_mm.of(x), 1)

                embed(it + 1, 1, range(EMB1))
                for x in XS:
                    wait(x, H_ready, 2)
                    unit(x, 0, c("centre"), flat(X[x][:]), cen_mm)
                embed(it + 1, 1, range(EMB1, KP))
                for x in XS:
                    wait(x, csq_ready, 4)
                    unit(x, 1, c("mean"), sq[x][:], var_mm)
                for x in XS:
                    wait(x, z_ready, 4)
                    zf = flat(z[x][:])
                    for k in range(NTK):
                        last = mm(bank(x, 2, E2 + 1, rows=TK, a=(E2 + 1) * k), zf[:, TK * k:TK * k + TK], w("gt"), start=True, stop=True)
                    last.then_inc(gl_mm.of(x), 1)
                    for e in range(E2):
                        if e >= 2:
                            wait(x, h2_ready, e - 2)
                        unit(x, e % 2, w("fc1", D * e, D * e + D), zf, h2_mm)
                for x in XS:
                    wait(x, wv_ready)
                    for k in range(NTK):
                        last = mm(bank(x, 2, TK, a=TK * k),
                                  wrep[x][:, k].rearrange("p e r -> p (e r)"),
                                  c("ident", 0, TK, rows=TK), start=True, stop=True)
                    last.then_inc(wr_mm.of(x), 1)
                    if x == 1:
                        pe.wait_ge(emb_ready.of(x), emb_ready.done(it + 1, x))
                    for e in range(E2):
                        wait(x, h2_ready, e)
                        last = mm(bank(x, 3, rows=BLK, row0=BLK * e), w("lA", BLK * e, BLK * e + BLK), hid[x][:, e],
                                  start=True, stop=True, tile_position=(0, BLK * e))
                    last.then_inc(lo_mm.of(x), 1)
                for x in XS:
                    wait(x, low_ready)
                    unit(x, 0, G[:], low[x], ro_mm)


def arrange(inp):
    b = inp["x"].shape[0]
    iters = b // (IMGS * STREAMS)
    pt = np.asarray(inp["x"]).reshape(iters, STREAMS, IMGS, 3, SIDE, PATCH, SIDE, PATCH)
    pt = pt.transpose(0, 1, 3, 5, 7, 2, 4, 6).reshape(iters, STREAMS, KP, P, IMGS * NPATCH)
    pt = np.ascontiguousarray(pt.transpose(0, 1, 3, 2, 4)).reshape(iters, STREAMS, P, KP, IMGS * NPATCH)
    a = {}

    def put(name, m):
        m = np.asarray(m)
        full = np.zeros((P, m.shape[1]), m.dtype)
        full[:m.shape[0]] = m
        a[name] = full

    def col(name, v):
        put(name, np.asarray(v).reshape(-1, 1))

    g = {k: np.asarray(v) for k, v in inp.items()}
    put("conv", g["L0_tok_conv_w"].reshape(D, KP, P).transpose(2, 1, 0).reshape(P, KP * D))
    for l in range(2):
        qkv = g[f"L0_tok_qkv_{l}"].T
        put(f"qkv{l}", np.concatenate([qkv[:, HR * k:HR * k + HR] for k in range(4) for _ in range(2)] + [qkv[:, 2 * D:]], axis=1))
        wo = np.zeros((2, 4, BLK, D), g[f"L0_tok_wo_{l}"].dtype)
        wo[:, :, 0:DH] = g[f"L0_tok_wo_{l}"].T.reshape(2, 4, DH, D)
        put(f"wo{l}", wo.reshape(2, P, D).transpose(1, 0, 2).reshape(P, 2 * D))
        put(f"gate{l}", g[f"L0_tok_gate_{l}"].T)
        put(f"up{l}", g[f"L0_tok_up_{l}"].T)
        dn = np.zeros((3 * P, D), np.float32)
        dn[0:DFF] = g[f"L0_tok_down_{l}"].T
        put(f"down{l}", dn.reshape(3, P, D).transpose(1, 0, 2).reshape(P, 3 * D))
        col(f"ln1_{l}", g[f"L0_tok_ln1_{l}"])
        col(f"ln2_{l}", g[f"L0_tok_ln2_{l}"])
    for n in ("k_w1", "q_w1", "k_w2", "q_w2", "v_w", "o_w"):
        put(n, g[f"L0_attn_{n}"])
    for n in ("k_b1", "q_b1", "k_b2", "q_b2", "ln_g", "ln_b", "o_b"):
        col(n, g[f"L0_attn_{n}"])
    put("v_b", np.broadcast_to(g["L0_attn_v_b"], (P, D)))
    put("Wr", g["L0_ffn_Wr"])
    experts = np.stack([g["L0_ffn_W1"].transpose(1, 0, 2).reshape(D, NE * HID),
                        g["L0_ffn_W2"].reshape(NE, NJ, P, D).transpose(2, 0, 1, 3).reshape(P, NE * NJ * D)])
    put("br", np.broadcast_to(np.tile(g["L0_ffn_br"], NTK), (P, NTK * NE)))
    put("b1", np.concatenate([g["L0_ffn_b1"]] * 2))
    put("b2", np.concatenate([g["L0_ffn_b2"]] * 2))
    for n in ("tW", "cW"):
        put(n, g[f"L1_attn_{n}"].transpose(1, 0, 2).reshape(D, 2 * D))
    for n in ("frW", "ffW"):
        put(n, g[f"L1_attn_{n}"].reshape(2, D, D).transpose(1, 0, 2).reshape(D, 2 * D))
    put("tb", g["L1_attn_tb"].T)
    put("cb", g["L1_attn_cb"].T)
    put("aw", g["L1_attn_aW"].reshape(3, D).T)
    put("ab", np.broadcast_to(g["L1_attn_ab"], (P, 1)))
    col("frb", g["L1_attn_frb"])
    col("ffb", g["L1_attn_ffb"])
    put("gt", np.concatenate([g["L1_ffn_gate_w"], g["L1_ffn_thr_w"]]).T)
    put("fc1", g["L1_ffn_fc1_w"].transpose(2, 0, 1).reshape(D, E2 * D))
    la = np.zeros((D, E2, BLK), np.float32)
    lb = np.zeros((D, E2, BLK), np.float32)
    for e in range(E2):
        la[:, e, 0:R2] = g["L1_ffn_lora_A"][e]
        lb[:, e, 0:R2] = g["L1_ffn_lora_B"][e].T
    put("lA", la.reshape(D, -1))
    put("lB", lb.reshape(D, -1))
    put("fc2", g["L1_ffn_fc2_w"].transpose(2, 0, 1).reshape(D, E2 * D))
    put("pos", g["L0_tok_pos_emb"].reshape(T, D).T)
    col("conv_b", g["L0_tok_conv_b"])
    col("cls_token", g["L0_tok_cls_token"])
    col("cls_tok", g["cls_tok"])
    col("ln_f", g["L0_tok_ln_f"])
    weights = np.concatenate([a[n] for n, _ in WSPEC], axis=1)
    assert weights.shape == (P, WTOT)

    k = {}
    k["ident"] = np.eye(P)
    k["centre"] = np.eye(P) - 1.0 / D
    k["mean"] = np.full((P, D), 1.0 / D)
    k["ones"] = np.ones((P, D))
    k["hmask"] = np.tile(np.repeat(np.eye(GH), DH, axis=0), (2, 1))
    k["smask"] = np.zeros((P, GH))
    k["smask"][0:HR] = k["hmask"][0:HR]
    k["smask"][HR:HR + GH] = np.eye(GH)
    k["lowrows"] = np.zeros((P, 2))
    k["lowrows"][HR:, 0] = -1.0
    k["lowrows"][NE:2 * NE, 1] = -1.0
    sel = np.zeros((P, P))
    for q in range(4):
        sel[BLK * q + DH, BLK * q:BLK * q + BLK] = 1.0
    k["sel"] = sel
    t = np.arange(L)
    full = (t[:, None] <= t[None, :]) / np.sqrt((t[None, :] + 1.0) * (KD // 2))
    causal = np.zeros((P, L + LC[1][1]))
    causal[:, 0:L] = full[0:P]
    causal[0:LC[1][1], L:] = full[P:L, P:L]
    k["causal"] = causal
    k["iota"] = np.broadcast_to(np.tile(np.arange(NE) - NE, NTK), (P, NTK * NE))
    es = np.zeros((P, NE, P))
    for e in range(NE):
        es[e, e] = 1.0
    k["expsel"] = es.reshape(P, NE * P)
    consts = np.concatenate([k[n] for n, _ in CSPEC], axis=1).astype(np.float32)
    return iters, pt, weights, experts, consts


def kernel(**inputs):
    import concourse.bacc as bacc
    from concourse.bass_utils import run_bass_kernel_spmd

    iters, patches, weights, experts, consts = arrange(inputs)
    nc = bacc.Bacc("TRN2", target_bir_lowering=False, num_devices=1)
    arrays = {"patches": patches, "weights": weights, "experts": experts, "consts": consts}
    args = [nc.dram_tensor(n, v.shape, mybir.dt.from_np(v.dtype), kind="ExternalInput").ap() for n, v in arrays.items()]
    out = nc.dram_tensor("out", (iters, STREAMS, P, N), mybir.dt.float32, kind="ExternalOutput").ap()
    build(nc, iters, *args, out)
    r = run_bass_kernel_spmd(nc, [arrays], core_ids=[0])
    got = r.results[0]["out"].reshape(iters, STREAMS, P, IMGS, L)
    return np.ascontiguousarray(got.transpose(0, 1, 3, 4, 2).reshape(iters * STREAMS * IMGS, L, D))
```
